# Optimizing a Trainium2 kernel written in Bass

```python
import numpy as np
import jax
import jax.numpy as jnp

def _softmax(x, axis=-1):
    return jax.nn.softmax(x, axis=axis)

def _gelu(x):
    return jax.nn.gelu(x, approximate=True)

def _silu(x):
    return jax.nn.silu(x)

def _sigmoid(x):
    return jax.nn.sigmoid(x)

def _layernorm(x, axis=-1, eps=1e-05):
    m = jnp.mean(x, axis=axis, keepdims=True)
    v = jnp.var(x, axis=axis, keepdims=True)
    return (x - m) / jnp.sqrt(v + eps)

def _scatter_add(tgt, idx, src, axis=0):
    return tgt.at[idx].add(src)

def _segment_sum(src, seg, n):
    return jax.ops.segment_sum(src, seg, n)
kernel_name = 'mk_sandwich_d1_jaxref_r8_143cb6'

def setup_inputs(seed: int=0):
    np.random.seed(seed)
    _w = jnp.asarray

    def _L0_attn_setup():
        import jax, jax.numpy as jnp
        import numpy as np
        D_MODEL = 256
        D_STATE = 128
        D_CONV = 4
        EXPAND = 2
        HEADDIM = 64
        NGROUPS = 1
        CHUNK = 32
        D_INNER = EXPAND * D_MODEL
        NHEADS = D_INNER // HEADDIM
        CONV_DIM = D_INNER + 2 * NGROUPS * D_STATE
        D_IN_PROJ = 2 * D_INNER + 2 * NGROUPS * D_STATE + NHEADS
        EPS = 1e-05

        def _segsum(x):
            T = x.shape[-1]
            cs = jnp.cumsum(x, axis=-1)
            seg = cs[..., :, None] - cs[..., None, :]
            mask = jnp.tril(jnp.ones((T, T), dtype=bool))
            return jnp.where(mask, seg, -jnp.inf)

        def _causal_conv1d_silu(x, w, b):
            K = w.shape[-1]
            Lx = x.shape[-1]
            xp = jnp.pad(x, ((0, 0), (0, 0), (K - 1, 0)))
            y = b[None, :, None]
            for k in range(K):
                y = y + w[None, :, k:k + 1] * xp[:, :, k:k + Lx]
            return jax.nn.silu(y)

        def _mamba2_forward(u, in_proj_kernel, conv1d_weight, conv1d_bias, dt_bias, A_log, D, norm_weight, out_proj_kernel):
            B_, L, _ = u.shape
            zxbcdt = u @ in_proj_kernel
            z = zxbcdt[..., :D_INNER]
            xBC = zxbcdt[..., D_INNER:D_INNER + CONV_DIM]
            dt = zxbcdt[..., D_INNER + CONV_DIM:]
            xBC = _causal_conv1d_silu(jnp.transpose(xBC, (0, 2, 1)), conv1d_weight, conv1d_bias)
            xBC = jnp.transpose(xBC, (0, 2, 1))
            x = xBC[..., :D_INNER].reshape(B_, L, NHEADS, HEADDIM)
            Bm = xBC[..., D_INNER:D_INNER + NGROUPS * D_STATE].reshape(B_, L, NGROUPS, D_STATE)
            Cm = xBC[..., D_INNER + NGROUPS * D_STATE:].reshape(B_, L, NGROUPS, D_STATE)
            dt = jax.nn.softplus(dt + dt_bias)
            A = -jnp.exp(A_log)
            nc = L // CHUNK
            r = NHEADS // NGROUPS
            xc = x.reshape(B_, nc, CHUNK, NGROUPS, r, HEADDIM)
            dtc = dt.reshape(B_, nc, CHUNK, NGROUPS, r)
            Bc = Bm.reshape(B_, nc, CHUNK, NGROUPS, D_STATE)
            Cc = Cm.reshape(B_, nc, CHUNK, NGROUPS, D_STATE)
            xdt = xc * dtc[..., None]
            dA = dtc * A.reshape(NGROUPS, r)
            dA = jnp.transpose(dA, (0, 3, 4, 1, 2))
            A_cs = jnp.cumsum(dA, axis=-1)
            Lmat = jnp.exp(_segsum(dA))
            Y_diag = jnp.einsum('bclgn,bcsgn,bgrcls,bcsgrp->bclgrp', Cc, Bc, Lmat, xdt)
            decay_states = jnp.exp(A_cs[..., -1:] - A_cs)
            states = jnp.einsum('bcsgn,bgrcs,bcsgrp->bcgrpn', Bc, decay_states, xdt)
            chunk_decay = jnp.exp(A_cs[..., -1])
            states_t = jnp.moveaxis(states, 1, 0)
            decay_t = jnp.moveaxis(chunk_decay, -1, 0)

            def step(S, inp):
                d, st = inp
                S_new = S * d[..., None, None] + st
                return (S_new, S)
            S0 = jnp.zeros(states_t.shape[1:], states_t.dtype)
            _, prev_states = jax.lax.scan(step, S0, (decay_t, states_t))
            prev_states = jnp.moveaxis(prev_states, 0, 1)
            state_decay = jnp.exp(A_cs)
            Y_off = jnp.einsum('bclgn,bcgrpn,bgrcl->bclgrp', Cc, prev_states, state_decay)
            Y = (Y_diag + Y_off).reshape(B_, nc, CHUNK, NHEADS, HEADDIM)
            Y = Y + x.reshape(B_, nc, CHUNK, NHEADS, HEADDIM) * D[:, None]
            y = Y.reshape(B_, L, D_INNER)
            y = y * jax.nn.silu(z)
            y = y * jax.lax.rsqrt(jnp.mean(y * y, axis=-1, keepdims=True) + EPS) * norm_weight
            return y @ out_proj_kernel
        key = jax.random.key(seed)
        ks = jax.random.split(key, 8)
        B, L = (2, 512)
        u = jax.random.normal(ks[0], (B, L, D_MODEL), jnp.float32)
        in_proj_kernel = jax.random.normal(ks[1], (D_MODEL, D_IN_PROJ), jnp.float32) * (1.0 / np.sqrt(D_MODEL))
        conv1d_weight = jax.random.normal(ks[2], (CONV_DIM, D_CONV), jnp.float32) * (1.0 / np.sqrt(D_CONV))
        conv1d_bias = jnp.zeros((CONV_DIM,), jnp.float32)
        uu = jax.random.uniform(ks[3], (NHEADS,), jnp.float32)
        dt = jnp.exp(uu * (np.log(0.1) - np.log(0.001)) + np.log(0.001))
        dt = jnp.maximum(dt, 0.0001)
        dt_bias = dt + jnp.log(-jnp.expm1(-dt))
        A_log = jnp.log(jax.random.uniform(ks[4], (NHEADS,), jnp.float32, minval=1.0, maxval=16.0))
        D = jnp.ones((NHEADS,), jnp.float32)
        norm_weight = jnp.ones((D_INNER,), jnp.float32)
        out_proj_kernel = jax.random.normal(ks[5], (D_INNER, D_MODEL), jnp.float32) * (1.0 / np.sqrt(D_INNER))
        return {'u': u, 'in_proj_kernel': in_proj_kernel, 'conv1d_weight': conv1d_weight, 'conv1d_bias': conv1d_bias, 'dt_bias': dt_bias, 'A_log': A_log, 'D': D, 'norm_weight': norm_weight, 'out_proj_kernel': out_proj_kernel}
    _L0_attn_in = _L0_attn_setup()

    def _L0_ffn_setup():
        import jax, jax.numpy as jnp
        import numpy as np
        BLOCK_SIZE = 32
        HIDDEN_SIZE = 256
        MLP_DIM = 2048
        NVFP4_LUT = jnp.array([0.0, 0.5, 1.0, 1.5, 2.0, 3.0, 4.0, 6.0, 0.0, -0.5, -1.0, -1.5, -2.0, -3.0, -4.0, -6.0], dtype=jnp.float32)

        def dequant_nvfp4(W_packed, scales, block=BLOCK_SIZE):
            N = W_packed.shape[0]
            low = W_packed & 15
            high = W_packed >> 4 & 15
            idx = jnp.stack([low, high], axis=-1).reshape(N, -1)
            vals = NVFP4_LUT[idx]
            K = vals.shape[1]
            vals = vals.reshape(N, K // block, block) * scales[:, :, None]
            return vals.reshape(N, K)
        key = jax.random.key(seed)
        ks = jax.random.split(key, 7)
        x = jax.random.normal(ks[0], (4, 32, HIDDEN_SIZE), dtype=jnp.float32)
        gate_W_packed = jax.random.randint(ks[1], (MLP_DIM, HIDDEN_SIZE // 2), 0, 32, dtype=jnp.int32)
        gate_scales = jax.random.uniform(ks[2], (MLP_DIM, HIDDEN_SIZE // BLOCK_SIZE), dtype=jnp.float32) * 0.1 + 0.001
        up_W_packed = jax.random.randint(ks[3], (MLP_DIM, HIDDEN_SIZE // 2), 0, 32, dtype=jnp.int32)
        up_scales = jax.random.uniform(ks[4], (MLP_DIM, HIDDEN_SIZE // BLOCK_SIZE), dtype=jnp.float32) * 0.1 + 0.001
        down_W_packed = jax.random.randint(ks[5], (HIDDEN_SIZE, MLP_DIM // 2), 0, 32, dtype=jnp.int32)
        down_scales = jax.random.uniform(ks[6], (HIDDEN_SIZE, MLP_DIM // BLOCK_SIZE), dtype=jnp.float32) * 0.1 + 0.001
        return {'x': x, 'gate_W_packed': gate_W_packed, 'gate_scales': gate_scales, 'up_W_packed': up_W_packed, 'up_scales': up_scales, 'down_W_packed': down_W_packed, 'down_scales': down_scales}
    _L0_ffn_in = _L0_ffn_setup()
    _d = {'L0_attn_u': _L0_attn_in['u'], 'L0_attn_in_proj_kernel': _L0_attn_in['in_proj_kernel'], 'L0_attn_conv1d_weight': _L0_attn_in['conv1d_weight'], 'L0_attn_conv1d_bias': _L0_attn_in['conv1d_bias'], 'L0_attn_dt_bias': _L0_attn_in['dt_bias'], 'L0_attn_A_log': _L0_attn_in['A_log'], 'L0_attn_D': _L0_attn_in['D'], 'L0_attn_norm_weight': _L0_attn_in['norm_weight'], 'L0_attn_out_proj_kernel': _L0_attn_in['out_proj_kernel'], 'L0_ffn_gate_W_packed': _L0_ffn_in['gate_W_packed'], 'L0_ffn_gate_scales': _L0_ffn_in['gate_scales'], 'L0_ffn_up_W_packed': _L0_ffn_in['up_W_packed'], 'L0_ffn_up_scales': _L0_ffn_in['up_scales'], 'L0_ffn_down_W_packed': _L0_ffn_in['down_W_packed'], 'L0_ffn_down_scales': _L0_ffn_in['down_scales']}
    _x0 = _d['L0_attn_u']
    _d['L0_attn_u'] = jax.random.normal(jax.random.fold_in(jax.random.key(seed), 1), (4, 1024, 256), dtype=_x0.dtype)
    del _x0
    return _d

def reference(L0_attn_u, L0_attn_in_proj_kernel, L0_attn_conv1d_weight, L0_attn_conv1d_bias, L0_attn_dt_bias, L0_attn_A_log, L0_attn_D, L0_attn_norm_weight, L0_attn_out_proj_kernel, L0_ffn_gate_W_packed, L0_ffn_gate_scales, L0_ffn_up_W_packed, L0_ffn_up_scales, L0_ffn_down_W_packed, L0_ffn_down_scales):

    def _L0_attn_ref(u, in_proj_kernel, conv1d_weight, conv1d_bias, dt_bias, A_log, D, norm_weight, out_proj_kernel):
        import jax, jax.numpy as jnp
        import numpy as np
        D_MODEL = 256
        D_STATE = 128
        D_CONV = 4
        EXPAND = 2
        HEADDIM = 64
        NGROUPS = 1
        CHUNK = 32
        D_INNER = EXPAND * D_MODEL
        NHEADS = D_INNER // HEADDIM
        CONV_DIM = D_INNER + 2 * NGROUPS * D_STATE
        D_IN_PROJ = 2 * D_INNER + 2 * NGROUPS * D_STATE + NHEADS
        EPS = 1e-05

        def _segsum(x):
            T = x.shape[-1]
            cs = jnp.cumsum(x, axis=-1)
            seg = cs[..., :, None] - cs[..., None, :]
            mask = jnp.tril(jnp.ones((T, T), dtype=bool))
            return jnp.where(mask, seg, -jnp.inf)

        def _causal_conv1d_silu(x, w, b):
            K = w.shape[-1]
            Lx = x.shape[-1]
            xp = jnp.pad(x, ((0, 0), (0, 0), (K - 1, 0)))
            y = b[None, :, None]
            for k in range(K):
                y = y + w[None, :, k:k + 1] * xp[:, :, k:k + Lx]
            return jax.nn.silu(y)

        def _mamba2_forward(u, in_proj_kernel, conv1d_weight, conv1d_bias, dt_bias, A_log, D, norm_weight, out_proj_kernel):
            B_, L, _ = u.shape
            zxbcdt = u @ in_proj_kernel
            z = zxbcdt[..., :D_INNER]
            xBC = zxbcdt[..., D_INNER:D_INNER + CONV_DIM]
            dt = zxbcdt[..., D_INNER + CONV_DIM:]
            xBC = _causal_conv1d_silu(jnp.transpose(xBC, (0, 2, 1)), conv1d_weight, conv1d_bias)
            xBC = jnp.transpose(xBC, (0, 2, 1))
            x = xBC[..., :D_INNER].reshape(B_, L, NHEADS, HEADDIM)
            Bm = xBC[..., D_INNER:D_INNER + NGROUPS * D_STATE].reshape(B_, L, NGROUPS, D_STATE)
            Cm = xBC[..., D_INNER + NGROUPS * D_STATE:].reshape(B_, L, NGROUPS, D_STATE)
            dt = jax.nn.softplus(dt + dt_bias)
            A = -jnp.exp(A_log)
            nc = L // CHUNK
            r = NHEADS // NGROUPS
            xc = x.reshape(B_, nc, CHUNK, NGROUPS, r, HEADDIM)
            dtc = dt.reshape(B_, nc, CHUNK, NGROUPS, r)
            Bc = Bm.reshape(B_, nc, CHUNK, NGROUPS, D_STATE)
            Cc = Cm.reshape(B_, nc, CHUNK, NGROUPS, D_STATE)
            xdt = xc * dtc[..., None]
            dA = dtc * A.reshape(NGROUPS, r)
            dA = jnp.transpose(dA, (0, 3, 4, 1, 2))
            A_cs = jnp.cumsum(dA, axis=-1)
            Lmat = jnp.exp(_segsum(dA))
            Y_diag = jnp.einsum('bclgn,bcsgn,bgrcls,bcsgrp->bclgrp', Cc, Bc, Lmat, xdt)
            decay_states = jnp.exp(A_cs[..., -1:] - A_cs)
            states = jnp.einsum('bcsgn,bgrcs,bcsgrp->bcgrpn', Bc, decay_states, xdt)
            chunk_decay = jnp.exp(A_cs[..., -1])
            states_t = jnp.moveaxis(states, 1, 0)
            decay_t = jnp.moveaxis(chunk_decay, -1, 0)

            def step(S, inp):
                d, st = inp
                S_new = S * d[..., None, None] + st
                return (S_new, S)
            S0 = jnp.zeros(states_t.shape[1:], states_t.dtype)
            _, prev_states = jax.lax.scan(step, S0, (decay_t, states_t))
            prev_states = jnp.moveaxis(prev_states, 0, 1)
            state_decay = jnp.exp(A_cs)
            Y_off = jnp.einsum('bclgn,bcgrpn,bgrcl->bclgrp', Cc, prev_states, state_decay)
            Y = (Y_diag + Y_off).reshape(B_, nc, CHUNK, NHEADS, HEADDIM)
            Y = Y + x.reshape(B_, nc, CHUNK, NHEADS, HEADDIM) * D[:, None]
            y = Y.reshape(B_, L, D_INNER)
            y = y * jax.nn.silu(z)
            y = y * jax.lax.rsqrt(jnp.mean(y * y, axis=-1, keepdims=True) + EPS) * norm_weight
            return y @ out_proj_kernel
        return _mamba2_forward(u, in_proj_kernel, conv1d_weight, conv1d_bias, dt_bias, A_log, D, norm_weight, out_proj_kernel)

    def _L0_ffn_ref(x, gate_W_packed, gate_scales, up_W_packed, up_scales, down_W_packed, down_scales):
        import jax, jax.numpy as jnp
        import numpy as np
        BLOCK_SIZE = 32
        HIDDEN_SIZE = 256
        MLP_DIM = 2048
        NVFP4_LUT = jnp.array([0.0, 0.5, 1.0, 1.5, 2.0, 3.0, 4.0, 6.0, 0.0, -0.5, -1.0, -1.5, -2.0, -3.0, -4.0, -6.0], dtype=jnp.float32)

        def dequant_nvfp4(W_packed, scales, block=BLOCK_SIZE):
            N = W_packed.shape[0]
            low = W_packed & 15
            high = W_packed >> 4 & 15
            idx = jnp.stack([low, high], axis=-1).reshape(N, -1)
            vals = NVFP4_LUT[idx]
            K = vals.shape[1]
            vals = vals.reshape(N, K // block, block) * scales[:, :, None]
            return vals.reshape(N, K)
        B, S, H = x.shape
        xt = x.reshape(B * S, H)
        Wg = dequant_nvfp4(gate_W_packed, gate_scales)
        Wu = dequant_nvfp4(up_W_packed, up_scales)
        Wd = dequant_nvfp4(down_W_packed, down_scales)
        gate = jnp.einsum('th,nh->tn', xt, Wg)
        up = jnp.einsum('th,nh->tn', xt, Wu)
        gelu = jnp.tanh(0.7978845608028654 * (gate + 0.044715 * gate ** 3)) * gate * 0.5 + gate * 0.5
        inter = gelu * up
        out = jnp.einsum('tn,hn->th', inter, Wd)
        return out.reshape(B, S, H)
    x = L0_attn_u
    x = x + _layernorm(_L0_attn_ref(_layernorm(x, axis=-1), L0_attn_in_proj_kernel, L0_attn_conv1d_weight, L0_attn_conv1d_bias, L0_attn_dt_bias, L0_attn_A_log, L0_attn_D, L0_attn_norm_weight, L0_attn_out_proj_kernel), axis=-1)
    x = x + _layernorm(_L0_ffn_ref(_layernorm(x, axis=-1), L0_ffn_gate_W_packed, L0_ffn_gate_scales, L0_ffn_up_W_packed, L0_ffn_up_scales, L0_ffn_down_W_packed, L0_ffn_down_scales), axis=-1)
    return x

_drawn_inputs = setup_inputs


def setup_inputs(seed=0):
    import zlib

    import numpy as np

    out = dict(_drawn_inputs(seed))
    spreads = {'L0_attn_conv1d_bias': (0.0, 0.1),
     'L0_attn_D': (1.0, 0.2),
     'L0_attn_norm_weight': (1.0, 0.2)}
    factors = {}
    for name, (base, spread) in spreads.items():
        noise = np.random.default_rng([zlib.crc32(name.encode()), seed]).standard_normal(out[name].shape)
        drawn = base * np.exp(spread * noise) if base else spread * noise
        out[name] = jnp.asarray(drawn.astype(out[name].dtype))
    for name, factor in factors.items():
        out[name] = (out[name] * factor).astype(out[name].dtype)
    return out
```

```python
from contextlib import ExitStack

import numpy as np

import concourse.bass as bass
from concourse import mybir

ALU = mybir.AluOpType
ACT = mybir.ActivationFunctionType
F32 = mybir.dt.float32
F32R = mybir.dt.float32r
F16 = mybir.dt.float16
BF16 = mybir.dt.bfloat16
I32 = mybir.dt.int32

P = 128
BATCH, SEQ, DM = 4, 1024, 256
HEADS, HD, DI, NSTATE, TAPS = 8, 64, 512, 128, 4
CONV = DI + 2 * NSTATE
ZX = 2 * DI + 2 * NSTATE + HEADS
MLP, SBLK = 2048, 32
EPS = 1e-5
BLK = 512
NBLK = BATCH * SEQ // BLK
SUB = 256
CH = 128
KD = DM // P
KI = DI // P
CT = CONV // P
NT = MLP // P
TT = BLK // P
TINY = 1e-30
MASKED = -1e30
PIECE = 256
PIECES = MLP // PIECE
MATS = 3

PASSES = ((0, 0), (0, 1), (1, 0))


def mamba_bank_uses():
    uses = []
    for j in range(2):
        uses += [("xt", j), ("dt", j)] + [("ip", 3 * j + r) for r in range(3)] + [("cs", j)]
        uses += [("seg", 4 * j + r) for r in range(4)] + [("z", 2 * j), ("z", 2 * j + 1), ("gb", j)]
        a, b = 2 * j, 2 * j + 1
        uses += [("xtr", a), ("yo", a), ("yd", a), ("st", a), ("yt", a), ("xtr", b)]
        uses += [("yo", b), ("yd", b), ("st", b), ("out", a), ("yt", b), ("out", b)]
    return uses


def ffn_bank_uses():
    uses = [("x1t", 0), ("x1t", 1)]
    for n in range(NT):
        uses += [("gate", n), ("up", n)]
    return uses


def earlier_use(uses, u):
    if u >= 3:
        return u - 3, 0
    return max(v for v in range(len(uses)) if v % 3 == u % 3), 1


def sub_steps(j, ffn):
    f = [[("ffn", 8 * j + r)] if ffn else [] for r in range(8)]
    a, b = 2 * j, 2 * j + 1
    s = [("ln1", j), ("xt", j), ("dt", j)]
    if j == 0 and ffn:
        s += [("x1t", 0), ("x1t", 1)]
    s += [("ip", 3 * j + r) for r in range(3)]
    s += [("cs", j)] + [("seg", 4 * j + r) for r in range(4)]
    s += [("silu", 3 * j + r) for r in range(3)] + [("z", a), ("z", b)]
    s += f[0] + [("gb", j), ("m", a)] + f[1] + [("xtr", a)] + f[2] + [("y", a), ("m", b)]
    s += f[3] + [("yt", a), ("xtr", b), ("y", b)] + f[4] + [("out", a), ("yt", b)] + f[5] + f[6] + [("out", b)] + f[7]
    return s


def iteration_steps(mamba, ffn):
    if not mamba:
        return [("x1t", 0), ("x1t", 1)] + [("ffn", n) for n in range(NT)] + [("fin", 0)]
    return sub_steps(0, ffn) + sub_steps(1, ffn) + ([("fin", 0)] if ffn else [])


def prologue_steps():
    steps = iteration_steps(True, False)
    pieces = [("dq", q) for q in range(MATS * PIECES)]
    out = []
    for n, s in enumerate(steps):
        out.append(s)
        if n >= 6:
            take = 1
            out += pieces[:take]
            pieces = pieces[take:]
    return out + pieces


def build(nc, u, in_proj, conv_w, conv_b, dt_bias, a_log, d_skip, norm_w, out_proj,
          packed, scales, out):
    ctx = ExitStack()
    with ctx:
        def sb(name, shape, dt=F32, stack=ctx):
            return stack.enter_context(nc.sbuf_tensor(name, shape, dt))

        def sem(name):
            return ctx.enter_context(nc.semaphore(name))

        wi = sb("wi", [P, 2, KD, ZX], F32R)
        wo = sb("wo", [P, 2, KI, DM], F32R)
        wg = sb("wg", [P, 2, KD, MLP], F32R)
        wu = sb("wu", [P, 2, KD, MLP], F32R)
        wd = sb("wd", [P, 2, NT, DM], F32R)
        ident = sb("ident", [P, P])
        upto = sb("upto", [P, P])
        after = sb("after", [P, P])
        ones = sb("ones", [P, P])
        ident_b = sb("ident_b", [P, P], BF16)
        masked_b = sb("masked_b", [P, P], BF16)
        pick = sb("pick", [96, 16], BF16)
        unpick = sb("unpick", [96, 16], BF16)
        neg_half = sb("neg_half", [P, TT])
        cw = sb("cw", [P, CT, TAPS])
        cb = sb("cb", [P, CT])
        dtb = sb("dtb", [P, HEADS])
        a_neg = sb("a_neg", [P, HEADS])
        dsk = sb("dsk", [P, HEADS])
        nw = sb("nw", [P, KI])
        xb = sb("xb", [P, 2, TT, DM])
        xn = sb("xn", [P, 2, DM])
        xnt = sb("xnt", [P, 2, KD, SUB], F32R)
        raw = sb("raw", [P, CT, SUB + TAPS - 1])
        xc = sb("xc", [P, CT, SUB])
        sz = sb("sz", [P, 2, DI])
        xdt = sb("xdt", [P, DI])
        t1 = sb("t1", [P, DI])
        yg = sb("yg", [P, DI])
        state = sb("state", [P, DI])
        yt = sb("yt", [P, 2, KI, CH], F32R)
        x1n = sb("x1n", [P, 2, 2, 2, CH])
        da = sb("da", [P, 3, 32])
        t3 = sb("t3", [96, CH], BF16)
        rest3 = sb("rest3", [96, CH])
        ex = sb("ex", [P, 3, 2, HEADS])
        pause = sb("pause", [P, 1])
        st1 = sb("st1", [P, 2, 6])
        mv1 = sb("mv1", [P, 2, 2])
        ve1 = sb("ve1", [P, 2])
        rs1 = sb("rs1", [P, 2])
        st2 = sb("st2", [P, 6])
        mv2 = sb("mv2", [P, 2])
        e2 = sb("e2", [P, 1])
        ve2 = sb("ve2", [P, 1])
        rs2 = sb("rs2", [P, 1])
        mr2 = sb("mr2", [P, 1])
        st3 = sb("st3", [P, 6])
        mv3 = sb("mv3", [P, 2])
        ve3 = sb("ve3", [P, 1])
        rs3 = sb("rs3", [P, 1])
        ssq = sb("ssq", [P, 4])
        spa = sb("spa", [P, 2 * HEADS])
        spn = sb("spn", [P, 2 * HEADS])
        spe = sb("spe", [P, 2 * HEADS])
        spl = sb("spl", [P, 2 * HEADS])
        spw = sb("spw", [P, 2 * HEADS])
        spr = sb("spr", [P, 2 * HEADS])
        dt_ = sb("dt_", [P, 2 * HEADS])
        st4 = sb("st4", [P, TT, 6])
        mv4 = sb("mv4", [P, TT, 2])
        ve4 = sb("ve4", [P, TT])
        rs4 = sb("rs4", [P, TT])
        mr4 = sb("mr4", [P, TT])
        x1t = sb("x1t", [P, 2, KD, BLK], F32R)
        with ExitStack() as early:
            wi_raw = sb("wi_raw", [P, KD, ZX], F32, early)
        lmat = sb("lmat", [P, 2, HEADS, CH])
        gb = sb("gb", [P, 4, CH])
        xdd = sb("xdd", [P, DI])
        with ExitStack() as early:
            words = sb("words", [P, 2, PIECE], I32, early)
            scl = sb("scl", [P, 2, PIECE], F32, early)
            spread = sb("spread", [P, PIECE], I32, early)
            mags = sb("mags", [P, PIECE], I32, early)
            signs = sb("signs", [P, PIECE], I32, early)
            wf = sb("wf", [P, 2, 2, PIECE], F32, early)
        with ExitStack() as early:
            wo_raw = sb("wo_raw", [P, KI, DM], F32, early)
        hid = sb("hid", [P, 2, BLK])
        hl = sb("hl", [P, 2, 2, BLK], F32R)

        mb = [ctx.enter_context(nc.psum_tensor(f"mb{b}", [P, 512], F32)) for b in range(3)]
        fb = [ctx.enter_context(nc.psum_tensor(f"fb{b}", [P, 512], F32)) for b in range(3)]
        db = [ctx.enter_context(nc.psum_tensor(f"db{b}", [P, 512], F32)) for b in range(2)]

        x_loaded = [sem(f"x_loaded{j}") for j in range(2)]
        out_stored = sem("out_stored")
        small_loaded = sem("small_loaded")
        wi_loaded = sem("wi_loaded")
        wo_loaded = sem("wo_loaded")
        piece_loaded = [sem(f"piece_loaded{r}") for r in range(2)]
        consts_ready = sem("consts_ready")
        setup = sem("setup")
        dve_setup = sem("dve_setup")
        wi_hi = sem("wi_hi")
        wi_ready = sem("wi_ready")
        wo_scaled = sem("wo_scaled")
        wo_hi = sem("wo_hi")
        wo_ready = sem("wo_ready")
        dve_dq = sem("dve_dq")
        piece_f32 = sem("piece_f32")
        piece_hi = sem("piece_hi")
        piece_lo = sem("piece_lo")

        per_block = dict(
            var1=2, rstd1=2, xn=2, xt=2, xnt_hi=2, xnt=2, dt=2, dt_read=2, spn=2, spe=2, softln=2, da=2,
            cs=2, ex=2, cs_read=2, t3=2, seg=8, lmat=8, ip=6, tap=6, conv=6, xc=6, hist=2,
            z=4, sz=4, gb=2, gbs=2, m=4, xtr=4, xdt=4, skip=4, xdd=4, yo=4, t1=4, yd=4, st=4,
            decayed=4, yskip=4, ydiag=4, state=4, y=4, yt=4, ssq=4, yt_hi=4, yts=4, out=4,
            var2=4, rstd2=4, attn=4, var3=4, rstd3=4, x1n=4,
            x1t=2, x1t_hi=2, x1ts=2, gate=NT, up=NT, gelu=NT, inter=NT, hi=NT, lo=NT, down=NT,
            var4=1, rstd4=1, d_read=1, outs=2, dve_m=80, dve_f=3)
        s = {name: sem("s_" + name) for name in per_block}

        def count(name, i, k):
            return i * per_block[name] + (k + 1)

        m_uses, f_uses = mamba_bank_uses(), ffn_bank_uses()
        read_by = dict(xt="xnt", dt="dt_read", ip="tap", cs="cs_read", seg="lmat", z="sz", gb="gbs",
                       xtr="skip", yo="t1", yd="ydiag", st="state", yt="yts", out="attn",
                       x1t="x1ts", gate="gelu", up="inter")
        m_bank = {use: mb[n % 3] for n, use in enumerate(m_uses)}
        f_bank = {use: fb[n % 3] for n, use in enumerate(f_uses)}

        def drive(eng, do, prologue):
            def iteration(i, par):
                for name, k in iteration_steps(True, True):
                    if name in do:
                        ffn = name in ("x1t", "ffn", "fin")
                        do[name](i - 1 if ffn else i, 1 - par if ffn else par, k)

            prologue()
            for name, k in prologue_steps():
                if name in do:
                    do[name](0, 0, k)
            iteration(1, 1)
            with eng.Fori(0, (NBLK - 2) // 2) as pair:
                for half in range(2):
                    iteration(pair * 2 + (2 + half), half)
            for name, k in iteration_steps(False, True):
                if name in do:
                    do[name](NBLK - 1, 1, k)

        u_v = u.rearrange("b (i j c p) d -> (b i) j p c d", j=2, c=2, p=P)
        o_v = out.rearrange("b (i j c p) d -> (b i) j p c d", j=2, c=2, p=P)

        def per_head(ap):
            return ap.rearrange("p (h q) -> p h q", h=HEADS)

        def spread_heads(ap):
            return ap.unsqueeze(2).broadcast_to([P, HEADS, HD])

        def weight_piece(mat, part, c0):
            if mat < 2:
                return (wg, wu)[mat][:, part, :, c0:c0 + PIECE]
            return wd[:, part, 2 * (c0 // DM):2 * (c0 // DM) + 2, :]

        def wf_piece(mat, r):
            return wf[:, r, :, :]

        block = ctx.enter_context(nc.Block())

        @block.sync
        def _(sp):
            def load_x(i, par, j):
                src = u_v[bass.ds(i, 1), j].rearrange("o p c d -> (o p) c d")
                sp.dma_start(xb[:, par, 2 * j:2 * j + 2, :], src).then_inc(x_loaded[j], 16)

            load_x(0, 0, 0)
            sp.dma_start(wi_raw[:], in_proj.rearrange("(k p) n -> p k n", p=P)).then_inc(wi_loaded, 16)
            for dst, src in ((cw, conv_w), (cb, conv_b), (nw, norm_w)):
                sp.dma_start(dst[:], src).then_inc(small_loaded, 16)
            for dst, src in ((dtb, dt_bias), (a_neg, a_log), (dsk, d_skip)):
                sp.dma_start(dst[:], src.partition_broadcast(P)).then_inc(small_loaded, 16)
            load_x(0, 0, 1)
            sp.dma_start(wo_raw[:], out_proj.rearrange("(k p) n -> p k n", p=P)).then_inc(wo_loaded, 16)
            for q in range(MATS * PIECES):
                mat, c0, r = q // PIECES, q % PIECES * PIECE, q % 2
                if q == 0:
                    sp.wait_ge(wo_ready, 1)
                if q >= 2:
                    sp.wait_ge(piece_f32, q - 1)
                sp.dma_start(words[:, r, :], packed[mat, :, c0:c0 + PIECE]).then_inc(piece_loaded[r], 16)
                sp.dma_start(scl[:, r, :], scales[mat, :, c0:c0 + PIECE].unsqueeze(1)
                             .broadcast_to([8, SBLK // 2, PIECE])).then_inc(piece_loaded[r], 16)
                if q == 4:
                    for j in range(2):
                        load_x(1, 1, j)

            def store(f, par, refill):
                for j in range(2):
                    sp.wait_ge(s["outs"], count("outs", f, j))
                    dst = o_v[bass.ds(f, 1), j].rearrange("o p c d -> (o p) c d")
                    sp.dma_start(dst, xb[:, par, 2 * j:2 * j + 2, :]).then_inc(out_stored, 16)
                for j in range(2):
                    if refill:
                        sp.wait_ge(out_stored, f * 32 + 32)
                        load_x(f + 2, par, j)

            with sp.Fori(0, (NBLK - 2) // 2) as pair:
                for half in range(2):
                    store(pair * 2 + half, half, True)
            store(NBLK - 2, 0, False)
            store(NBLK - 1, 1, False)
            sp.wait_ge(out_stored, NBLK * 32)

        @block.gpsimd
        def _(pool):
            def consts():
                n = [0]

                def link(ins):
                    n[0] += 1
                    ins.then_inc(setup, 1)
                    pool.wait_ge(setup, n[0])

                pool.memset(neg_half[:], -0.5)
                pool.memset(ones[:], 1.0)
                pool.memset(ident[:], 0.0)
                pool.memset(ident_b[:], 0.0)
                pool.memset(masked_b[:], 0.0)
                pool.memset(upto[:], 1.0)
                pool.memset(after[:], 0.0)
                pool.memset(pick[:], 0.0)
                pool.memset(da[:], 0.0)
                pool.memset(state[:], 0.0)
                pool.memset(raw[:, :, 0:TAPS - 1], 0.0)
                link(pool.memset(unpick[:], 0.0))
                for m in (ident, ident_b):
                    pool.affine_select(out=m[:], in_=m[:], compare_op=ALU.not_equal, fill=1.0, base=0,
                                       pattern=[[-1, P]], channel_multiplier=1)
                pool.affine_select(out=upto[:], in_=upto[:], compare_op=ALU.is_ge, fill=0.0, base=0,
                                   pattern=[[1, P]], channel_multiplier=-1)
                pool.affine_select(out=after[:], in_=after[:], compare_op=ALU.is_ge, fill=1.0, base=0,
                                   pattern=[[1, P]], channel_multiplier=-1)
                pool.affine_select(out=masked_b[:], in_=masked_b[:], compare_op=ALU.is_ge, fill=MASKED, base=0,
                                   pattern=[[1, P]], channel_multiplier=-1)
                for part in range(3):
                    a = pool.affine_select(out=pick[:], in_=pick[:], compare_op=ALU.not_equal, fill=1.0,
                                           base=-32 * part, pattern=[[-1, 16]], channel_multiplier=1)
                    b = pool.affine_select(out=unpick[:], in_=unpick[:], compare_op=ALU.not_equal, fill=-1.0,
                                           base=-32 * part, pattern=[[-1, 16]], channel_multiplier=1)
                    if part < 2:
                        link(b)
                b.then_inc(consts_ready, 1)

            def rstd(name, dst, src, i, k):
                pool.wait_ge(s["var" + name], count("var" + name, i, k))
                pool.tensor_tensor(dst, src, neg_half[:, 0:src.shape[1]], ALU.pow).then_inc(s["rstd" + name], 1)

            def ln1(i, par, j):
                rstd("1", rs1[:], ve1[:], i, j)

            def xtr(i, par, q):
                pool.wait_ge(s["ex"], count("ex", i, q // 2))
                pool.wait_ge(s["xdt"], count("xdt", i, q))
                pool.tensor_tensor(per_head(xdd[:]), per_head(xdt[:]), spread_heads(ex[:, 1, q % 2, :]),
                                   ALU.mult).then_inc(s["xdd"], 1)

            def y(i, par, q):
                pool.wait_ge(s["yo"], count("yo", i, q))
                pool.tensor_tensor(per_head(state[:]), per_head(state[:]), spread_heads(ex[:, 2, q % 2, :]),
                                   ALU.mult).then_inc(s["decayed"], 1)
                pool.wait_ge(s["t1"], count("t1", i, q))
                pool.tensor_tensor(yg[:], yg[:], t1[:], ALU.add).then_inc(s["yskip"], 1)

            def out_(i, par, q):
                rstd("2", rs2[:], ve2[:], i, q)
                rstd("3", rs3[:], ve3[:], i, q)

            def lo(f, n):
                pool.wait_ge(s["hi"], count("hi", f, n))
                pool.tensor_tensor(hl[:, n % 2, 1, :], hid[:, n % 2, :], hl[:, n % 2, 0, :].bitcast(F32),
                                   ALU.subtract).then_inc(s["lo"], 1)

            def ffn(f, par, n):
                if n:
                    lo(f, n - 1)
                if n == NT - 1:
                    lo(f, n)

            def fin(f, par, _):
                rstd("4", rs4[:], ve4[:], f, 0)

            def dq(i, par, q):
                mat, c0, r = q // PIECES, q % PIECES * PIECE, q % 2
                pool.wait_ge(piece_hi, q + 1)
                pool.tensor_tensor(weight_piece(mat, 1, c0), wf_piece(mat, r),
                                   weight_piece(mat, 0, c0).bitcast(F32), ALU.subtract).then_inc(piece_lo, 1)

            drive(pool, dict(ln1=ln1, xtr=xtr, y=y, out=out_, ffn=ffn, fin=fin, dq=dq), consts)

        @block.scalar
        def _(act):
            def setup_act():
                act.wait_ge(small_loaded, 96)
                act.activation(a_neg[:], a_neg[:], ACT.Exp).then_inc(dve_setup, 1)
                act.wait_ge(wi_loaded, 16)
                act.activation(wi[:, 0, :, :], wi_raw[:], ACT.Copy).then_inc(wi_hi, 1)
                act.wait_ge(wo_scaled, 1)
                act.activation(wo[:, 0, :, :], wo_raw[:], ACT.Copy).then_inc(wo_hi, 1)

            def xt(i, par, j):
                act.wait_ge(s["xt"], count("xt", i, j))
                act.activation(xnt[:, 0, :, :], m_bank["xt", j][:], ACT.Copy).then_inc(s["xnt_hi"], 1)

            def dt(i, par, j):
                act.preload_act_table_set("natural_log_exp_and_others")
                act.wait_ge(s["spn"], count("spn", i, j))
                act.activation(spe[:], spn[:], ACT.Exp).then_inc(s["spe"], 1)
                act.wait_ge(s["spe"], count("spe", i, j))
                act.activation(spl[:], spe[:], ACT.Ln, bias=1.0).then_inc(s["softln"], 1)

            def cs(i, par, j):
                act.wait_ge(s["cs"], count("cs", i, j))
                act.activation(ex[:].rearrange("p a c h -> p (a c h)"), m_bank["cs", j][:, 0:48],
                               ACT.Exp).then_inc(s["ex"], 1)

            def seg(i, par, k):
                c, h = k // 2 % 2, k % 2
                act.wait_ge(s["seg"], count("seg", i, k))
                act.activation(lmat[:, c, 4 * h:4 * h + 4, :].rearrange("p h l -> p (h l)"), m_bank["seg", k][:],
                               ACT.Exp).then_inc(s["lmat"], 1)

            def ip(i, par, k):
                j, pr = k // 3, k % 3
                act.wait_ge(s["ip"], count("ip", i, k))
                if j or not (isinstance(i, int) and i == 0):
                    act.wait_ge(s["hist"], count("hist", i, j - 1))
                ps = m_bank["ip", k][:].rearrange("p (two t) -> p two t", two=2)
                act.activation(raw[:, 2 * pr:2 * pr + 2, TAPS - 1:], ps, ACT.Copy)
                for e in range(2):
                    ct = 2 * pr + e
                    last = act.activation(xc[:, ct, :], ps[:, e, :], ACT.Identity, bias=cb[:, ct:ct + 1],
                                          scale=cw[:, ct, TAPS - 1:TAPS])
                last.then_inc(s["tap"], 1)

            def silu(i, par, k):
                pr = k % 3
                act.wait_ge(s["conv"], count("conv", i, k))
                act.activation(xc[:, 2 * pr:2 * pr + 2, :], xc[:, 2 * pr:2 * pr + 2, :], ACT.Silu).then_inc(s["xc"], 1)

            def z(i, par, q):
                act.wait_ge(s["z"], count("z", i, q))
                act.activation(sz[:, q % 2, :], m_bank["z", q][:], ACT.Silu).then_inc(s["sz"], 1)

            def gb_(i, par, j):
                act.wait_ge(s["gb"], count("gb", i, j))
                act.activation(gb[:].rearrange("p a l -> p (a l)"), m_bank["gb", j][:], ACT.Copy).then_inc(s["gbs"], 1)

            def yt_(i, par, q):
                act.wait_ge(s["y"], count("y", i, q))
                act.activation(t1[:], yg[:], ACT.Square, accum_out=ssq[:, q:q + 1]).then_inc(s["ssq"], 1)
                act.wait_ge(s["yt"], count("yt", i, q))
                act.activation(yt[:, 0, :, :].rearrange("p k t -> p (k t)"), m_bank["yt", q][:],
                               ACT.Copy).then_inc(s["yt_hi"], 1)

            def x1t_(f, par, j):
                act.wait_ge(s["x1t"], count("x1t", f, j))
                act.activation(x1t[:, 0, :, SUB * j:SUB * j + SUB],
                               f_bank["x1t", j][:].rearrange("p (k t) -> p k t", k=KD),
                               ACT.Copy).then_inc(s["x1t_hi"], 1)

            def hi(f, n):
                act.wait_ge(s["inter"], count("inter", f, n))
                if n >= 2 or not (isinstance(f, int) and f == 0):
                    act.wait_ge(s["down"], count("down", f, n - 2))
                act.activation(hl[:, n % 2, 0, :], hid[:, n % 2, :], ACT.Copy).then_inc(s["hi"], 1)

            def ffn(f, par, n):
                if n:
                    hi(f, n - 1)
                act.wait_ge(s["gate"], count("gate", f, n))
                if n >= 2 or not (isinstance(f, int) and f == 0):
                    act.wait_ge(s["lo"], count("lo", f, n - 2))
                elif n == 0:
                    act.wait_ge(piece_lo, MATS * PIECES)
                act.activation(hid[:, n % 2, :], f_bank["gate", n][:], ACT.Gelu_apprx_tanh).then_inc(s["gelu"], 1)
                if n == NT - 1:
                    hi(f, n)

            def dq(i, par, q):
                mat, c0, r = q // PIECES, q % PIECES * PIECE, q % 2
                act.wait_ge(piece_f32, q + 1)
                act.activation(weight_piece(mat, 0, c0), wf_piece(mat, r), ACT.Copy).then_inc(piece_hi, 1)

            drive(act, dict(xt=xt, dt=dt, cs=cs, seg=seg, ip=ip, silu=silu, z=z, gb=gb_, yt=yt_, x1t=x1t_,
                            ffn=ffn, dq=dq), setup_act)

        @block.vector
        def _(dve):
            links = {"dve_m": 0, "dve_f": 0}

            def link(name, i, ins, wait=True):
                k = links[name]
                links[name] += 1
                ins.then_inc(s[name], 1)
                if wait:
                    dve.wait_ge(s[name], count(name, i, k % per_block[name]))
                return k % per_block[name]

            def before_aggr(name, i, ins):
                link(name, i, ins)
                dve.memset(pause[:], 0.0)

            def setup_dve():
                dve.wait_ge(dve_setup, 1)
                dve.tensor_scalar(a_neg[:], a_neg[:], -1.0, None, ALU.mult).then_inc(dve_setup, 1)
                dve.wait_ge(wi_hi, 1)
                dve.tensor_tensor(wi[:, 1, :, :], wi_raw[:], wi[:, 0, :, :].bitcast(F32), ALU.subtract).then_inc(wi_ready, 1)
                dve.wait_ge(wo_loaded, 16)
                for k in range(KI):
                    last = dve.tensor_scalar(wo_raw[:, k, :], wo_raw[:, k, :], nw[:, k:k + 1], None, ALU.mult)
                last.then_inc(wo_scaled, 1)
                dve.wait_ge(wo_hi, 1)
                dve.tensor_tensor(wo[:, 1, :, :], wo_raw[:], wo[:, 0, :, :].bitcast(F32), ALU.subtract).then_inc(wo_ready, 1)
                dve.wait_ge(dve_setup, 2)
                dve.wait_ge(consts_ready, 1)

            def ln1(i, par, j):
                dve.wait_ge(x_loaded[j], i * 16 + 16)
                x = xb[:, par, 2 * j:2 * j + 2, :]
                for c in range(2):
                    last = dve.bn_stats(st1[:, c, :], x[:, c, :])
                before_aggr("dve_m", i, last)
                for c in range(2):
                    last = dve.bn_aggr(mv1[:, c, :], st1[:, c, :])
                link("dve_m", i, last)
                dve.tensor_scalar(ve1[:], mv1[:, :, 1], EPS, None, ALU.add).then_inc(s["var1"], 1)
                dve.wait_ge(s["rstd1"], count("rstd1", i, j))
                if j or not (isinstance(i, int) and i == 0):
                    dve.wait_ge(s["xt"], count("xt", i, j - 1))
                for c in range(2):
                    last = dve.tensor_scalar(xn[:, c, :], x[:, c, :], mv1[:, c, 0:1], rs1[:, c:c + 1],
                                             ALU.subtract, ALU.mult)
                last.then_inc(s["xn"], 1)

            def xt(i, par, j):
                dve.wait_ge(s["xnt_hi"], count("xnt_hi", i, j))
                dve.tensor_tensor(xnt[:, 1, :, :], m_bank["xt", j][:].rearrange("p (k t) -> p k t", k=KD),
                                  xnt[:, 0, :, :].bitcast(F32), ALU.subtract).then_inc(s["xnt"], 1)

            def dt(i, par, j):
                dve.wait_ge(s["dt"], count("dt", i, j))
                dve.tensor_tensor(spa[:].rearrange("p (c h) -> p c h", c=2),
                                  m_bank["dt", j][:, 0:16].rearrange("p (c h) -> p c h", c=2),
                                  dtb[:].unsqueeze(1).broadcast_to([P, 2, HEADS]), ALU.add).then_inc(s["dt_read"], 1)
                dve.wait_ge(s["dt_read"], count("dt_read", i, j))
                dve.scalar_tensor_tensor(out=spn[:], in0=spa[:], scalar=-1.0, in1=spa[:], op0=ALU.mult,
                                         op1=ALU.min).then_inc(s["spn"], 1)
                dve.wait_ge(s["softln"], count("softln", i, j))
                link("dve_m", i, dve.tensor_scalar(spw[:], spe[:], 1.0, 1.0, ALU.add, ALU.subtract))
                link("dve_m", i, dve.tensor_scalar(spw[:], spw[:], TINY, None, ALU.max))
                link("dve_m", i, dve.reciprocal(spr[:], spw[:]))
                link("dve_m", i, dve.scalar_tensor_tensor(out=spw[:], in0=spl[:], scalar=TINY, in1=spr[:],
                                                          op0=ALU.max, op1=ALU.mult))
                link("dve_m", i, dve.scalar_tensor_tensor(out=spr[:], in0=spw[:], scalar=1.0, in1=spe[:],
                                                          op0=ALU.min, op1=ALU.mult))
                link("dve_m", i, dve.scalar_tensor_tensor(out=dt_[:], in0=spa[:], scalar=0.0, in1=spr[:],
                                                          op0=ALU.max, op1=ALU.add))
                shape = [P, 3, 2, HEADS]
                dve.tensor_tensor(da[:, :, 0:16].rearrange("p r (c h) -> p r c h", c=2),
                                  dt_[:].rearrange("p (c h) -> p c h", c=2).unsqueeze(1).broadcast_to(shape),
                                  a_neg[:].unsqueeze(1).unsqueeze(1).broadcast_to(shape), ALU.mult).then_inc(s["da"], 1)

            def cs(i, par, j):
                ps = m_bank["cs", j][0:96, 128:256]
                dve.wait_ge(s["ex"], count("ex", i, j))
                link("dve_m", i, dve.tensor_copy(t3[:], ps))
                dve.tensor_tensor(rest3[0:64, :], ps[0:64, :], t3[0:64, :], ALU.subtract).then_inc(s["cs_read"], 1)
                dve.wait_ge(s["cs_read"], count("cs_read", i, j))
                link("dve_m", i, dve.tensor_copy(t3[0:64, :], rest3[0:64, :]))
                link("dve_m", i, dve.tensor_tensor(rest3[0:32, :], rest3[0:32, :], t3[0:32, :], ALU.subtract))
                dve.tensor_copy(t3[0:32, :], rest3[0:32, :]).then_inc(s["t3"], 1)

            def ip(i, par, k):
                j, pr = k // 3, k % 3
                dve.wait_ge(s["tap"], count("tap", i, k))
                if pr == 0 and (j or not (isinstance(i, int) and i == 0)):
                    dve.wait_ge(s["hist"], count("hist", i, j - 1))
                at = {}
                for tap in (2, 1, 0):
                    for e in range(2):
                        ct = 2 * pr + e
                        if e in at:
                            dve.wait_ge(s["dve_m"], count("dve_m", i, at[e]))
                        ins = dve.scalar_tensor_tensor(out=xc[:, ct, :], in0=raw[:, ct, tap:tap + SUB],
                                                       scalar=cw[:, ct, tap:tap + 1], in1=xc[:, ct, :],
                                                       op0=ALU.mult, op1=ALU.add)
                        if tap == 0 and e == 1:
                            ins.then_inc(s["conv"], 1)
                        else:
                            at[e] = link("dve_m", i, ins, wait=False)
                if pr == 2:
                    dve.wait_ge(s["conv"], count("conv", i, k))
                    if par == 1 and j == 1:
                        last = dve.memset(raw[:, :, 0:TAPS - 1], 0.0)
                    else:
                        last = dve.tensor_copy(raw[:, :, 0:TAPS - 1], raw[:, :, SUB:SUB + TAPS - 1])
                    last.then_inc(s["hist"], 1)

            def m(i, par, q):
                c = q % 2
                dve.wait_ge(s["lmat"], count("lmat", i, 2 * q + 1))
                dve.wait_ge(s["gbs"], count("gbs", i, q // 2))
                dve.tensor_tensor(lmat[:, c, :, :], lmat[:, c, :, :],
                                  gb[:, c, :].unsqueeze(1).broadcast_to([P, HEADS, CH]), ALU.mult).then_inc(s["m"], 1)

            def xtr(i, par, q):
                c = q % 2
                ps = per_head(m_bank["xtr", q][:])
                dve.wait_ge(s["xtr"], count("xtr", i, q))
                dve.tensor_tensor(per_head(xdt[:]), ps, spread_heads(dt_[:, 8 * c:8 * c + 8]), ALU.mult).then_inc(s["xdt"], 1)
                dve.tensor_tensor(per_head(yg[:]), ps, spread_heads(dsk[:]), ALU.mult).then_inc(s["skip"], 1)

            def y(i, par, q):
                c = q % 2
                dve.wait_ge(s["yo"], count("yo", i, q))
                dve.tensor_tensor(per_head(t1[:]), per_head(m_bank["yo", q][:]), spread_heads(ex[:, 0, c, :]),
                                  ALU.mult).then_inc(s["t1"], 1)
                dve.wait_ge(s["decayed"], count("decayed", i, q))
                dve.wait_ge(s["st"], count("st", i, q))
                if par == 1 and q == 3:
                    dve.memset(state[:], 0.0).then_inc(s["state"], 1)
                else:
                    dve.tensor_tensor(state[:], m_bank["st", q][:], state[:], ALU.add).then_inc(s["state"], 1)
                dve.wait_ge(s["yskip"], count("yskip", i, q))
                dve.wait_ge(s["yd"], count("yd", i, q))
                dve.tensor_tensor(yg[:], m_bank["yd", q][:], yg[:], ALU.add).then_inc(s["ydiag"], 1)
                dve.wait_ge(s["ydiag"], count("ydiag", i, q))
                dve.wait_ge(s["sz"], count("sz", i, q))
                dve.tensor_tensor(yg[:], yg[:], sz[:, c, :], ALU.mult).then_inc(s["y"], 1)

            def yt_(i, par, q):
                dve.wait_ge(s["yt_hi"], count("yt_hi", i, q))
                dve.tensor_tensor(yt[:, 1, :, :].rearrange("p k t -> p (k t)"), m_bank["yt", q][:],
                                  yt[:, 0, :, :].rearrange("p k t -> p (k t)").bitcast(F32),
                                  ALU.subtract).then_inc(s["yts"], 1)

            def out_(i, par, q):
                ps = m_bank["out", q][:, 0:DM]
                x = xb[:, par, q, :]
                dve.wait_ge(s["out"], count("out", i, q))
                before_aggr("dve_m", i, dve.bn_stats(st2[:], ps))
                link("dve_m", i, dve.bn_aggr(mv2[:], st2[:]))
                dve.wait_ge(s["ssq"], count("ssq", i, q))
                link("dve_m", i, dve.tensor_scalar(e2[:], ssq[:, q:q + 1], EPS / DI, EPS * EPS, ALU.mult, ALU.add))
                dve.tensor_tensor(ve2[:], mv2[:, 1:2], e2[:], ALU.add).then_inc(s["var2"], 1)
                dve.wait_ge(s["rstd2"], count("rstd2", i, q))
                link("dve_m", i, dve.tensor_tensor(mr2[:], mv2[:, 0:1], rs2[:], ALU.mult))
                dve.scalar_tensor_tensor(out=x, in0=ps, scalar=rs2[:], in1=x, op0=ALU.mult,
                                         op1=ALU.add).then_inc(s["attn"], 1)
                dve.wait_ge(s["attn"], count("attn", i, q))
                link("dve_m", i, dve.tensor_scalar(x, x, mr2[:], None, ALU.subtract))
                before_aggr("dve_m", i, dve.bn_stats(st3[:], x))
                link("dve_m", i, dve.bn_aggr(mv3[:], st3[:]))
                dve.tensor_scalar(ve3[:], mv3[:, 1:2], EPS, None, ALU.add).then_inc(s["var3"], 1)
                dve.wait_ge(s["rstd3"], count("rstd3", i, q))
                if not (isinstance(i, int) and i == 0):
                    dve.wait_ge(s["x1t"], count("x1t", i - 1, q // 2))
                dve.tensor_scalar(x1n[:, q // 2, q % 2, :, :], halves_even_odd(x), mv3[:, 0:1], rs3[:],
                                  ALU.subtract, ALU.mult).then_inc(s["x1n"], 1)

            def halves_even_odd(x):
                return x.rearrange("p (n two) -> p two n", two=2)

            def x1t_(f, par, j):
                dve.wait_ge(s["x1t_hi"], count("x1t_hi", f, j))
                dve.tensor_tensor(x1t[:, 1, :, SUB * j:SUB * j + SUB],
                                  f_bank["x1t", j][:].rearrange("p (k t) -> p k t", k=KD),
                                  x1t[:, 0, :, SUB * j:SUB * j + SUB].bitcast(F32), ALU.subtract).then_inc(s["x1ts"], 1)

            def ffn(f, par, n):
                dve.wait_ge(s["gelu"], count("gelu", f, n))
                dve.wait_ge(s["up"], count("up", f, n))
                dve.tensor_tensor(hid[:, n % 2, :], f_bank["up", n][:], hid[:, n % 2, :], ALU.mult).then_inc(s["inter"], 1)

            def fin(f, par, _):
                dve.wait_ge(s["down"], count("down", f, NT - 1))
                for t in range(TT):
                    last = dve.bn_stats(st4[:, t, :], db[t // 2][:, t % 2 * DM:t % 2 * DM + DM])
                before_aggr("dve_f", f, last)
                for t in range(TT):
                    last = dve.bn_aggr(mv4[:, t, :], st4[:, t, :])
                link("dve_f", f, last)
                dve.tensor_scalar(ve4[:], mv4[:, :, 1], EPS, None, ALU.add).then_inc(s["var4"], 1)
                dve.wait_ge(s["rstd4"], count("rstd4", f, 0))
                link("dve_f", f, dve.tensor_tensor(mr4[:], mv4[:, :, 0], rs4[:], ALU.mult))
                for t in range(TT):
                    x = xb[:, par, t, :]
                    last = dve.scalar_tensor_tensor(out=x, in0=db[t // 2][:, t % 2 * DM:t % 2 * DM + DM],
                                                    scalar=rs4[:, t:t + 1], in1=x, op0=ALU.mult, op1=ALU.add)
                last.then_inc(s["d_read"], 1)
                dve.wait_ge(s["d_read"], count("d_read", f, 0))
                for t in range(TT):
                    x = xb[:, par, t, :]
                    last = dve.tensor_scalar(x, x, mr4[:, t:t + 1], None, ALU.subtract)
                    if t % 2:
                        last.then_inc(s["outs"], 1)

            dq_links = [0]

            def dq(i, par, q):
                mat, r = q // PIECES, q % 2

                def step(ins):
                    dq_links[0] += 1
                    ins.then_inc(dve_dq, 1)
                    dve.wait_ge(dve_dq, dq_links[0])

                w = words[:, r, :]
                if q:
                    dve.wait_ge(piece_f32, q)
                dve.wait_ge(piece_loaded[r], 32 * (q // 2 + 1))
                step(dve.tensor_scalar(mags[:], w, 0xFF, None, ALU.bitwise_and))
                step(dve.scalar_tensor_tensor(out=spread[:], in0=mags[:], scalar=12, in1=mags[:],
                                              op0=ALU.logical_shift_left, op1=ALU.bitwise_or))
                dve.tensor_scalar(mags[:], spread[:], 0x00070007, 9, ALU.bitwise_and, ALU.logical_shift_left)
                step(dve.tensor_scalar(signs[:], spread[:], 0x00080008, 12, ALU.bitwise_and, ALU.logical_shift_left))
                step(dve.tensor_tensor(mags[:], mags[:], signs[:], ALU.bitwise_or))
                if q >= 2:
                    dve.wait_ge(piece_lo, q - 1)
                codes = mags[:].bitcast(F16).rearrange("p (n two) -> p two n", two=2)
                for e in range(2):
                    last = dve.scalar_tensor_tensor(out=wf[:, r, e, :], in0=codes[:, e, :], scalar=2.0 ** 14,
                                                    in1=scl[:, r, :], op0=ALU.mult, op1=ALU.mult)
                last.then_inc(piece_f32, 1)

            drive(dve, dict(ln1=ln1, xt=xt, dt=dt, cs=cs, ip=ip, m=m, xtr=xtr, y=y, yt=yt_, out=out_, x1t=x1t_,
                            ffn=ffn, fin=fin, dq=dq), setup_dve)

        @block.tensor
        def _(pe):
            def bank_read(uses, use, i):
                u, before = earlier_use(uses, uses.index(use))
                if before and isinstance(i, int) and i == 0:
                    return
                name, k = uses[u]
                pe.wait_ge(s[read_by[name]], count(read_by[name], i - 1 if before else i, k))

            def split_matmul(ps, lhs, rhs, nk, start=True, stop=True, check=False):
                todo = [(a, b, k) for k in range(nk) for a, b in PASSES]
                for n, (a, b, k) in enumerate(todo):
                    last = pe.matmul(ps, lhs(a, k), rhs(b, k), start=start and n == 0,
                                     stop=stop and n == len(todo) - 1, skip_group_check=check)
                return last

            def setup_pe():
                pe.wait_ge(consts_ready, 1)

            def xt(i, par, j):
                ps = m_bank["xt", j]
                pe.wait_ge(s["xn"], count("xn", i, j))
                bank_read(m_uses, ("xt", j), i)
                for c in range(2):
                    for k in range(KD):
                        last = pe.transpose(ps[:, SUB * k + CH * c:SUB * k + CH * c + CH], xn[:, c, P * k:P * k + P],
                                            ident[:])
                last.then_inc(s["xt"], 1)

            def dt(i, par, j):
                ps = m_bank["dt", j]
                if isinstance(i, int) and i == 0 and j == 0:
                    pe.wait_ge(wi_ready, 1)
                pe.wait_ge(s["xnt"], count("xnt", i, j))
                bank_read(m_uses, ("dt", j), i)
                for c in range(2):
                    last = split_matmul(ps[:, HEADS * c:HEADS * c + HEADS],
                                        lambda a, k: xnt[:, a, k, CH * c:CH * c + CH],
                                        lambda b, k: wi[:, b, k, ZX - HEADS:ZX], KD)
                last.then_inc(s["dt"], 1)

            def ip(i, par, q):
                ps = m_bank["ip", q]
                bank_read(m_uses, ("ip", q), i)
                for e in range(2):
                    c0 = DI + P * (2 * (q % 3) + e)
                    last = split_matmul(ps[:, SUB * e:SUB * e + SUB], lambda a, k: wi[:, a, k, c0:c0 + P],
                                        lambda b, k: xnt[:, b, k, :], KD)
                last.then_inc(s["ip"], 1)

            def cs(i, par, j):
                ps = m_bank["cs", j]
                pe.wait_ge(s["da"], count("da", i, j))
                bank_read(m_uses, ("cs", j), i)
                for n, tri in enumerate((upto, after, ones)):
                    pe.matmul(ps[:, 16 * n:16 * n + 16], tri[:], da[:, 0, 0:16], start=True, stop=True)
                pe.matmul(ps[0:96, 128:256], da[:].rearrange("p r n -> p (r n)"), upto[:], start=True,
                          stop=True).then_inc(s["cs"], 1)

            def seg(i, par, k):
                c, h0 = k // 2 % 2, 4 * (k % 2)
                ps = m_bank["seg", k][:].rearrange("p (h l) -> p h l", h=4)
                pe.wait_ge(s["t3"], count("t3", i, k // 4))
                bank_read(m_uses, ("seg", k), i)
                pe.matmul(ps, ident_b[:], masked_b[:].unsqueeze(1).broadcast_to([P, 4, CH]), start=True, stop=False,
                          skip_group_check=True)
                r0 = HEADS * c + h0
                pe.matmul(ps, t3[:], unpick[:, r0:r0 + 4].unsqueeze(2).broadcast_to([96, 4, CH]), start=False, stop=False,
                          skip_group_check=True)
                for h in range(4):
                    last = pe.matmul(ps[:, h, :], pick[:, r0 + h:r0 + h + 1].broadcast_to([96, CH]), t3[:],
                                     start=False, stop=(h == 3), skip_group_check=True)
                last.then_inc(s["seg"], 1)

            def z(i, par, q):
                bank_read(m_uses, ("z", q), i)
                c = q % 2
                split_matmul(m_bank["z", q][:], lambda a, k: xnt[:, a, k, CH * c:CH * c + CH],
                             lambda b, k: wi[:, b, k, 0:DI], KD).then_inc(s["z"], 1)

            def gb_(i, par, j):
                ps = m_bank["gb", j]
                pe.wait_ge(s["xc"], count("xc", i, 3 * j + 2))
                bank_read(m_uses, ("gb", j), i)
                for c in range(2):
                    pe.matmul(ps[:, CH * c:CH * c + CH], xc[:, 4, CH * c:CH * c + CH], xc[:, 5, CH * c:CH * c + CH],
                              start=True, stop=True)
                for c in range(2):
                    last = pe.transpose(ps[:, SUB + CH * c:SUB + CH * c + CH], xc[:, 4, CH * c:CH * c + CH], ident[:])
                last.then_inc(s["gb"], 1)

            def xtr(i, par, q):
                c = q % 2
                bank_read(m_uses, ("xtr", q), i)
                for k in range(KI):
                    last = pe.transpose(m_bank["xtr", q][:, P * k:P * k + P], xc[:, k, CH * c:CH * c + CH], ident[:])
                last.then_inc(s["xtr"], 1)

            def y(i, par, q):
                c = q % 2
                if q or not (isinstance(i, int) and i == 0):
                    pe.wait_ge(s["state"], count("state", i, q - 1))
                bank_read(m_uses, ("yo", q), i)
                pe.matmul(m_bank["yo", q][:], xc[:, 5, CH * c:CH * c + CH], state[:], start=True,
                          stop=True).then_inc(s["yo"], 1)
                pe.wait_ge(s["xdt"], count("xdt", i, q))
                pe.wait_ge(s["m"], count("m", i, q))
                bank_read(m_uses, ("yd", q), i)
                for h in range(HEADS):
                    last = pe.matmul(m_bank["yd", q][:, HD * h:HD * h + HD], lmat[:, c, h, :], xdt[:, HD * h:HD * h + HD],
                                     start=True, stop=True)
                last.then_inc(s["yd"], 1)
                pe.wait_ge(s["xdd"], count("xdd", i, q))
                pe.wait_ge(s["gbs"], count("gbs", i, q // 2))
                bank_read(m_uses, ("st", q), i)
                pe.matmul(m_bank["st", q][:], gb[:, 2 + c, :], xdd[:], start=True, stop=True).then_inc(s["st"], 1)

            def yt_(i, par, q):
                pe.wait_ge(s["y"], count("y", i, q))
                bank_read(m_uses, ("yt", q), i)
                for k in range(KI):
                    last = pe.transpose(m_bank["yt", q][:, CH * k:CH * k + CH], yg[:, P * k:P * k + P], ident[:])
                last.then_inc(s["yt"], 1)

            def out_(i, par, q):
                if isinstance(i, int) and i == 0 and q == 0:
                    pe.wait_ge(wo_ready, 1)
                pe.wait_ge(s["yts"], count("yts", i, q))
                bank_read(m_uses, ("out", q), i)
                split_matmul(m_bank["out", q][:, 0:DM], lambda a, k: yt[:, a, k, :], lambda b, k: wo[:, b, k, :],
                             KI).then_inc(s["out"], 1)

            def x1t_(f, par, j):
                ps = f_bank["x1t", j]
                pe.wait_ge(s["x1n"], count("x1n", f, 2 * j + 1))
                bank_read(f_uses, ("x1t", j), f)
                for c in range(2):
                    for k in range(KD):
                        last = pe.transpose(ps[:, SUB * k + CH * c:SUB * k + CH * c + CH], x1n[:, j, c, k, :], ident[:])
                last.then_inc(s["x1t"], 1)

            def down(f, n):
                pe.wait_ge(s["lo"], count("lo", f, n))
                if n == 0 and not (isinstance(f, int) and f == 0):
                    pe.wait_ge(s["d_read"], count("d_read", f - 1, 0))
                for t in range(TT):
                    last = split_matmul(db[t // 2][:, t % 2 * DM:t % 2 * DM + DM],
                                        lambda a, k: hl[:, n % 2, a, CH * t:CH * t + CH],
                                        lambda b, k: wd[:, b, n, :], 1, start=(n == 0 and t % 2 == 0),
                                        stop=(n == NT - 1), check=True)
                last.then_inc(s["down"], 1)

            def ffn(f, par, n):
                if n == 0:
                    pe.wait_ge(s["x1ts"], count("x1ts", f, 1))
                    if isinstance(f, int) and f == 0:
                        pe.wait_ge(piece_lo, MATS * PIECES)
                for name, w in (("gate", wg), ("up", wu)):
                    bank_read(f_uses, (name, n), f)
                    split_matmul(f_bank[name, n][:], lambda a, k: w[:, a, k, P * n:P * n + P],
                                 lambda b, k: x1t[:, b, k, :], KD).then_inc(s[name], 1)
                if n:
                    down(f, n - 1)
                if n == NT - 1:
                    down(f, n)

            drive(pe, dict(xt=xt, dt=dt, ip=ip, cs=cs, seg=seg, z=z, gb=gb_, xtr=xtr, y=y, yt=yt_, out=out_,
                           x1t=x1t_, ffn=ffn), setup_pe)


def kernel(**inputs):
    import numpy as _np
    import concourse.bacc as _bacc
    from concourse import mybir as _mybir
    from concourse.bass_utils import run_bass_kernel_spmd as _run

    x = {k.replace("L0_attn_", "").replace("L0_ffn_", ""): _np.asarray(v) for k, v in inputs.items()}

    def columns(a):
        return a.reshape(8, 128, 2, -1).transpose(3, 0, 2, 1).reshape(a.shape[1], -1)

    def down_words(a):
        return a.T.reshape(8, 128, 256).transpose(1, 0, 2).reshape(128, -1)

    def down_scales(a):
        return a.T.reshape(8, 8, 256).transpose(1, 0, 2).reshape(8, -1)

    arrays = {
        "u": x["u"],
        "in_proj": x["in_proj_kernel"],
        "conv_w": x["conv1d_weight"].reshape(6, 128, 4).transpose(1, 0, 2),
        "conv_b": x["conv1d_bias"].reshape(6, 128).T,
        "dt_bias": x["dt_bias"],
        "a_log": x["A_log"],
        "d_skip": x["D"],
        "norm_w": x["norm_weight"].reshape(4, 128).T,
        "out_proj": x["out_proj_kernel"],
        "packed": _np.stack([columns(x["gate_W_packed"]), columns(x["up_W_packed"]), down_words(x["down_W_packed"])]),
        "scales": _np.stack([columns(x["gate_scales"]), columns(x["up_scales"]), down_scales(x["down_scales"])]),
    }
    arrays = {f"in_{k}": _np.ascontiguousarray(v) for k, v in arrays.items()}
    nc = _bacc.Bacc("TRN2", target_bir_lowering=False, num_devices=1)
    args = [nc.dram_tensor(k, v.shape, _mybir.dt.from_np(v.dtype), kind="ExternalInput").ap() for k, v in arrays.items()]
    args.append(nc.dram_tensor("out_0", (BATCH, SEQ, DM), F32, kind="ExternalOutput").ap())
    build(nc, *args)
    r = _run(nc, [arrays], core_ids=[0])
    return r.results[0]["out_0"]
```

```python
from contextlib import ExitStack

import numpy as np

import concourse.bass as bass
from concourse import mybir

ALU = mybir.AluOpType
ACT = mybir.ActivationFunctionType
F32 = mybir.dt.float32
F32R = mybir.dt.float32r
F16 = mybir.dt.float16
BF16 = mybir.dt.bfloat16
I32 = mybir.dt.int32

P = 128
BATCH, SEQ, DM = 4, 1024, 256
HEADS, HD, DI, NSTATE, TAPS = 8, 64, 512, 128, 4
CONV = DI + 2 * NSTATE
ZX = 2 * DI + 2 * NSTATE + HEADS
MLP, SBLK = 2048, 32
EPS = 1e-5
BLK = 512
NBLK = BATCH * SEQ // BLK
SUB = 256
CH = 128
KD = DM // P
KI = DI // P
CT = CONV // P
NT = MLP // P
TT = BLK // P
TINY = 1e-30
PIECE = 512
PIECES = MLP // PIECE
MATS = 3

PASSES = ((0, 0), (0, 1), (1, 0))


MAMBA_BANKS = dict(xt=("xt",), dt=("dt",), cs=("cs",), ct=("ct",), seg=("seg",), ip=("ip",), z=("z",), gb=("gb",),
                   xtr=("xtr",), yo=("yo",), yd=("yd",), st=("st",), yt=("yt",), out=("out",))
FFN_BANKS = dict(x1t=("x1t",), gu=("gate", "up"))


ORDER = {
    "pe": """
        xtr:0 yo:0 gu:1< xt:1 gu:2< dn:0< yd:0 st:0 dn:1< yt:0 xtr:1 yo:1 dn:2< out:0 yd:1 gu:3< st:1 yt:1
        gu:4< out:1 dn:3< gu:5< dn:4< dt:1 gu:6< dn:5< ip:3 cs:1 ip:4 gu:7< dn:6< ct:1 seg:4 ip:5 gu:8<
        seg:5 seg:6 seg:7 gu:9< dn:7< z:2 z:3 gb:1 xtr:2 yo:2 xt:0> gu:10< dn:8< yd:2 st:2 dn:9< yt:2 xtr:3
        yo:3 dn:10< out:2 yd:3 gu:11< st:3 yt:3 gu:12< out:3 dn:11< gu:13< dn:12< dt:0> gu:14< dn:13< ip:0>
        cs:0> ip:1> gu:15< dn:14< ct:0> seg:0> ip:2> x1t:0 seg:1> seg:2> seg:3> z:0> x1t:1 z:1> dn:15< gb:0>
        gu:0""",
    "act": """
        gelu:0< split:0< gelu:1< xn_split:1 split:1< gelu:2< split:2< square:0 yt_split:0 square:1 gelu:3<
        yt_split:1 split:3< gelu:4< split:4< gelu:5< split:5< dt_bias:1 gelu:6< taps:3 split:6< decays:1
        taps:4 gelu:7< silu:3 taps:5 decay_matrix:4 split:7< gelu:8< decay_matrix:5 decay_matrix:6
        decay_matrix:7 silu:4 silu:5 gate:2 gate:3 split:8< gb_copy:1 gelu:9< xn_split:0> split:9< gelu:10<
        split:10< square:2 yt_split:2 square:3 gelu:11< yt_split:3 split:11< gelu:12< split:12< gelu:13<
        split:13< dt_bias:0> gelu:14< taps:0> split:14< decays:0> taps:1> gelu:15< silu:0> taps:2>
        decay_matrix:0> decay_matrix:1> split:15< x1_split:0 decay_matrix:2> x1_split:1 silu:1> silu:2>
        gate:0> gate:1> decay_matrix:3> gb_copy:0>""",
    "dve": """
        inter:0< xdt:0 yoff:0 inter:1< decayed_products:1 xn_split:1 inter:2< ydiag:0 state:0 xdt:1
        yt_split:0 yoff:1 stats2:0 ydiag:1 ln2:0 state:1 inter:3< yt_split:1 x1n:0 inter:4< stats2:1 ln2:1
        inter:5< dt_bias:1 stats1:0> x1n:1 softplus:1 xn:0> inter:6< conv:3 decays:1 conv:4 sums:1
        decay_sums:4 inter:7< conv:5 decay_sums:5 decay_sums:6 decay_sums:7 inter:8< gb_copy:1
        decayed_products:2 xdt:2 yoff:2 inter:9< decayed_products:3 xn_split:0> inter:10< ydiag:2 state:2
        xdt:3 yt_split:2 yoff:3 stats2:2 ydiag:3 ln2:2 state:3 inter:11< yt_split:3 inter:12< stats2:3 ln2:3
        inter:13< dt_bias:0> stats1:1> softplus:0> xn:1> inter:14< conv:0> decays:0> conv:1> sums:0>
        decay_sums:0> decay_sums:1> inter:15< x1n:2 x1n:3 decay_sums:2> conv:2> x1_split:0 decay_sums:3>
        x1_split:1 fin:0< gb_copy:0> decayed_products:0> ln4:0<""",
    "pool": """
        split:0< xdt:0 yoff:0 split:1< split:2< xdt:1 yoff:1 stats2:0 ln2:0 split:3< split:4< stats2:1 ln2:1
        split:5< stats1:0> split:6< split:7< split:8< xdt:2 yoff:2 split:9< split:10< xdt:3 yoff:3 stats2:2
        ln2:2 split:11< split:12< stats2:3 ln2:3 split:13< stats1:1> split:14< split:15< fin:0<""",
}

FIRST = {
    "pe": """
        xt:0 dt:0 ip:0 cs:0 ip:1 ct:0 seg:0 ip:2 seg:1 seg:2 seg:3 z:0 z:1 gb:0 xtr:0 yo:0 xt:1 yd:0 st:0
        yt:0 xtr:1 yo:1 out:0 yd:1 st:1 yt:1 out:1 dt:1 ip:3 cs:1 ip:4 ct:1 seg:4 ip:5 seg:5 seg:6 seg:7 z:2
        z:3 gb:1 xtr:2 yo:2 xt:0> yd:2 st:2 yt:2 xtr:3 yo:3 out:2 yd:3 st:3 yt:3 out:3 dt:0> ip:0> cs:0>
        ip:1> ct:0> seg:0> ip:2> dl:11 x1t:0 seg:1> seg:2> seg:3> z:0> x1t:1 z:1> gb:0> gu:0""",
    "act": """
        wi_split:0 dq:0 dq:1 dl:0 dq:2 xn_split:0 rates:0 dl:1 dq:3 taps:0 dt_bias:0 dl:2 dq:4 wo_split:0
        dl:3 silu:0 decays:0 taps:1 dq:5 dl:4 dq:6 taps:2 silu:1 decay_matrix:0 decay_matrix:1
        decay_matrix:2 gate:0 decay_matrix:3 silu:2 gate:1 dl:5 dl:6 gb_copy:0 dq:7 dq:8 xn_split:1 square:0
        yt_split:0 dl:7 dl:8 dq:9 dq:10 square:1 yt_split:1 dl:9 dq:11 dl:10 taps:3 dt_bias:1 silu:3 dl:11
        decays:1 taps:4 taps:5 silu:4 decay_matrix:4 decay_matrix:5 decay_matrix:6 gate:2 decay_matrix:7
        silu:5 gate:3 gb_copy:1 xn_split:0> square:2 yt_split:2 square:3 yt_split:3 dt_bias:0> taps:0>
        decays:0> taps:1> silu:0> taps:2> x1_split:0 decay_matrix:0> decay_matrix:1> silu:1> decay_matrix:2>
        x1_split:1 silu:2> decay_matrix:3> gate:0> gate:1> gb_copy:0>""",
    "dve": """
        stats1:0 dq:0 wi_split:0 dq:1 xn:0 dq:2 rates:0 xn_split:0 dq:3 dt_bias:0 wo_split:0 stats1:1 conv:0
        softplus:0 dq:4 dq:5 decays:0 conv:1 sums:0 decay_sums:0 decay_sums:1 decay_sums:2 conv:2
        decay_sums:3 dq:6 dq:7 gb_copy:0 decayed_products:0 xdt:0 yoff:0 decayed_products:1 dq:8 xn:1
        xn_split:1 ydiag:0 state:0 dq:9 yt_split:0 xdt:1 yoff:1 stats2:0 dq:10 ln2:0 state:1 ydiag:1
        yt_split:1 dq:11 stats2:1 dt_bias:1 ln2:1 conv:3 softplus:1 stats1:0> xn:0> decays:1 conv:4 sums:1
        decay_sums:4 decay_sums:5 decay_sums:6 conv:5 decay_sums:7 x1n:0 x1n:1 gb_copy:1 decayed_products:2
        xdt:2 yoff:2 decayed_products:3 xn_split:0> state:2 ydiag:2 xdt:3 yt_split:2 yoff:3 stats2:2 ydiag:3
        ln2:2 state:3 yt_split:3 stats2:3 dt_bias:0> ln2:3 softplus:0> conv:0> decays:0> conv:1> sums:0>
        decay_sums:0> decay_sums:1> x1n:2 x1n:3 decay_sums:2> conv:2> x1_split:0 decay_sums:3> x1_split:1
        stats1:1> gb_copy:0> decayed_products:0> xn:1>""",
    "pool": """
        stats1:0 wi_split:0 dq:0 dq:1 dl:0 dl:1 dq:2 dq:3 dl:2 dl:3 dq:4 wo_split:0 dl:4 dq:5 stats1:1 dq:6
        dl:5 dl:6 xdt:0 yoff:0 dq:7 dq:8 dl:7 dl:8 stats2:0 xdt:1 yoff:1 ln2:0 dq:9 dq:10 dl:9 stats2:1
        dl:10 ln2:1 dq:11 stats1:0> dl:11 xdt:2 yoff:2 xdt:3 yoff:3 stats2:2 ln2:2 stats2:3 ln2:3 stats1:1>""",
}


def parse(orders):
    whose = {"<": "before", ">": "next"}
    steps = {}
    for engine, text in orders.items():
        steps[engine] = []
        for token in text.split():
            name, k = token.rstrip("<>").split(":")
            steps[engine].append((name, int(k), whose.get(token[-1], "this")))
    return steps


ORDER, FIRST = parse(ORDER), parse(FIRST)


def iteration_steps(engine, mamba=True, ffn_too=True, ahead=True):
    return [s for s in ORDER[engine] if (mamba or s[2] == "before") and (ffn_too or s[2] != "before")
            and (ahead or s[2] != "next")]


def bank_uses(banks):
    return [(use, k, whose) for name, k, whose in iteration_steps("pe") for use in banks.get(name, ())]


def build(nc, u, in_proj, conv_w, conv_b, dt_bias, a_log, d_skip, norm_w, out_proj,
          packed, scales, out):
    ctx = ExitStack()
    with ctx:
        def sb(name, shape, dt=F32, stack=ctx):
            return stack.enter_context(nc.sbuf_tensor(name, shape, dt))

        def sem(name):
            return ctx.enter_context(nc.semaphore(name))

        wi = sb("wi", [P, 2, KD, ZX], F32R)
        wo = sb("wo", [P, 2, KI, DM], F32R)
        wg = sb("wg", [P, 2, KD, MLP], F32R)
        wu = sb("wu", [P, 2, KD, MLP], F32R)
        wd = sb("wd", [P, 2, NT, DM], F32R)
        ident = sb("ident", [P, P])
        upto = sb("upto", [P, P])
        after = sb("after", [P, P])
        ones = sb("ones", [P, 1])
        pick = sb("pick", [96, 16], BF16)
        neg_half = sb("neg_half", [P, TT])
        cw = sb("cw", [P, CT, TAPS])
        cb = sb("cb", [P, CT])
        dtb = sb("dtb", [P, HEADS])
        a_neg = sb("a_neg", [P, HEADS])
        dsk = sb("dsk", [P, HEADS])
        nw = sb("nw", [P, KI])
        with ExitStack() as early:
            wo_raw = sb("wo_raw", [P, KI, DM], F32, early)
        xb = sb("xb", [P, 2, TT, DM])
        xin = sb("xin", [P, 2, 2, DM])
        xn = sb("xn", [P, 2, DM])
        xnt = sb("xnt", [P, 2, KD, SUB], F32R)
        raw = sb("raw", [P, 2, 2, SUB + TAPS - 1])
        hist = sb("hist", [P, CT, TAPS - 1])
        xc = sb("xc", [P, CT, SUB])
        sz = sb("sz", [P, 2, DI])
        xdt = sb("xdt", [P, DI])
        t1 = sb("t1", [P, DI])
        yg = sb("yg", [P, DI])
        state = sb("state", [P, DI])
        yt = sb("yt", [P, 2, KI, CH], F32R)
        da = sb("da", [P, 3, 32])
        t3 = sb("t3", [96, CH], BF16)
        rest3 = sb("rest3", [96, CH])
        ct_ = sb("ct_", [P, 2 * HEADS])
        ex = sb("ex", [P, 2, 3, 2, HEADS])
        pause = sb("pause", [P, 1])
        st1 = sb("st1", [P, 2, 6])
        mv1 = sb("mv1", [P, 2, 2])
        ve1 = sb("ve1", [P, 2])
        rs1 = sb("rs1", [P, 2])
        st2 = sb("st2", [P, 6])
        mv2 = sb("mv2", [P, 2])
        e2 = sb("e2", [P, 1])
        ve2 = sb("ve2", [P, 1])
        rs2 = sb("rs2", [P, 1])
        mr2 = sb("mr2", [P, 1])
        st3 = sb("st3", [P, 6])
        mv3 = sb("mv3", [P, TT, 2])
        ve3 = sb("ve3", [P, 1])
        rs3 = sb("rs3", [P, TT])
        ssq = sb("ssq", [P, 4])
        spa = sb("spa", [P, 2 * HEADS])
        spn = sb("spn", [P, 2 * HEADS])
        spe = sb("spe", [P, 2 * HEADS])
        spl = sb("spl", [P, 2 * HEADS])
        spw = sb("spw", [P, 2 * HEADS])
        spr = sb("spr", [P, 2 * HEADS])
        dt_ = sb("dt_", [P, 2, 2 * HEADS])
        st4 = sb("st4", [P, TT, 6])
        mv4 = sb("mv4", [P, TT, 2])
        ve4 = sb("ve4", [P, TT])
        rs4 = sb("rs4", [P, TT])
        mr4 = sb("mr4", [P, TT])
        with ExitStack() as early:
            wi_raw = sb("wi_raw", [P, KD, ZX], F32, early)
        lmat = sb("lmat", [P, 2, HEADS, CH])
        gb = sb("gb", [P, 4, CH])
        xdd = sb("xdd", [P, DI])
        with ExitStack() as early:
            words = sb("words", [P, 2, PIECE], I32, early)
            scl = sb("scl", [P, 2, PIECE], F32, early)
            spread = sb("spread", [P, PIECE], I32, early)
            mags = sb("mags", [P, PIECE], I32, early)
            signs = sb("signs", [P, PIECE], I32, early)
            wf = sb("wf", [P, 2, 2, PIECE], F32, early)
        x1n = sb("x1n", [P, 2, 2, CH])
        x1t = sb("x1t", [P, 2, KD, BLK], F32R)
        hid = sb("hid", [P, 2, BLK])
        hl = sb("hl", [P, 2, 2, BLK], F32R)

        mb = [ctx.enter_context(nc.psum_tensor(f"mb{b}", [P, 512], F32)) for b in range(3)]
        fb = [ctx.enter_context(nc.psum_tensor(f"fb{b}", [P, 512], F32)) for b in range(3)]
        db = [ctx.enter_context(nc.psum_tensor(f"db{b}", [P, 512], F32)) for b in range(2)]

        x_loaded = [sem(f"x_loaded{j}") for j in range(2)]
        out_stored = sem("out_stored")
        small_loaded = sem("small_loaded")
        wi_loaded = [sem(f"wi_loaded{k}") for k in range(KD)]
        wo_loaded = sem("wo_loaded")
        piece_loaded = [sem(f"piece_loaded{r}") for r in range(2)]
        consts_ready = sem("consts_ready")
        setup = sem("setup")
        ident_ready = sem("ident_ready")
        a_exp = sem("a_exp")
        a_ready = sem("a_ready")
        wi_hi = sem("wi_hi")
        wi_ready = sem("wi_ready")
        wo_scaled = sem("wo_scaled")
        wo_hi = sem("wo_hi")
        wo_ready = sem("wo_ready")
        dve_dq = sem("dve_dq")
        codes_ready = sem("codes_ready")
        scale_ready = sem("scale_ready")
        piece_f32 = sem("piece_f32")
        piece_hi = sem("piece_hi")
        piece_lo = sem("piece_lo")

        per_block = dict(
            var1=2, rstd1=2, xn=2, xt=2, xnt_hi=2, xnt=2, dt=2, dt_read=2, spn=2, spe=2, softln=2, da=2,
            cs=2, ex=2, cs_read=2, t3=2, ct=2, ct_read=2, seg=8, upto_s=8, lmat=8, ip=6, raw=6, tap=6, hin=6, conv=6, xc=6, hist=6,
            z=4, sz=4, gb=2, gm=2, gbs=2, m=4, xtr=4, xdt=4, skip=4, xdd=4, yo=4, t1=4, yd=4, st=4,
            decayed=4, yskip=4, ydiag=4, state=4, y=4, yt=4, ssq=4, yt_hi=4, yts=4, out=4,
            var2=4, rstd2=4, attn=4, x1=4, var3=4, rstd3=4, x1n=4,
            x1t=2, x1t_hi=2, x1ts=2, gate=NT, up=NT, gelu=NT, inter=NT, hi=NT, lo=NT, down=NT,
            var4=1, rstd4=1, d_read=1, outs=2,
            ln1_link=4, dt_link=12, cs_link=6, conv_link=30, out_link=24, fin_link=3)
        s = {name: sem("s_" + name) for name in per_block}
        from_before = ("lo", "down", "gelu", "inter", "x1ts", "d_read", "x1t")

        def count(name, i, k):
            return (i + (name in from_before)) * per_block[name] + (k + 1)

        m_uses, f_uses = bank_uses(MAMBA_BANKS), bank_uses(FFN_BANKS)
        read_by = dict(xt="xnt", dt="dt_read", ip="tap", cs="cs_read", ct="ct_read", seg="upto_s", z="sz", gb="gbs",
                       xtr="skip", yo="t1", yd="ydiag", st="state", yt="yts", out="attn",
                       x1t="x1ts", gate="gelu", up="inter")
        m_bank = {use[:2]: mb[n % 3] for n, use in enumerate(m_uses)}
        f_bank = {use[:2]: fb[n % 3] for n, use in enumerate(f_uses)}

        def drive(eng, engine, do, prologue):
            def run(steps, i, par):
                for name, k, whose in steps:
                    away = dict(before=-1, this=0, next=1)[whose]
                    do[name](i + away, par if away == 0 else 1 - par, k)

            prologue()
            run(FIRST[engine], 0, 0)
            with eng.Fori(0, (NBLK - 2) // 2) as pair:
                for half in range(2):
                    run(iteration_steps(engine), pair * 2 + (1 + half), 1 - half)
            run(iteration_steps(engine, ahead=False), NBLK - 1, 1)
            run(iteration_steps(engine, mamba=False), NBLK, 0)

        u_v = u.rearrange("b (i j c p) d -> (b i) j p c d", j=2, c=2, p=P)
        o_v = out.rearrange("b (i j c p) d -> (b i) j p c d", j=2, c=2, p=P)

        def per_head(ap):
            return ap.rearrange("p (h q) -> p h q", h=HEADS)

        def spread_heads(ap):
            return ap.unsqueeze(2).broadcast_to([P, HEADS, HD])

        def weight_piece(mat, part, c0):
            if mat < 2:
                return (wg, wu)[mat][:, part, :, c0:c0 + PIECE].rearrange("p e (g n) -> p e g n", n=DM)
            n0 = 2 * (c0 // DM)
            return wd[:, part, n0:n0 + 2 * PIECE // DM, :].rearrange("p (g e) n -> p e g n", e=2)

        def wf_piece(r):
            return wf[:, r, :, :].rearrange("p e (g n) -> p e g n", n=DM)

        block = ctx.enter_context(nc.Block())

        @block.sync
        def _(sp):
            def load_x(i, j):
                src = u_v[bass.ds(i, 1), j].rearrange("o p c d -> (o p) c d")
                sp.dma_start(xin[:, j, :, :], src).then_inc(x_loaded[j], 16)

            load_x(0, 0)
            for k in range(KD):
                sp.dma_start(wi_raw[:, k, :], in_proj[P * k:P * k + P, :]).then_inc(wi_loaded[k], 16)
            for dst, src in ((cw, conv_w), (cb, conv_b), (nw, norm_w)):
                sp.dma_start(dst[:], src).then_inc(small_loaded, 16)
            for dst, src in ((dtb, dt_bias), (a_neg, a_log), (dsk, d_skip)):
                sp.dma_start(dst[:], src.partition_broadcast(P)).then_inc(small_loaded, 16)
            load_x(0, 1)
            for q in range(MATS * PIECES):
                mat, c0, r = q // PIECES, q % PIECES * PIECE, q % 2
                if q == 2:
                    sp.dma_start(wo_raw[:], out_proj.rearrange("(k p) n -> p k n", p=P)).then_inc(wo_loaded, 16)
                if q >= 2:
                    sp.wait_ge(piece_f32, q - 1)
                sp.dma_start(words[:, r, :], packed[mat, :, c0:c0 + PIECE]).then_inc(piece_loaded[r], 16)
                sp.dma_start(scl[:, r, :], scales[mat, :, c0:c0 + PIECE].unsqueeze(1)
                             .broadcast_to([8, SBLK // 2, PIECE])).then_inc(piece_loaded[r], 16)

            def next_x(i):
                for j in range(2):
                    sp.wait_ge(s["attn"], count("attn", i, 2 * j + 1))
                    load_x(i + 1, j)

            def store(f, par):
                for j in range(2):
                    sp.wait_ge(s["outs"], count("outs", f, j))
                    dst = o_v[bass.ds(f, 1), j].rearrange("o p c d -> (o p) c d")
                    sp.dma_start(dst, xb[:, par, 2 * j:2 * j + 2, :]).then_inc(out_stored, 16)

            next_x(0)
            with sp.Fori(0, (NBLK - 2) // 2) as pair:
                for half in range(2):
                    next_x(pair * 2 + (1 + half))
                    store(pair * 2 + half, half)
            store(NBLK - 2, 0)
            store(NBLK - 1, 1)
            sp.wait_ge(out_stored, NBLK * 32 + 32)

        @block.gpsimd
        def _(pool):
            def consts():
                n = [0]

                def link(ins):
                    n[0] += 1
                    ins.then_inc(setup, 1)
                    pool.wait_ge(setup, n[0])

                link(pool.memset(ident[:], 0.0))
                pool.affine_select(out=ident[:], in_=ident[:], compare_op=ALU.not_equal, fill=1.0, base=0,
                                   pattern=[[-1, P]], channel_multiplier=1).then_inc(ident_ready, 1)
                pool.memset(neg_half[:, 0:2], -0.5).then_inc(s["lo"], NT)
                pool.memset(neg_half[:, 2:TT], -0.5).then_inc(out_stored, 32)
                pool.memset(ones[:], 1.0).then_inc(s["down"], NT)
                pool.memset(state[:], 0.0).then_inc(s["inter"], NT)
                pool.memset(hist[:], 0.0).then_inc(s["x1ts"], 2)
                pool.memset(upto[:], 1.0).then_inc(s["d_read"], 1)
                pool.memset(after[:], 0.0).then_inc(s["x1t"], 2)
                pool.memset(da[:], 0.0).then_inc(s["gelu"], NT)
                link(pool.memset(pick[:], 0.0))
                pool.affine_select(out=upto[:], in_=upto[:], compare_op=ALU.is_ge, fill=0.0, base=0,
                                   pattern=[[1, P]], channel_multiplier=-1)
                pool.affine_select(out=after[:], in_=after[:], compare_op=ALU.is_ge, fill=1.0, base=0,
                                   pattern=[[1, P]], channel_multiplier=-1)
                for part in range(3):
                    last = pool.affine_select(out=pick[:], in_=pick[:], compare_op=ALU.not_equal, fill=1.0,
                                              base=-32 * part, pattern=[[-1, 16]], channel_multiplier=1)
                    if part < 2:
                        link(last)
                last.then_inc(consts_ready, 1)

            def wi_split(i, par, _):
                pool.wait_ge(wi_hi, 2)
                pool.tensor_tensor(wi[:, 1, 1, :], wi_raw[:, 1, :], wi[:, 0, 1, :].bitcast(F32),
                                   ALU.subtract).then_inc(wi_ready, 1)

            def wo_split(i, par, _):
                pool.wait_ge(wo_hi, 1)
                pool.tensor_tensor(wo[:, 1, :, :], wo_raw[:], wo[:, 0, :, :].bitcast(F32),
                                   ALU.subtract).then_inc(wo_ready, 1)

            def rstd(name, dst, src, i, k):
                pool.wait_ge(s["var" + name], count("var" + name, i, k))
                pool.tensor_tensor(dst, src, neg_half[:, 0:src.shape[1]], ALU.pow).then_inc(s["rstd" + name], 1)

            def stats1(i, par, j):
                rstd("1", rs1[:], ve1[:], i, j)

            def xdt_(i, par, q):
                pool.wait_ge(s["ex"], count("ex", i, q // 2))
                pool.wait_ge(s["xdt"], count("xdt", i, q))
                pool.tensor_tensor(per_head(xdd[:]), per_head(xdt[:]), spread_heads(ex[:, q // 2, 1, q % 2, :]),
                                   ALU.mult).then_inc(s["xdd"], 1)

            def yoff(i, par, q):
                pool.wait_ge(s["yo"], count("yo", i, q))
                pool.tensor_tensor(per_head(state[:]), per_head(state[:]), spread_heads(ex[:, q // 2, 2, q % 2, :]),
                                   ALU.mult).then_inc(s["decayed"], 1)
                pool.wait_ge(s["t1"], count("t1", i, q))
                pool.tensor_tensor(yg[:], yg[:], t1[:], ALU.add).then_inc(s["yskip"], 1)

            def stats2(i, par, q):
                rstd("2", rs2[:], ve2[:], i, q)

            def ln2(i, par, q):
                rstd("3", rs3[:, q:q + 1], ve3[:], i, q)

            def split(f, par, n):
                pool.wait_ge(s["hi"], count("hi", f, n))
                pool.tensor_tensor(hl[:, n % 2, 1, :], hid[:, n % 2, :], hl[:, n % 2, 0, :].bitcast(F32),
                                   ALU.subtract).then_inc(s["lo"], 1)

            def fin(f, par, _):
                rstd("4", rs4[:], ve4[:], f, 0)

            def dq(i, par, q):
                r = q % 2
                pool.wait_ge(codes_ready, q + 1)
                pool.wait_ge(scale_ready, q + 1)
                if q >= 2:
                    pool.wait_ge(piece_lo, q - 1)
                codes = words[:, r, :].bitcast(F16).rearrange("p (n two) -> p two n", two=2)
                for e in range(2):
                    last = pool.tensor_tensor(wf[:, r, e, :], codes[:, e, :], scl[:, r, :], ALU.mult)
                last.then_inc(piece_f32, 1)

            def dl(i, par, q):
                mat, c0, r = q // PIECES, q % PIECES * PIECE, q % 2
                pool.wait_ge(piece_hi, q + 1)
                pool.tensor_tensor(weight_piece(mat, 1, c0), wf_piece(r),
                                   weight_piece(mat, 0, c0).bitcast(F32), ALU.subtract).then_inc(piece_lo, 1)

            drive(pool, "pool", dict(wi_split=wi_split, wo_split=wo_split, stats1=stats1, stats2=stats2, xdt=xdt_, yoff=yoff, ln2=ln2, split=split, fin=fin, dq=dq, dl=dl), consts)

        @block.scalar
        def _(act):
            def wi_split(i, par, _):
                for k in range(KD):
                    act.wait_ge(wi_loaded[k], 16)
                    act.activation(wi[:, 0, k, :], wi_raw[:, k, :], ACT.Copy).then_inc(wi_hi, 1)

            def rates(i, par, _):
                act.preload_act_table_set("natural_log_exp_and_others")
                act.wait_ge(small_loaded, 96)
                act.activation(a_neg[:], a_neg[:], ACT.Exp).then_inc(a_exp, 1)

            def wo_split(i, par, _):
                act.wait_ge(wo_scaled, 1)
                act.activation(wo[:, 0, :, :], wo_raw[:], ACT.Copy).then_inc(wo_hi, 1)

            def xn_split(i, par, j):
                act.wait_ge(s["xt"], count("xt", i, j))
                act.activation(xnt[:, 0, :, :], m_bank["xt", j][:], ACT.Copy).then_inc(s["xnt_hi"], 1)

            def dt_bias(i, par, j):
                act.preload_act_table_set("natural_log_exp_and_others")
                act.wait_ge(s["spn"], count("spn", i, j))
                act.activation(spe[:], spn[:], ACT.Exp).then_inc(s["spe"], 1)
                act.wait_ge(s["spe"], count("spe", i, j))
                act.activation(spl[:], spe[:], ACT.Ln, bias=1.0).then_inc(s["softln"], 1)

            def decays(i, par, j):
                act.wait_ge(s["cs"], count("cs", i, j))
                act.activation(ex[:, j].rearrange("p a c h -> p (a c h)"), m_bank["cs", j][:, 0:48],
                               ACT.Exp).then_inc(s["ex"], 1)

            def decay_matrix(i, par, k):
                c, h = k // 2 % 2, k % 2
                act.wait_ge(s["upto_s"], count("upto_s", i, k))
                part = lmat[:, c, 4 * h:4 * h + 4, :].rearrange("p h l -> p (h l)")
                act.activation(part, part, ACT.Exp).then_inc(s["lmat"], 1)

            def taps(i, par, k):
                j, pr = k // 3, k % 3
                act.wait_ge(s["ip"], count("ip", i, k))
                if k >= 2 or not (isinstance(i, int) and i == 0):
                    act.wait_ge(s["hist"], count("hist", i, k - 2))
                ps = m_bank["ip", k][:].rearrange("p (two t) -> p two t", two=2)
                act.activation(raw[:, k % 2, :, TAPS - 1:], ps, ACT.Copy).then_inc(s["raw"], 1)
                for e in range(2):
                    ct = 2 * pr + e
                    last = act.activation(xc[:, ct, :], ps[:, e, :], ACT.Identity, bias=cb[:, ct:ct + 1],
                                          scale=cw[:, ct, TAPS - 1:TAPS])
                last.then_inc(s["tap"], 1)

            def silu(i, par, k):
                pr = k % 3
                act.wait_ge(s["conv"], count("conv", i, k))
                act.activation(xc[:, 2 * pr:2 * pr + 2, :], xc[:, 2 * pr:2 * pr + 2, :], ACT.Silu).then_inc(s["xc"], 1)

            def gate(i, par, q):
                act.wait_ge(s["z"], count("z", i, q))
                act.activation(sz[:, q % 2, :], m_bank["z", q][:], ACT.Silu).then_inc(s["sz"], 1)

            def gb_copy(i, par, j):
                act.wait_ge(s["gm"], count("gm", i, j))
                act.activation(gb[:, 2:4, :].rearrange("p a l -> p (a l)"), m_bank["gb", j][:, SUB:],
                               ACT.Copy).then_inc(s["gbs"], 1)

            def square(i, par, q):
                act.wait_ge(s["y"], count("y", i, q))
                act.activation(t1[:], yg[:], ACT.Square, accum_out=ssq[:, q:q + 1]).then_inc(s["ssq"], 1)

            def yt_split(i, par, q):
                act.wait_ge(s["yt"], count("yt", i, q))
                act.activation(yt[:, 0, :, :].rearrange("p k t -> p (k t)"), m_bank["yt", q][:],
                               ACT.Copy).then_inc(s["yt_hi"], 1)

            def x1_split(f, par, j):
                act.wait_ge(s["x1t"], count("x1t", f, j))
                act.activation(x1t[:, 0, :, SUB * j:SUB * j + SUB],
                               f_bank["x1t", j][:].rearrange("p (k t) -> p k t", k=KD),
                               ACT.Copy).then_inc(s["x1t_hi"], 1)

            def gelu(f, par, n):
                act.wait_ge(s["gate"], count("gate", f, n))
                act.wait_ge(s["lo"], count("lo", f, n - 2))
                act.activation(hid[:, n % 2, :], f_bank["gate", n][:], ACT.Gelu_apprx_tanh).then_inc(s["gelu"], 1)

            def split(f, par, n):
                act.wait_ge(s["inter"], count("inter", f, n))
                act.wait_ge(s["down"], count("down", f, n - 2))
                act.activation(hl[:, n % 2, 0, :], hid[:, n % 2, :], ACT.Copy).then_inc(s["hi"], 1)

            def dq(i, par, q):
                r = q % 2
                act.wait_ge(piece_loaded[r], 32 * (q // 2 + 1))
                act.activation(scl[:, r, :], scl[:, r, :], ACT.Copy, scale=2.0 ** 14).then_inc(scale_ready, 1)

            def dl(i, par, q):
                mat, c0, r = q // PIECES, q % PIECES * PIECE, q % 2
                act.wait_ge(piece_f32, q + 1)
                act.activation(weight_piece(mat, 0, c0), wf_piece(r), ACT.Copy).then_inc(piece_hi, 1)

            drive(act, "act", dict(xn_split=xn_split, dt_bias=dt_bias, decays=decays, decay_matrix=decay_matrix, taps=taps,
                            silu=silu, gate=gate, gb_copy=gb_copy, square=square, yt_split=yt_split,
                            x1_split=x1_split, gelu=gelu, split=split, dq=dq, dl=dl, wi_split=wi_split,
                            wo_split=wo_split, rates=rates), lambda: None)

        @block.vector
        def _(dve):
            def link(name, i, k, ins):
                ins.then_inc(s[name], 1)
                dve.wait_ge(s[name], count(name, i, k))

            def before_aggr(name, i, k, ins):
                link(name, i, k, ins)
                dve.memset(pause[:], 0.0)

            def wi_split(i, par, _):
                dve.wait_ge(wi_hi, 1)
                dve.tensor_tensor(wi[:, 1, 0, :], wi_raw[:, 0, :], wi[:, 0, 0, :].bitcast(F32),
                                  ALU.subtract).then_inc(wi_ready, 1)

            def rates(i, par, _):
                dve.wait_ge(a_exp, 1)
                dve.tensor_scalar(a_neg[:], a_neg[:], -1.0, None, ALU.mult).then_inc(a_ready, 1)
                dve.wait_ge(a_ready, 1)
                dve.wait_ge(consts_ready, 1)

            def wo_split(i, par, _):
                dve.wait_ge(wo_loaded, 16)
                for k in range(KI):
                    last = dve.tensor_scalar(wo_raw[:, k, :], wo_raw[:, k, :], nw[:, k:k + 1], None, ALU.mult)
                last.then_inc(wo_scaled, 1)

            def stats1(i, par, j):
                dve.wait_ge(x_loaded[j], i * 16 + 16)
                x = xin[:, j, :, :]
                for c in range(2):
                    last = dve.bn_stats(st1[:, c, :], x[:, c, :])
                before_aggr("ln1_link", i, 2 * j, last)
                for c in range(2):
                    last = dve.bn_aggr(mv1[:, c, :], st1[:, c, :])
                link("ln1_link", i, 2 * j + 1, last)
                dve.tensor_scalar(ve1[:], mv1[:, :, 1], EPS, None, ALU.add).then_inc(s["var1"], 1)

            def xn_(i, par, j):
                x = xin[:, j, :, :]
                dve.wait_ge(s["rstd1"], count("rstd1", i, j))
                if j or not (isinstance(i, int) and i == 0):
                    dve.wait_ge(s["xt"], count("xt", i, j - 1))
                for c in range(2):
                    last = dve.tensor_scalar(xn[:, c, :], x[:, c, :], mv1[:, c, 0:1], rs1[:, c:c + 1],
                                             ALU.subtract, ALU.mult)
                last.then_inc(s["xn"], 1)

            def xn_split(i, par, j):
                dve.wait_ge(s["xnt_hi"], count("xnt_hi", i, j))
                dve.tensor_tensor(xnt[:, 1, :, :], m_bank["xt", j][:].rearrange("p (k t) -> p k t", k=KD),
                                  xnt[:, 0, :, :].bitcast(F32), ALU.subtract).then_inc(s["xnt"], 1)

            def dt_bias(i, par, j):
                dve.wait_ge(s["dt"], count("dt", i, j))
                dve.tensor_tensor(spa[:].rearrange("p (c h) -> p c h", c=2),
                                  m_bank["dt", j][:, 0:16].rearrange("p (c h) -> p c h", c=2),
                                  dtb[:].unsqueeze(1).broadcast_to([P, 2, HEADS]), ALU.add).then_inc(s["dt_read"], 1)
                dve.wait_ge(s["dt_read"], count("dt_read", i, j))
                dve.scalar_tensor_tensor(out=spn[:], in0=spa[:], scalar=-1.0, in1=spa[:], op0=ALU.mult,
                                         op1=ALU.min).then_inc(s["spn"], 1)

            def softplus(i, par, j):
                dve.wait_ge(s["softln"], count("softln", i, j))
                link("dt_link", i, 6 * j + 0, dve.tensor_scalar(spw[:], spe[:], 1.0, 1.0, ALU.add, ALU.subtract))
                link("dt_link", i, 6 * j + 1, dve.tensor_scalar(spw[:], spw[:], TINY, None, ALU.max))
                link("dt_link", i, 6 * j + 2, dve.reciprocal(spr[:], spw[:]))
                link("dt_link", i, 6 * j + 3, dve.scalar_tensor_tensor(out=spw[:], in0=spl[:], scalar=TINY, in1=spr[:],
                                                              op0=ALU.max, op1=ALU.mult))
                link("dt_link", i, 6 * j + 4, dve.scalar_tensor_tensor(out=spr[:], in0=spw[:], scalar=1.0, in1=spe[:],
                                                              op0=ALU.min, op1=ALU.mult))
                link("dt_link", i, 6 * j + 5, dve.scalar_tensor_tensor(out=dt_[:, j, :], in0=spa[:], scalar=0.0, in1=spr[:],
                                                              op0=ALU.max, op1=ALU.add))
                shape = [P, 3, 2, HEADS]
                dve.tensor_tensor(da[:, :, 0:16].rearrange("p r (c h) -> p r c h", c=2),
                                  dt_[:, j, :].rearrange("p (c h) -> p c h", c=2).unsqueeze(1).broadcast_to(shape),
                                  a_neg[:].unsqueeze(1).unsqueeze(1).broadcast_to(shape), ALU.mult).then_inc(s["da"], 1)

            def decays(i, par, j):
                ps = m_bank["cs", j][0:96, 128:256]
                dve.wait_ge(s["ex"], count("ex", i, j))
                link("cs_link", i, 3 * j, dve.tensor_copy(t3[:], ps))
                dve.tensor_tensor(rest3[0:64, :], ps[0:64, :], t3[0:64, :], ALU.subtract).then_inc(s["cs_read"], 1)
                dve.wait_ge(s["cs_read"], count("cs_read", i, j))
                link("cs_link", i, 3 * j + 1, dve.tensor_copy(t3[0:64, :], rest3[0:64, :]))
                link("cs_link", i, 3 * j + 2, dve.tensor_tensor(rest3[0:32, :], rest3[0:32, :], t3[0:32, :], ALU.subtract))
                dve.tensor_copy(t3[0:32, :], rest3[0:32, :]).then_inc(s["t3"], 1)

            def sums(i, par, j):
                dve.wait_ge(s["ct"], count("ct", i, j))
                dve.tensor_copy(ct_[:], m_bank["ct", j][:, 0:16]).then_inc(s["ct_read"], 1)

            def decay_sums(i, par, k):
                c, h0 = k // 2 % 2, 4 * (k % 2)
                dve.wait_ge(s["ct_read"], count("ct_read", i, k // 4))
                dve.wait_ge(s["seg"], count("seg", i, k))
                for h in range(4):
                    r = HEADS * c + h0 + h
                    last = dve.tensor_scalar(lmat[:, c, h0 + h, :], m_bank["seg", k][:, CH * h:CH * h + CH],
                                             ct_[:, r:r + 1], 0.0, ALU.subtract, ALU.min)
                last.then_inc(s["upto_s"], 1)

            def gb_copy(i, par, j):
                dve.wait_ge(s["gb"], count("gb", i, j))
                dve.tensor_tensor(gb[:, 0:2, :], m_bank["gb", j][:, 0:SUB].rearrange("p (c l) -> p c l", c=2),
                                  upto[:].unsqueeze(1).broadcast_to([P, 2, CH]), ALU.mult).then_inc(s["gm"], 1)

            def conv(i, par, k):
                pr, slot = k % 3, k % 2
                pair = slice(2 * pr, 2 * pr + 2)
                if k >= 2 or not (isinstance(i, int) and i == 0):
                    dve.wait_ge(s["hist"], count("hist", i, k - 2))
                dve.tensor_copy(raw[:, slot, :, 0:TAPS - 1], hist[:, pair, :]).then_inc(s["hin"], 1)
                dve.wait_ge(s["hin"], count("hin", i, k))
                dve.wait_ge(s["tap"], count("tap", i, k))
                at = {}
                for r, tap in enumerate((2, 1, 0)):
                    for e in range(2):
                        ct = 2 * pr + e
                        if e in at:
                            dve.wait_ge(s["conv_link"], count("conv_link", i, at[e]))
                        ins = dve.scalar_tensor_tensor(out=xc[:, ct, :], in0=raw[:, slot, e, tap:tap + SUB],
                                                       scalar=cw[:, ct, tap:tap + 1], in1=xc[:, ct, :],
                                                       op0=ALU.mult, op1=ALU.add)
                        at[e] = 5 * k + 2 * r + e
                        ins.then_inc(s["conv_link"] if 2 * r + e < 5 else s["conv"], 1)
                dve.wait_ge(s["conv"], count("conv", i, k))
                if par == 1 and k >= 3:
                    last = dve.memset(hist[:, pair, :], 0.0)
                else:
                    last = dve.tensor_copy(hist[:, pair, :], raw[:, slot, :, SUB:SUB + TAPS - 1])
                last.then_inc(s["hist"], 1)

            def decayed_products(i, par, q):
                c = q % 2
                dve.wait_ge(s["lmat"], count("lmat", i, 2 * q + 1))
                dve.wait_ge(s["gm"], count("gm", i, q // 2))
                dve.tensor_tensor(lmat[:, c, :, :], lmat[:, c, :, :],
                                  gb[:, c, :].unsqueeze(1).broadcast_to([P, HEADS, CH]), ALU.mult).then_inc(s["m"], 1)

            def xdt_(i, par, q):
                c = q % 2
                ps = per_head(m_bank["xtr", q][:])
                if q or not (isinstance(i, int) and i == 0):
                    dve.wait_ge(s["ssq"], count("ssq", i, q - 1))
                dve.wait_ge(s["xtr"], count("xtr", i, q))
                dve.tensor_tensor(per_head(xdt[:]), ps, spread_heads(dt_[:, q // 2, 8 * c:8 * c + 8]), ALU.mult).then_inc(s["xdt"], 1)
                dve.tensor_tensor(per_head(yg[:]), ps, spread_heads(dsk[:]), ALU.mult).then_inc(s["skip"], 1)

            def yoff(i, par, q):
                c = q % 2
                dve.wait_ge(s["yo"], count("yo", i, q))
                dve.tensor_tensor(per_head(t1[:]), per_head(m_bank["yo", q][:]), spread_heads(ex[:, q // 2, 0, c, :]),
                                  ALU.mult).then_inc(s["t1"], 1)

            def state_(i, par, q):
                dve.wait_ge(s["decayed"], count("decayed", i, q))
                dve.wait_ge(s["st"], count("st", i, q))
                if par == 1 and q == 3:
                    dve.memset(state[:], 0.0).then_inc(s["state"], 1)
                else:
                    dve.tensor_tensor(state[:], m_bank["st", q][:], state[:], ALU.add).then_inc(s["state"], 1)

            def ydiag(i, par, q):
                dve.wait_ge(s["yskip"], count("yskip", i, q))
                dve.wait_ge(s["yd"], count("yd", i, q))
                dve.tensor_tensor(yg[:], m_bank["yd", q][:], yg[:], ALU.add).then_inc(s["ydiag"], 1)
                dve.wait_ge(s["ydiag"], count("ydiag", i, q))
                dve.wait_ge(s["sz"], count("sz", i, q))
                dve.tensor_tensor(yg[:], yg[:], sz[:, q % 2, :], ALU.mult).then_inc(s["y"], 1)

            def yt_split(i, par, q):
                dve.wait_ge(s["yt_hi"], count("yt_hi", i, q))
                dve.tensor_tensor(yt[:, 1, :, :].rearrange("p k t -> p (k t)"), m_bank["yt", q][:],
                                  yt[:, 0, :, :].rearrange("p k t -> p (k t)").bitcast(F32),
                                  ALU.subtract).then_inc(s["yts"], 1)

            def stats2(i, par, q):
                ps = m_bank["out", q][:, 0:DM]
                dve.wait_ge(s["out"], count("out", i, q))
                before_aggr("out_link", i, 6 * q, dve.bn_stats(st2[:], ps))
                link("out_link", i, 6 * q + 1, dve.bn_aggr(mv2[:], st2[:]))
                dve.wait_ge(s["ssq"], count("ssq", i, q))
                link("out_link", i, 6 * q + 2, dve.tensor_scalar(e2[:], ssq[:, q:q + 1], EPS / DI, EPS * EPS,
                                                                 ALU.mult, ALU.add))
                dve.tensor_tensor(ve2[:], mv2[:, 1:2], e2[:], ALU.add).then_inc(s["var2"], 1)

            def ln2(i, par, q):
                ps = m_bank["out", q][:, 0:DM]
                x = xb[:, par, q, :]
                dve.wait_ge(s["rstd2"], count("rstd2", i, q))
                link("out_link", i, 6 * q + 3, dve.tensor_tensor(mr2[:], mv2[:, 0:1], rs2[:], ALU.mult))
                if q == 0 and not (isinstance(i, int) and i == 0):
                    dve.wait_ge(out_stored, i * 32)
                dve.scalar_tensor_tensor(out=x, in0=ps, scalar=rs2[:], in1=xin[:, q // 2, q % 2, :], op0=ALU.mult,
                                         op1=ALU.add).then_inc(s["attn"], 1)
                dve.wait_ge(s["attn"], count("attn", i, q))
                dve.tensor_scalar(x, x, mr2[:], None, ALU.subtract).then_inc(s["x1"], 1)
                dve.wait_ge(s["x1"], count("x1", i, q))
                before_aggr("out_link", i, 6 * q + 4, dve.bn_stats(st3[:], x))
                link("out_link", i, 6 * q + 5, dve.bn_aggr(mv3[:, q, :], st3[:]))
                dve.tensor_scalar(ve3[:], mv3[:, q, 1:2], EPS, None, ALU.add).then_inc(s["var3"], 1)

            def x1n_(f, par, t):
                if t == 0 and isinstance(f, int) and f == 0:
                    dve.wait_ge(piece_lo, MATS * PIECES)
                dve.wait_ge(s["rstd3"], count("rstd3", f, t))
                dve.wait_ge(s["x1"], count("x1", f, t))
                dve.wait_ge(s["x1t"], count("x1t", f, t // 2 - 1))
                dve.tensor_scalar(x1n[:, t % 2, :, :], xb[:, par, t, :].rearrange("p (n two) -> p two n", two=2),
                                  mv3[:, t, 0:1], rs3[:, t:t + 1], ALU.subtract, ALU.mult).then_inc(s["x1n"], 1)

            def x1_split(f, par, j):
                dve.wait_ge(s["x1t_hi"], count("x1t_hi", f, j))
                dve.tensor_tensor(x1t[:, 1, :, SUB * j:SUB * j + SUB],
                                  f_bank["x1t", j][:].rearrange("p (k t) -> p k t", k=KD),
                                  x1t[:, 0, :, SUB * j:SUB * j + SUB].bitcast(F32), ALU.subtract).then_inc(s["x1ts"], 1)

            def inter(f, par, n):
                dve.wait_ge(s["gelu"], count("gelu", f, n))
                dve.wait_ge(s["up"], count("up", f, n))
                dve.tensor_tensor(hid[:, n % 2, :], f_bank["up", n][:], hid[:, n % 2, :], ALU.mult).then_inc(s["inter"], 1)

            def fin(f, par, _):
                dve.wait_ge(s["down"], count("down", f, NT - 1))
                for t in range(TT):
                    last = dve.bn_stats(st4[:, t, :], db[t // 2][:, t % 2 * DM:t % 2 * DM + DM])
                before_aggr("fin_link", f, 0, last)
                for t in range(TT):
                    last = dve.bn_aggr(mv4[:, t, :], st4[:, t, :])
                link("fin_link", f, 1, last)
                dve.tensor_scalar(ve4[:], mv4[:, :, 1], EPS, None, ALU.add).then_inc(s["var4"], 1)

            def ln4(f, par, _):
                dve.wait_ge(s["rstd4"], count("rstd4", f, 0))
                link("fin_link", f, 2, dve.tensor_tensor(mr4[:], mv4[:, :, 0], rs4[:], ALU.mult))
                for t in range(TT):
                    x = xb[:, par, t, :]
                    last = dve.scalar_tensor_tensor(out=x, in0=db[t // 2][:, t % 2 * DM:t % 2 * DM + DM],
                                                    scalar=rs4[:, t:t + 1], in1=x, op0=ALU.mult, op1=ALU.add)
                last.then_inc(s["d_read"], 1)
                dve.wait_ge(s["d_read"], count("d_read", f, 0))
                for t in range(TT):
                    x = xb[:, par, t, :]
                    last = dve.tensor_scalar(x, x, mr4[:, t:t + 1], None, ALU.subtract)
                    if t % 2:
                        last.then_inc(s["outs"], 1)

            dq_links = [0]

            def dq(i, par, q):
                r = q % 2

                def step(ins):
                    dq_links[0] += 1
                    ins.then_inc(dve_dq, 1)
                    dve.wait_ge(dve_dq, dq_links[0])

                w = words[:, r, :]
                if q:
                    dve.wait_ge(codes_ready, q)
                dve.wait_ge(piece_loaded[r], 32 * (q // 2 + 1))
                step(dve.tensor_scalar(mags[:], w, 0xFF, None, ALU.bitwise_and))
                step(dve.scalar_tensor_tensor(out=spread[:], in0=mags[:], scalar=12, in1=mags[:],
                                              op0=ALU.logical_shift_left, op1=ALU.bitwise_or))
                dve.tensor_scalar(mags[:], spread[:], 0x00070007, 9, ALU.bitwise_and, ALU.logical_shift_left)
                step(dve.tensor_scalar(signs[:], spread[:], 0x00080008, 12, ALU.bitwise_and, ALU.logical_shift_left))
                dve.tensor_tensor(w, mags[:], signs[:], ALU.bitwise_or).then_inc(codes_ready, 1)

            drive(dve, "dve", dict(stats1=stats1, xn=xn_, xn_split=xn_split, dt_bias=dt_bias, softplus=softplus, decays=decays, sums=sums, decay_sums=decay_sums,
                            conv=conv, gb_copy=gb_copy,
                            decayed_products=decayed_products, xdt=xdt_, yoff=yoff, state=state_, ydiag=ydiag,
                            yt_split=yt_split, stats2=stats2, ln2=ln2, x1n=x1n_, x1_split=x1_split, inter=inter, fin=fin, ln4=ln4, dq=dq,
                            wi_split=wi_split, rates=rates, wo_split=wo_split), lambda: None)

        @block.tensor
        def _(pe):
            def bank_read(uses, use, i):
                u = [v[:2] for v in uses].index(use)
                it = i - dict(before=-1, this=0, next=1)[uses[u][2]]
                v, back = u, 0
                while True:
                    v -= 3
                    if v < 0:
                        v, back = max(w for w in range(len(uses)) if w % 3 == u % 3), back + 1
                    name, k, whose = uses[v]
                    if isinstance(it, int):
                        if whose != "before" and (it - back < -1 or (it - back == -1 and whose != "next")):
                            return
                        if it - back == NBLK - 1 and whose == "next":
                            continue
                    away = dict(before=-1, this=0, next=1)[whose]
                    pe.wait_ge(s[read_by[name]], count(read_by[name], it - back + away, k))
                    return

            def split_matmul(ps, lhs, rhs, nk, start=True, stop=True, check=False):
                todo = [(a, b, k) for k in range(nk) for a, b in PASSES]
                for n, (a, b, k) in enumerate(todo):
                    last = pe.matmul(ps, lhs(a, k), rhs(b, k), start=start and n == 0,
                                     stop=stop and n == len(todo) - 1, skip_group_check=check)
                return last

            def setup_pe():
                pe.wait_ge(ident_ready, 1)

            def xt(i, par, j):
                ps = m_bank["xt", j]
                pe.wait_ge(s["xn"], count("xn", i, j))
                bank_read(m_uses, ("xt", j), i)
                for c in range(2):
                    for k in range(KD):
                        last = pe.transpose(ps[:, SUB * k + CH * c:SUB * k + CH * c + CH], xn[:, c, P * k:P * k + P],
                                            ident[:])
                last.then_inc(s["xt"], 1)

            def dt(i, par, j):
                ps = m_bank["dt", j]
                if isinstance(i, int) and i == 0 and j == 0:
                    pe.wait_ge(wi_ready, 2)
                pe.wait_ge(s["xnt"], count("xnt", i, j))
                bank_read(m_uses, ("dt", j), i)
                for c in range(2):
                    last = split_matmul(ps[:, HEADS * c:HEADS * c + HEADS],
                                        lambda a, k: xnt[:, a, k, CH * c:CH * c + CH],
                                        lambda b, k: wi[:, b, k, ZX - HEADS:ZX], KD)
                last.then_inc(s["dt"], 1)

            def ip(i, par, q):
                ps = m_bank["ip", q]
                if isinstance(i, int) and i == 0 and q == 0:
                    pe.wait_ge(wi_ready, 2)
                pe.wait_ge(s["xnt"], count("xnt", i, q // 3))
                bank_read(m_uses, ("ip", q), i)
                for e in range(2):
                    c0 = DI + P * (2 * (q % 3) + e)
                    last = split_matmul(ps[:, SUB * e:SUB * e + SUB], lambda a, k: wi[:, a, k, c0:c0 + P],
                                        lambda b, k: xnt[:, b, k, :], KD)
                last.then_inc(s["ip"], 1)

            def cs(i, par, j):
                ps = m_bank["cs", j]
                if isinstance(i, int) and i == 0 and j == 0:
                    pe.wait_ge(consts_ready, 1)
                pe.wait_ge(s["da"], count("da", i, j))
                bank_read(m_uses, ("cs", j), i)
                for n, tri in enumerate((upto[:], after[:], ones[:].broadcast_to([P, P]))):
                    pe.matmul(ps[:, 16 * n:16 * n + 16], tri, da[:, 0, 0:16], start=True, stop=True)
                pe.matmul(ps[0:96, 128:256], da[:].rearrange("p r n -> p (r n)"), upto[:], start=True,
                          stop=True).then_inc(s["cs"], 1)

            def ct(i, par, j):
                pe.wait_ge(s["t3"], count("t3", i, j))
                bank_read(m_uses, ("ct", j), i)
                pe.matmul(m_bank["ct", j][:, 0:16], t3[:], pick[:], start=True, stop=True).then_inc(s["ct"], 1)

            def seg(i, par, k):
                c, h0 = k // 2 % 2, 4 * (k % 2)
                bank_read(m_uses, ("seg", k), i)
                for h in range(4):
                    r = HEADS * c + h0 + h
                    last = pe.matmul(m_bank["seg", k][:, CH * h:CH * h + CH],
                                     pick[:, r:r + 1].broadcast_to([96, CH]), t3[:], start=True, stop=True)
                last.then_inc(s["seg"], 1)

            def z(i, par, q):
                bank_read(m_uses, ("z", q), i)
                c = q % 2
                split_matmul(m_bank["z", q][:], lambda a, k: xnt[:, a, k, CH * c:CH * c + CH],
                             lambda b, k: wi[:, b, k, 0:DI], KD).then_inc(s["z"], 1)

            def gb_(i, par, j):
                ps = m_bank["gb", j]
                pe.wait_ge(s["xc"], count("xc", i, 3 * j + 2))
                bank_read(m_uses, ("gb", j), i)
                for c in range(2):
                    pe.matmul(ps[:, CH * c:CH * c + CH], xc[:, 4, CH * c:CH * c + CH], xc[:, 5, CH * c:CH * c + CH],
                              start=True, stop=True)
                for c in range(2):
                    last = pe.transpose(ps[:, SUB + CH * c:SUB + CH * c + CH], xc[:, 4, CH * c:CH * c + CH], ident[:])
                last.then_inc(s["gb"], 1)

            def xtr(i, par, q):
                c = q % 2
                bank_read(m_uses, ("xtr", q), i)
                for k in range(KI):
                    last = pe.transpose(m_bank["xtr", q][:, P * k:P * k + P], xc[:, k, CH * c:CH * c + CH], ident[:])
                last.then_inc(s["xtr"], 1)

            def yo(i, par, q):
                c = q % 2
                if q or not (isinstance(i, int) and i == 0):
                    pe.wait_ge(s["state"], count("state", i, q - 1))
                bank_read(m_uses, ("yo", q), i)
                pe.matmul(m_bank["yo", q][:], xc[:, 5, CH * c:CH * c + CH], state[:], start=True,
                          stop=True).then_inc(s["yo"], 1)

            def yd(i, par, q):
                c = q % 2
                pe.wait_ge(s["xdt"], count("xdt", i, q))
                pe.wait_ge(s["m"], count("m", i, q))
                bank_read(m_uses, ("yd", q), i)
                for h in range(HEADS):
                    last = pe.matmul(m_bank["yd", q][:, HD * h:HD * h + HD], lmat[:, c, h, :], xdt[:, HD * h:HD * h + HD],
                                     start=True, stop=True)
                last.then_inc(s["yd"], 1)

            def st(i, par, q):
                c = q % 2
                pe.wait_ge(s["xdd"], count("xdd", i, q))
                pe.wait_ge(s["gbs"], count("gbs", i, q // 2))
                bank_read(m_uses, ("st", q), i)
                pe.matmul(m_bank["st", q][:], gb[:, 2 + c, :], xdd[:], start=True, stop=True).then_inc(s["st"], 1)

            def yt_(i, par, q):
                pe.wait_ge(s["y"], count("y", i, q))
                bank_read(m_uses, ("yt", q), i)
                for k in range(KI):
                    last = pe.transpose(m_bank["yt", q][:, CH * k:CH * k + CH], yg[:, P * k:P * k + P], ident[:])
                last.then_inc(s["yt"], 1)

            def out_(i, par, q):
                if isinstance(i, int) and i == 0 and q == 0:
                    pe.wait_ge(wo_ready, 1)
                pe.wait_ge(s["yts"], count("yts", i, q))
                bank_read(m_uses, ("out", q), i)
                split_matmul(m_bank["out", q][:, 0:DM], lambda a, k: yt[:, a, k, :], lambda b, k: wo[:, b, k, :],
                             KI).then_inc(s["out"], 1)

            def x1t_(f, par, j):
                ps = f_bank["x1t", j]
                pe.wait_ge(s["x1n"], count("x1n", f, 2 * j + 1))
                bank_read(f_uses, ("x1t", j), f)
                for c in range(2):
                    for k in range(KD):
                        last = pe.transpose(ps[:, SUB * k + CH * c:SUB * k + CH * c + CH], x1n[:, c, k, :], ident[:])
                last.then_inc(s["x1t"], 1)

            def gu(f, par, n):
                if n == 0:
                    pe.wait_ge(s["x1ts"], count("x1ts", f, 1))
                for name, w in (("gate", wg), ("up", wu)):
                    bank_read(f_uses, (name, n), f)
                    split_matmul(f_bank[name, n][:], lambda a, k: w[:, a, k, P * n:P * n + P],
                                 lambda b, k: x1t[:, b, k, :], KD).then_inc(s[name], 1)

            def dn(f, par, n):
                pe.wait_ge(s["lo"], count("lo", f, n))
                if n == 0:
                    pe.wait_ge(s["d_read"], count("d_read", f - 1, 0))
                for t in range(TT):
                    last = split_matmul(db[t // 2][:, t % 2 * DM:t % 2 * DM + DM],
                                        lambda a, k: hl[:, n % 2, a, CH * t:CH * t + CH],
                                        lambda b, k: wd[:, b, n, :], 1, start=(n == 0 and t % 2 == 0),
                                        stop=(n == NT - 1), check=True)
                last.then_inc(s["down"], 1)

            def dl(i, par, q):
                if q == MATS * PIECES - 1:
                    pe.wait_ge(piece_lo, q + 1)

            drive(pe, "pe", dict(xt=xt, dt=dt, ip=ip, cs=cs, ct=ct, seg=seg, z=z, gb=gb_, xtr=xtr, yo=yo, yd=yd, st=st, yt=yt_, out=out_,
                           x1t=x1t_, gu=gu, dn=dn, dl=dl), setup_pe)


def kernel(**inputs):
    import numpy as _np
    import concourse.bacc as _bacc
    from concourse import mybir as _mybir
    from concourse.bass_utils import run_bass_kernel_spmd as _run

    x = {k.replace("L0_attn_", "").replace("L0_ffn_", ""): _np.asarray(v) for k, v in inputs.items()}

    def columns(a):
        return a.reshape(8, 128, 2, -1).transpose(3, 0, 2, 1).reshape(a.shape[1], -1)

    def down_words(a):
        return a.T.reshape(8, 128, 256).transpose(1, 0, 2).reshape(128, -1)

    def down_scales(a):
        return a.T.reshape(8, 8, 256).transpose(1, 0, 2).reshape(8, -1)

    arrays = {
        "u": x["u"],
        "in_proj": x["in_proj_kernel"],
        "conv_w": x["conv1d_weight"].reshape(6, 128, 4).transpose(1, 0, 2),
        "conv_b": x["conv1d_bias"].reshape(6, 128).T,
        "dt_bias": x["dt_bias"],
        "a_log": x["A_log"],
        "d_skip": x["D"],
        "norm_w": x["norm_weight"].reshape(4, 128).T,
        "out_proj": x["out_proj_kernel"],
        "packed": _np.stack([columns(x["gate_W_packed"]), columns(x["up_W_packed"]), down_words(x["down_W_packed"])]),
        "scales": _np.stack([columns(x["gate_scales"]), columns(x["up_scales"]), down_scales(x["down_scales"])]),
    }
    arrays = {f"in_{k}": _np.ascontiguousarray(v) for k, v in arrays.items()}
    nc = _bacc.Bacc("TRN2", target_bir_lowering=False, num_devices=1)
    args = [nc.dram_tensor(k, v.shape, _mybir.dt.from_np(v.dtype), kind="ExternalInput").ap() for k, v in arrays.items()]
    args.append(nc.dram_tensor("out_0", (BATCH, SEQ, DM), F32, kind="ExternalOutput").ap())
    build(nc, *args)
    r = _run(nc, [arrays], core_ids=[0])
    return r.results[0]["out_0"]
```

```python
from contextlib import ExitStack

import numpy as np

import concourse.bass as bass
from concourse import mybir

ALU = mybir.AluOpType
ACT = mybir.ActivationFunctionType
F32 = mybir.dt.float32
F32R = mybir.dt.float32r
F16 = mybir.dt.float16
BF16 = mybir.dt.bfloat16
I32 = mybir.dt.int32

P = 128
BATCH, SEQ, DM = 4, 1024, 256
HEADS, HD, DI, NSTATE, TAPS = 8, 64, 512, 128, 4
CONV = DI + 2 * NSTATE
ZX = 2 * DI + 2 * NSTATE + HEADS
MLP, SBLK = 2048, 32
EPS = 1e-5
BLK = 512
NBLK = BATCH * SEQ // BLK + 1
SUB = 256
CH = 128
KD = DM // P
KI = DI // P
CT = CONV // P
NT = MLP // P
TT = BLK // P
TINY = 1e-30
CODE_BITS = 0x8E00
PIECE = 512
PIECES = MLP // PIECE
MATS = 3

PASSES = ((0, 0), (0, 1), (1, 0))


MAMBA_BANKS = dict(xt=("xt",), dt=("dt",), dt_t=("dt_t",), cs=("cs",), ct=("ct",), seg=("seg",), ip=("ip",), z=("z",), gb=("gb",),
                   xtr=("xtr",), yo=("yo",), yd=("yd",), st=("st",), yt=("yt",), out=("out",))
FFN_BANKS = dict(x1t=("x1t",), gu=("gate", "up"))


ORDER = {
    "pe": """
        gu:0< cs:0 gu:1< gu:2< dn:0< dn:1< ct:0 gu:3< seg:0 seg:1 seg:2 dn:2< xtr:0 gu:4< gb:0 seg:3 yo:0
        gu:5< dn:3< yd:0 st:0 gu:6< yt:0 dn:4< xtr:1 out:0 yo:1 yd:1 dn:5< dn:6< st:1 xt:1 gu:7< yt:1 ip:3
        gu:8< out:1 dn:7< ip:4 dt:1 gu:9< dt_t:1 gu:10< dn:8< ip:5 dn:9< z:2 cs:1 z:3 gu:11< ct:1 seg:4
        seg:5 gu:12< seg:6 seg:7 gb:1 dn:10< yo:2 xtr:2 xt:0> gu:13< yd:2 st:2 dn:11< yt:2 dn:12< xtr:3
        out:2 yo:3 yd:3 gu:14< st:3 dn:13< yt:3 gu:15< out:3 dn:14< x1t:0 dt:0> dn:15< ip:0> dt_t:0> ip:1>
        ip:2> x1t:1 z:0> z:1>""",
    "act": """
        silu:0 gelu:0< gelu:1< split:0< split:1< gelu:2< silu:1 gate:0 gate:1 split:2< silu:2 exps:0 gelu:3<
        decay_matrix:0 decay_matrix:1 decay_matrix:2 split:3< gelu:4< decay_matrix:3 gb_copy:0 split:4<
        gelu:5< square:0 split:5< yt_split:0 gelu:6< split:6< xn_split:1 square:1 gelu:7< yt_split:1
        split:7< taps:3 gelu:8< silu:3 split:8< dt_copy:1 taps:4 gelu:9< gelu:10< split:9< dt_bias:1 taps:5
        silu:4 gate:2 silu:5 gate:3 split:10< gelu:11< decay_matrix:4 exps:1 decay_matrix:5 decay_matrix:6
        decay_matrix:7 gb_copy:1 split:11< gelu:12< split:12< gelu:13< xn_split:0> square:2 yt_split:2
        split:13< gelu:14< square:3 yt_split:3 split:14< gelu:15< split:15< x1_split:0 dt_copy:0> taps:0>
        dt_bias:0> x1_split:1 taps:1> taps:2>""",
    "dve": """
        conv:1 inter:0< inter:1< decays:0 conv:2 inter:2< stats1:1 sums:0 decay_sums:0 decay_sums:1
        decay_sums:2 xdt:0 inter:3< xn:1 decay_sums:3 gb_copy:0 decayed_products:0 yoff:0 inter:4<
        decayed_products:1 ydiag:0 state:0 inter:5< yt_split:0 inter:6< xdt:1 stats2:0 yoff:1 ln2:0 state:1
        ydiag:1 xn_split:1 x1n:0 inter:7< yt_split:1 conv:3 stats2:1 inter:8< ln2:1 conv:4 dt_bias:1
        inter:9< inter:10< stats1:0> x1n:1 softplus:1 conv:5 decays:1 xn:0> sums:1 decay_sums:4 decay_sums:5
        inter:11< decay_sums:6 decay_sums:7 gb_copy:1 decayed_products:2 xdt:2 yoff:2 inter:12<
        decayed_products:3 inter:13< xn_split:0> ydiag:2 state:2 yt_split:2 xdt:3 stats2:2 yoff:3 ln2:2
        ydiag:3 state:3 inter:14< yt_split:3 inter:15< stats2:3 x1n:2 ln2:3 fin:0< x1_split:0 x1n:3
        dt_bias:0> conv:0> softplus:0> x1_split:1 ln4:0<""",
    "pool": """
        split:0< split:1< split:2< stats1:1 xdt:0 split:3< yoff:0 split:4< split:5< split:6< stats2:0 xdt:1
        yoff:1 ln2:0 split:7< stats2:1 split:8< ln2:1 split:9< stats1:0> split:10< split:11< xdt:2 yoff:2
        split:12< split:13< xdt:3 stats2:2 yoff:3 ln2:2 split:14< split:15< stats2:3 ln2:3 fin:0<""",
}

FIRST = {
    "pe": """
        xt:1 ip:3 ip:4 dt:1 dt_t:1 ip:5 z:2 cs:1 z:3 ct:1 seg:4 seg:5 seg:6 seg:7 gb:1 yo:2 xtr:2 xt:0> yd:2
        st:2 yt:2 xtr:3 out:2 yo:3 yd:3 st:3 yt:3 out:3 dt:0> ip:0> dt_t:0> ip:1> ip:2> z:0> z:1> dl:11
        x1t:1 cs:0> gu:0 ct:0> seg:0> seg:1> gu:1 seg:2> xtr:0> gb:0> dn:0 seg:3> gu:2 yo:0> gu:3 dn:1 yd:0>
        st:0> gu:4 dn:2 yt:0> xtr:1> dn:3 gu:5 out:0> yo:1> yd:1> dn:4 dn:5 gu:6 st:1> xt:1> yt:1> gu:7 gu:8
        dn:6 ip:3> out:1> dn:7 ip:4> dt:1> dn:8 gu:9 gu:10 dt_t:1> ip:5> z:2> gu:11 cs:1> z:3> dn:9 ct:1>
        seg:4> seg:5> seg:6> dn:10 seg:7> gu:12 gb:1> yo:2> xtr:2> gu:13 xt:0>> yd:2> st:2> dn:11 yt:2>
        xtr:3> gu:14 out:2> yo:3> yd:3> dn:12 dn:13 gu:15 st:3> yt:3> dn:14 x1t:0> out:3> dt:0>> ip:0>>
        dn:15 dt_t:0>> ip:1>> x1t:1> ip:2>> z:0>> z:1>>""",
    "act": """
        wi_split:0 dq:0 dq:1 xn_split:1 rates:0 dl:0 dq:2 wo_split:0 taps:3 dl:1 dt_copy:1 dl:2 taps:4 dq:3
        dt_bias:1 taps:5 dq:4 silu:3 dl:3 silu:4 gate:2 gate:3 silu:5 dq:5 exps:1 decay_matrix:4
        decay_matrix:5 dl:4 decay_matrix:6 decay_matrix:7 dq:6 gb_copy:1 dl:5 dq:7 xn_split:0> square:2 dl:6
        yt_split:2 dl:7 dq:8 dq:9 dl:8 dq:10 dl:9 square:3 dq:11 yt_split:3 dl:10 dt_copy:0> dl:11 taps:0>
        dt_bias:0> taps:1> taps:2> gate:0> x1_split:1 gate:1> silu:0> silu:1> gelu:0 silu:2> split:0
        decay_matrix:0> exps:0> decay_matrix:1> gelu:1 split:1 gelu:2 gb_copy:0> gelu:3 split:2
        decay_matrix:2> decay_matrix:3> split:3 square:0> gelu:4 yt_split:0> split:4 gelu:5 split:5 gelu:6
        yt_split:1> square:1> split:6 gelu:7 xn_split:1> split:7 gelu:8 split:8 taps:3> dt_copy:1> taps:4>
        gelu:9 silu:3> gelu:10 dt_bias:1> taps:5> silu:4> split:9 gate:2> gate:3> silu:5> split:10 gelu:11
        exps:1> decay_matrix:4> gelu:12 decay_matrix:5> decay_matrix:6> decay_matrix:7> gb_copy:1> split:11
        xn_split:0>> split:12 gelu:13 yt_split:2> square:2> split:13 gelu:14 split:14 gelu:15 yt_split:3>
        square:3> x1_split:0> split:15 dt_copy:0>> taps:0>> taps:1>> x1_split:1> dt_bias:0>> taps:2>>""",
    "dve": """
        stats1:1 xn:1 stats1:0> xn:0> dq:0 wi_split:0 rates:0 scale:0 dq:1 wo_split:0 xn_split:1 dq:2
        wo_lo:0 scale:2 conv:3 dt_bias:1 dq:3 conv:4 softplus:1 conv:5 decays:1 dq:4 sums:1 decay_sums:4
        decay_sums:5 decay_sums:6 decay_sums:7 dq:5 xdt:2 gb_copy:1 decayed_products:2 yoff:2 dq:6
        decayed_products:3 dq:7 ydiag:2 state:2 xn_split:0> scale:7 xdt:3 yt_split:2 dq:8 stats2:2 yoff:3
        scale:8 dq:9 scale:9 ydiag:3 ln2:2 dq:10 state:3 yt_split:3 dq:11 stats2:3 scale:11 ln2:3 dt_bias:0>
        conv:0> softplus:0> x1n:2 x1n:3 conv:1> x1_split:1 decays:0> conv:2> inter:0 sums:0> decay_sums:0>
        decay_sums:1> decay_sums:2> xdt:0> decay_sums:3> gb_copy:0> inter:1 decayed_products:0> yoff:0>
        inter:2 stats1:1> inter:3 ydiag:0> decayed_products:1> state:0> xn:1> xdt:1> yt_split:0> inter:4
        inter:5 stats2:0> yoff:1> ln2:0> ydiag:1> state:1> inter:6 x1n:0> yt_split:1> inter:7 xn_split:1>
        inter:8 stats2:1> conv:3> ln2:1> conv:4> dt_bias:1> inter:9 inter:10 stats1:0>> x1n:1> softplus:1>
        conv:5> decays:1> xn:0>> sums:1> decay_sums:4> decay_sums:5> decay_sums:6> decay_sums:7> gb_copy:1>
        inter:11 xdt:2> yoff:2> decayed_products:2> decayed_products:3> inter:12 xn_split:0>> ydiag:2>
        state:2> inter:13 yt_split:2> xdt:3> inter:14 stats2:2> yoff:3> ln2:2> ydiag:3> inter:15 state:3>
        yt_split:3> x1n:2> x1_split:0> stats2:3> ln2:3> fin:0 dt_bias:0>> x1n:3> conv:0>> x1_split:1> ln4:0
        softplus:0>>""",
    "pool": """
        stats1:1 stats1:0> wi_split:0 dl:0 scale:1 dl:1 dl:2 scale:3 dl:3 scale:4 dl:4 scale:5 xdt:2 yoff:2
        dl:5 scale:6 dl:6 xdt:3 dl:7 yoff:3 stats2:2 dl:8 dl:9 ln2:2 scale:10 stats2:3 dl:10 ln2:3 dl:11
        split:0 xdt:0> split:1 yoff:0> split:2 stats1:1> split:3 xdt:1> split:4 split:5 stats2:0> yoff:1>
        ln2:0> split:6 split:7 split:8 stats2:1> ln2:1> stats1:0>> split:9 split:10 xdt:2> yoff:2> split:11
        split:12 split:13 xdt:3> stats2:2> yoff:3> ln2:2> split:14 split:15 stats2:3> ln2:3> fin:0""",
}

LAST = {
    "pe": """
        gu:0< gu:1< gu:2< dn:0< gu:3< dn:1< gu:4< dn:2< gu:5< dn:3< gu:6< dn:4< gu:7< dn:5< gu:8< dn:6<
        gu:9< dn:7< gu:10< dn:8< gu:11< dn:9< gu:12< dn:10< gu:13< dn:11< gu:14< dn:12< gu:15< dn:13< dn:14<
        dn:15<""",
    "act": """
        gelu:0< split:0< gelu:1< split:1< gelu:2< split:2< gelu:3< split:3< gelu:4< split:4< gelu:5<
        split:5< gelu:6< split:6< gelu:7< split:7< gelu:8< split:8< gelu:9< split:9< gelu:10< split:10<
        gelu:11< split:11< gelu:12< split:12< gelu:13< split:13< gelu:14< split:14< gelu:15< split:15<""",
    "dve": """
        inter:0< inter:1< inter:2< inter:3< inter:4< inter:5< inter:6< inter:7< inter:8< inter:9< inter:10<
        inter:11< inter:12< inter:13< inter:14< inter:15< fin:0< ln4:0<""",
    "pool": """
        split:0< split:1< split:2< split:3< split:4< split:5< split:6< split:7< split:8< split:9< split:10<
        split:11< split:12< split:13< split:14< split:15< fin:0<""",
}


def parse(orders):
    whose = {"<": "before", "": "this", ">": "next", ">>": "after"}
    steps = {}
    for engine, text in orders.items():
        steps[engine] = []
        for token in text.split():
            step = token.rstrip("<>")
            name, k = step.split(":")
            steps[engine].append((name, int(k), whose[token[len(step):]]))
    return steps


ORDER, FIRST, LAST = parse(ORDER), parse(FIRST), parse(LAST)

PER_HALF = dict(stats1=1, xn=1, xt=1, xn_split=1, dt=1, dt_copy=1, dt_t=1, dt_bias=1, softplus=1, cs=1,
                decays=1, ct=1, sums=1, exps=1,
                seg=4, decay_sums=4, decay_matrix=4, ip=3, taps=3, conv=3, silu=3, z=2, gate=2, gb=1, gb_copy=1,
                decayed_products=2, xtr=2, xdt=2, yo=2, yoff=2, yd=2, st=2, state=2, ydiag=2, square=2, yt=2,
                yt_split=2, out=2, stats2=2, ln2=2, x1n=2, x1t=1, x1_split=1)


AWAY = dict(before=-1, this=0, next=1, after=2)


def there(name, k, i):
    if not isinstance(i, int):
        return True
    if name in PER_HALF and (i, k // PER_HALF[name]) in ((0, 0), (NBLK - 1, 1)):
        return False
    return 0 <= i < NBLK


def tiles(f):
    if isinstance(f, int) and f in (0, NBLK - 1):
        return range(TT // 2, TT) if f == 0 else range(TT // 2)
    return range(TT)


def columns(f):
    return slice(CH * tiles(f)[0], CH * (tiles(f)[-1] + 1))


def iteration_steps(engine):
    return ORDER[engine]


def bank_uses(banks):
    return [(use, k, whose, name) for name, k, whose in iteration_steps("pe") for use in banks.get(name, ())]


def build(nc, u, in_proj, conv_w, conv_b, dt_bias, a_log, d_skip, norm_w, out_proj,
          packed, scales, out):
    ctx = ExitStack()
    with ctx:
        def sb(name, shape, dt=F32, stack=ctx):
            return stack.enter_context(nc.sbuf_tensor(name, shape, dt))

        def sem(name):
            return ctx.enter_context(nc.semaphore(name))

        wi = sb("wi", [P, 2, KD, ZX], F32R)
        wdt = sb("wdt", [P, KD, 2 * HEADS], F32R)
        wo = sb("wo", [P, 2, KI, DM], F32R)
        wg = sb("wg", [P, 2, KD, MLP], F32R)
        wu = sb("wu", [P, 2, KD, MLP], F32R)
        wd = sb("wd", [P, 2, NT, DM], F32R)
        ident = sb("ident", [P, P])
        upto = sb("upto", [P, P])
        both = sb("both", [2 * HEADS, HEADS])
        pick = sb("pick", [96, 16], BF16)
        neg_half = sb("neg_half", [P, TT])
        cw = sb("cw", [P, CT, TAPS])
        cb = sb("cb", [P, CT])
        dtb = sb("dtb", [P, HEADS])
        a_neg = sb("a_neg", [P, HEADS])
        dsk = sb("dsk", [P, HEADS])
        nw = sb("nw", [P, KI])
        with ExitStack() as early:
            wo_raw = sb("wo_raw", [P, KI, DM], F32, early)
        xb = sb("xb", [P, 2, TT, DM])
        xin = sb("xin", [P, 2, 2, DM])
        xn = sb("xn", [P, 2, DM])
        xnt = sb("xnt", [P, 2, KD, SUB], F32R)
        raw = sb("raw", [P, 2, 2, SUB + TAPS - 1])
        hist = sb("hist", [P, CT, TAPS - 1])
        xc = sb("xc", [P, CT, SUB])
        sz = sb("sz", [P, 2, DI])
        xdt = sb("xdt", [P, DI])
        t1 = sb("t1", [P, DI])
        yg = sb("yg", [P, DI])
        state = sb("state", [P, DI])
        yt = sb("yt", [P, 2, KI, CH], F32R)
        da = sb("da", [P, 3, 32])
        t3 = sb("t3", [96, CH], BF16)
        rest3 = sb("rest3", [96, CH])
        ct_ = sb("ct_", [P, 3, 2 * HEADS])
        dt_rows = sb("dt_rows", [2 * HEADS, SUB])
        ex = sb("ex", [P, 2, 3, 2, HEADS])
        pause = sb("pause", [P, 1])
        st1 = sb("st1", [P, 2, 6])
        mv1 = sb("mv1", [P, 2, 2])
        ve1 = sb("ve1", [P, 2])
        rs1 = sb("rs1", [P, 2])
        st2 = sb("st2", [P, 6])
        mv2 = sb("mv2", [P, 2])
        e2 = sb("e2", [P, 1])
        ve2 = sb("ve2", [P, 1])
        rs2 = sb("rs2", [P, 1])
        mr2 = sb("mr2", [P, 1])
        st3 = sb("st3", [P, 6])
        mv3 = sb("mv3", [P, TT, 2])
        ve3 = sb("ve3", [P, 1])
        rs3 = sb("rs3", [P, TT])
        ssq = sb("ssq", [P, 4])
        spa = sb("spa", [P, 2 * HEADS])
        spn = sb("spn", [P, 2 * HEADS])
        spe = sb("spe", [P, 2 * HEADS])
        spl = sb("spl", [P, 2 * HEADS])
        spw = sb("spw", [P, 2 * HEADS])
        spr = sb("spr", [P, 2 * HEADS])
        dt_ = sb("dt_", [P, 2, 2 * HEADS])
        st4 = sb("st4", [P, TT, 6])
        mv4 = sb("mv4", [P, TT, 2])
        ve4 = sb("ve4", [P, TT])
        rs4 = sb("rs4", [P, TT])
        mr4 = sb("mr4", [P, TT])
        with ExitStack() as early:
            wi_raw = sb("wi_raw", [P, KD, ZX], F32, early)
        lmat = sb("lmat", [P, 2, HEADS, CH])
        gb = sb("gb", [P, 4, CH])
        xdd = sb("xdd", [P, DI])
        with ExitStack() as early:
            words = sb("words", [P, 2, PIECE], I32, early)
            scl = sb("scl", [P, 2, PIECE], F32, early)
            low = sb("low", [P, PIECE], I32, early)
            high = sb("high", [P, PIECE], I32, early)
            wf = sb("wf", [P, 2, 2, PIECE], F32, early)
        x1n = sb("x1n", [P, 2, 2, CH])
        x1t = sb("x1t", [P, 2, KD, BLK], F32R)
        hid = sb("hid", [P, 2, BLK])
        hl = sb("hl", [P, 2, 2, BLK], F32R)

        mb = [ctx.enter_context(nc.psum_tensor(f"mb{b}", [P, 512], F32)) for b in range(3)]
        fb = [ctx.enter_context(nc.psum_tensor(f"fb{b}", [P, 512], F32)) for b in range(3)]
        db = [ctx.enter_context(nc.psum_tensor(f"db{b}", [P, 512], F32)) for b in range(2)]

        x_loaded = [sem(f"x_loaded{j}") for j in range(2)]
        out_stored = sem("out_stored")
        small_loaded = sem("small_loaded")
        wi_loaded = [sem(f"wi_loaded{k}") for k in range(KD)]
        wo_loaded = sem("wo_loaded")
        piece_loaded = [sem(f"piece_loaded{r}") for r in range(2)]
        consts_ready = sem("consts_ready")
        setup = sem("setup")
        ident_ready = sem("ident_ready")
        a_exp = sem("a_exp")
        a_ready = sem("a_ready")
        wi_hi = sem("wi_hi")
        wi_ready = sem("wi_ready")
        wo_scaled = sem("wo_scaled")
        wo_hi = sem("wo_hi")
        wo_ready = sem("wo_ready")
        dve_dq = sem("dve_dq")
        codes_ready = sem("codes_ready")
        scale_ready = sem("scale_ready")
        piece_f32 = sem("piece_f32")
        piece_hi = sem("piece_hi")
        piece_lo = [sem(f"piece_lo{r}") for r in range(2)]

        per_block = dict(
            var1=2, rstd1=2, xn=2, xt=2, xnt_hi=2, xnt=2, dt=2, dt_rows=2, dt_t=2, dt_read=2, spn=2, spe=2, softln=2, da=2,
            cs=2, ex=2, cs_read=2, t3=2, ct=2, ct_read=2, sums=2, seg=8, upto_s=8, lmat=8, ip=6, raw=6, tap=6, hin=6, conv=6, xc=6, hist=6,
            z=4, sz=4, gb=2, gm=2, gbs=2, m=4, xtr=4, xdt=4, skip=4, xdd=4, yo=4, t1=4, yd=4, st=4,
            decayed=4, yskip=4, ydiag=4, state=4, y=4, yt=4, ssq=4, yt_hi=4, yts=4, out=4,
            var2=4, rstd2=4, attn=4, x1=4, var3=4, rstd3=4, x1n=4,
            x1t=2, x1t_hi=2, x1ts=2, gate=NT, up=NT, gelu=NT, inter=NT, hi=NT, lo=NT, down=NT,
            var4=1, rstd4=1, d_read=1, outs=2,
            ln1_link=4, dt_link=12, cs_link=6, conv_link=30, out_link=24, fin_link=3)
        s = {name: sem("s_" + name) for name in per_block}
        whole = ("gate", "up", "gelu", "inter", "hi", "lo", "down", "var4", "rstd4", "d_read", "fin_link")

        def count(name, i, k):
            absent = 0 if name in whole else per_block[name] // 2
            return i * per_block[name] - absent + (k + 1)

        def wait_before(eng, name, i, k):
            value = count(name, i, k)
            if not isinstance(value, int) or value > 0:
                eng.wait_ge(s[name], value)

        m_uses, f_uses = bank_uses(MAMBA_BANKS), bank_uses(FFN_BANKS)
        read_by = dict(xt="xnt", dt="dt_rows", dt_t="dt_read", ip="tap", cs="cs_read", ct="ct_read", seg="upto_s", z="sz", gb="gbs",
                       xtr="skip", yo="t1", yd="ydiag", st="state", yt="yts", out="attn",
                       x1t="x1ts", gate="gelu", up="inter")
        m_bank = {use[:2]: mb[n % 3] for n, use in enumerate(m_uses)}
        f_bank = {use[:2]: fb[n % 3] for n, use in enumerate(f_uses)}

        def drive(eng, engine, do, prologue):
            def run(steps, i, par):
                for name, k, whose in steps:
                    away = AWAY[whose]
                    if there(name, k, i + away):
                        do[name](i + away, par if away % 2 == 0 else 1 - par, k)

            prologue()
            run(FIRST[engine], 0, 0)
            with eng.Fori(0, (NBLK - 3) // 2) as pair:
                for half in range(2):
                    run(iteration_steps(engine), pair * 2 + (2 + half), half)
            run(iteration_steps(engine), NBLK - 1, 0)
            run(LAST[engine], NBLK, 1)

        u_v = u.rearrange("b (h c p) d -> (b h) p c d", c=2, p=P)
        o_v = out.rearrange("b (h c p) d -> (b h) p c d", c=2, p=P)

        def per_head(ap):
            return ap.rearrange("p (h q) -> p h q", h=HEADS)

        def spread_heads(ap):
            return ap.unsqueeze(2).broadcast_to([P, HEADS, HD])

        def weight_piece(mat, part, c0):
            if mat < 2:
                return (wg, wu)[mat][:, part, :, c0:c0 + PIECE].rearrange("p e (g n) -> p e g n", n=DM)
            n0 = 2 * (c0 // DM)
            return wd[:, part, n0:n0 + 2 * PIECE // DM, :].rearrange("p (g e) n -> p e g n", e=2)

        def wf_piece(r):
            return wf[:, r, :, :].rearrange("p e (g n) -> p e g n", n=DM)

        block = ctx.enter_context(nc.Block())

        @block.sync
        def _(sp):
            def load_x(i, j):
                src = u_v[bass.ds(i * 2 + (j - 1), 1)].rearrange("o p c d -> (o p) c d")
                sp.dma_start(xin[:, j, :, :], src).then_inc(x_loaded[j], 16)

            load_x(0, 1)
            for k in range(KD):
                sp.dma_start(wi_raw[:, k, :], in_proj[P * k:P * k + P, :]).then_inc(wi_loaded[k], 16)
            for dst, src in ((cw, conv_w), (cb, conv_b), (nw, norm_w)):
                sp.dma_start(dst[:], src).then_inc(small_loaded, 16)
            for dst, src in ((dtb, dt_bias), (a_neg, a_log), (dsk, d_skip)):
                sp.dma_start(dst[:], src.partition_broadcast(P)).then_inc(small_loaded, 16)
            load_x(1, 0)
            for q in range(MATS * PIECES):
                mat, c0, r = q // PIECES, q % PIECES * PIECE, q % 2
                if q == 2:
                    sp.dma_start(wo_raw[:], out_proj.rearrange("(k p) n -> p k n", p=P)).then_inc(wo_loaded, 16)
                if q >= 2:
                    sp.wait_ge(piece_f32, q - 1)
                sp.dma_start(words[:, r, :], packed[mat, :, c0:c0 + PIECE]).then_inc(piece_loaded[r], 16)
                sp.dma_start(scl[:, r, :], scales[mat, :, c0:c0 + PIECE].unsqueeze(1)
                             .broadcast_to([8, SBLK // 2, PIECE])).then_inc(piece_loaded[r], 16)

            def next_x(i):
                for j in range(2):
                    if there("ln2", 2 * j + 1, i + 1) and not (isinstance(i, int) and (i, j) == (0, 0)):
                        sp.wait_ge(s["attn"], count("attn", i, 2 * j + 1))
                        load_x(i + 1, j)

            def store(f, par):
                for j in range(tiles(f)[0] // 2, tiles(f)[-1] // 2 + 1):
                    sp.wait_ge(s["outs"], count("outs", f, j))
                    dst = o_v[bass.ds(f * 2 + (j - 1), 1)].rearrange("o p c d -> (o p) c d")
                    sp.dma_start(dst, xb[:, par, 2 * j:2 * j + 2, :]).then_inc(out_stored, 16)

            next_x(0)
            next_x(1)
            store(0, 0)
            with sp.Fori(0, (NBLK - 5) // 2) as pair:
                for half in range(2):
                    next_x(pair * 2 + (2 + half))
                    store(pair * 2 + (1 + half), 1 - half)
            for i in range(NBLK - 3, NBLK + 1):
                if i + 1 < NBLK:
                    next_x(i)
                store(i - 1, (i - 1) % 2)
            sp.wait_ge(out_stored, 32 * (NBLK - 1))

        @block.gpsimd
        def _(pool):
            def consts():
                n = [0]

                def link(ins):
                    n[0] += 1
                    ins.then_inc(setup, 1)
                    pool.wait_ge(setup, n[0])

                link(pool.memset(ident[:], 0.0))
                pool.affine_select(out=ident[:], in_=ident[:], compare_op=ALU.not_equal, fill=1.0, base=0,
                                   pattern=[[-1, P]], channel_multiplier=1).then_inc(ident_ready, 1)
                pool.memset(neg_half[:], -0.5)
                pool.memset(state[:], 0.0)
                pool.memset(hist[:], 0.0)
                pool.memset(upto[:], 1.0)
                pool.memset(both[:], 0.0)
                pool.memset(da[:], 0.0)
                link(pool.memset(pick[:], 0.0))
                pool.affine_select(out=upto[:], in_=upto[:], compare_op=ALU.is_ge, fill=0.0, base=0,
                                   pattern=[[1, P]], channel_multiplier=-1)
                for part in range(3):
                    last = pool.affine_select(out=pick[:], in_=pick[:], compare_op=ALU.not_equal, fill=1.0,
                                              base=-32 * part, pattern=[[-1, 16]], channel_multiplier=1)
                    if part < 2:
                        last = pool.affine_select(out=both[:], in_=both[:], compare_op=ALU.not_equal, fill=1.0,
                                                  base=-HEADS * part, pattern=[[-1, HEADS]], channel_multiplier=1)
                        link(last)
                last.then_inc(consts_ready, 1)

            def wi_split(i, par, _):
                pool.wait_ge(wi_hi, 2)
                pool.tensor_tensor(wi[:, 1, 1, :], wi_raw[:, 1, :], wi[:, 0, 1, :].bitcast(F32),
                                   ALU.subtract).then_inc(wi_ready, 1)

            def rstd(name, dst, src, i, k):
                pool.wait_ge(s["var" + name], count("var" + name, i, k))
                pool.tensor_tensor(dst, src, neg_half[:, 0:src.shape[1]], ALU.pow).then_inc(s["rstd" + name], 1)

            def stats1(i, par, j):
                rstd("1", rs1[:], ve1[:], i, j)

            def xdt_(i, par, q):
                pool.wait_ge(s["ex"], count("ex", i, q // 2))
                pool.wait_ge(s["xdt"], count("xdt", i, q))
                pool.tensor_tensor(per_head(xdd[:]), per_head(xdt[:]), spread_heads(ex[:, q // 2, 1, q % 2, :]),
                                   ALU.mult).then_inc(s["xdd"], 1)

            def yoff(i, par, q):
                pool.wait_ge(s["yo"], count("yo", i, q))
                pool.tensor_tensor(per_head(state[:]), per_head(state[:]), spread_heads(ex[:, q // 2, 2, q % 2, :]),
                                   ALU.mult).then_inc(s["decayed"], 1)
                pool.wait_ge(s["t1"], count("t1", i, q))
                pool.tensor_tensor(yg[:], yg[:], t1[:], ALU.add).then_inc(s["yskip"], 1)

            def stats2(i, par, q):
                rstd("2", rs2[:], ve2[:], i, q)

            def ln2(i, par, q):
                rstd("3", rs3[:, q:q + 1], ve3[:], i, q)

            def split(f, par, n):
                pool.wait_ge(s["hi"], count("hi", f, n))
                at = columns(f)
                pool.tensor_tensor(hl[:, n % 2, 1, at], hid[:, n % 2, at], hl[:, n % 2, 0, at].bitcast(F32),
                                   ALU.subtract).then_inc(s["lo"], 1)

            def fin(f, par, _):
                at = slice(tiles(f)[0], tiles(f)[-1] + 1)
                rstd("4", rs4[:, at], ve4[:, at], f, 0)

            def scale(i, par, q):
                r = q % 2
                pool.wait_ge(codes_ready, q + 1)
                pool.wait_ge(scale_ready, q + 1)
                if q:
                    pool.wait_ge(piece_f32, q)
                if q >= 2:
                    pool.wait_ge(piece_lo[r], q // 2)
                codes = words[:, r, :].bitcast(F16).rearrange("p (n two) -> p two n", two=2)
                for e in range(2):
                    last = pool.tensor_tensor(wf[:, r, e, :], codes[:, e, :], scl[:, r, :], ALU.mult)
                last.then_inc(piece_f32, 1)

            def dl(i, par, q):
                mat, c0, r = q // PIECES, q % PIECES * PIECE, q % 2
                pool.wait_ge(piece_hi, q + 1)
                pool.tensor_tensor(weight_piece(mat, 1, c0), wf_piece(r),
                                   weight_piece(mat, 0, c0).bitcast(F32), ALU.subtract).then_inc(piece_lo[r], 1)

            drive(pool, "pool", dict(wi_split=wi_split, stats1=stats1, stats2=stats2, xdt=xdt_, yoff=yoff, ln2=ln2, split=split, fin=fin, scale=scale, dl=dl), consts)

        @block.scalar
        def _(act):
            def wi_split(i, par, _):
                for k in range(KD):
                    act.wait_ge(wi_loaded[k], 16)
                    act.activation(wi[:, 0, k, :], wi_raw[:, k, :], ACT.Copy).then_inc(wi_hi, 1)
                act.activation(wdt[:, :, 0:HEADS], wi_raw[:, :, ZX - HEADS:], ACT.Copy).then_inc(wi_hi, 1)

            def rates(i, par, _):
                act.preload_act_table_set("natural_log_exp_and_others")
                act.wait_ge(small_loaded, 96)
                act.activation(a_neg[:], a_neg[:], ACT.Exp).then_inc(a_exp, 1)

            def wo_split(i, par, _):
                act.wait_ge(wo_scaled, 1)
                act.activation(wo[:, 0, :, :], wo_raw[:], ACT.Copy).then_inc(wo_hi, 1)

            def xn_split(i, par, j):
                act.wait_ge(s["xt"], count("xt", i, j))
                act.activation(xnt[:, 0, :, :], m_bank["xt", j][:], ACT.Copy).then_inc(s["xnt_hi"], 1)

            def dt_bias(i, par, j):
                act.preload_act_table_set("natural_log_exp_and_others")
                act.wait_ge(s["spn"], count("spn", i, j))
                act.activation(spe[:], spn[:], ACT.Exp).then_inc(s["spe"], 1)
                act.wait_ge(s["spe"], count("spe", i, j))
                act.activation(spl[:], spe[:], ACT.Ln, bias=1.0).then_inc(s["softln"], 1)

            def dt_copy(i, par, j):
                act.wait_ge(s["dt"], count("dt", i, j))
                act.activation(dt_rows[:], m_bank["dt", j][0:2 * HEADS, 0:SUB], ACT.Copy).then_inc(s["dt_rows"], 1)

            def exps(i, par, j):
                act.wait_ge(s["sums"], count("sums", i, j))
                act.activation(ex[:, j].rearrange("p a c h -> p (a c h)"), ct_[:].rearrange("p a n -> p (a n)"),
                               ACT.Exp).then_inc(s["ex"], 1)

            def decay_matrix(i, par, k):
                c, h = k // 2 % 2, k % 2
                act.wait_ge(s["upto_s"], count("upto_s", i, k))
                part = lmat[:, c, 4 * h:4 * h + 4, :].rearrange("p h l -> p (h l)")
                act.activation(part, part, ACT.Exp).then_inc(s["lmat"], 1)

            def taps(i, par, k):
                j, pr = k // 3, k % 3
                act.wait_ge(s["ip"], count("ip", i, k))
                wait_before(act, "hist", i, k - 2)
                ps = m_bank["ip", k][:].rearrange("p (two t) -> p two t", two=2)
                act.activation(raw[:, k % 2, :, TAPS - 1:], ps, ACT.Copy).then_inc(s["raw"], 1)
                for e in range(2):
                    ct = 2 * pr + e
                    last = act.activation(xc[:, ct, :], ps[:, e, :], ACT.Identity, bias=cb[:, ct:ct + 1],
                                          scale=cw[:, ct, TAPS - 1:TAPS])
                last.then_inc(s["tap"], 1)

            def silu(i, par, k):
                pr = k % 3
                act.wait_ge(s["conv"], count("conv", i, k))
                act.activation(xc[:, 2 * pr:2 * pr + 2, :], xc[:, 2 * pr:2 * pr + 2, :], ACT.Silu).then_inc(s["xc"], 1)

            def gate(i, par, q):
                act.wait_ge(s["z"], count("z", i, q))
                act.activation(sz[:, q % 2, :], m_bank["z", q][:], ACT.Silu).then_inc(s["sz"], 1)

            def gb_copy(i, par, j):
                act.wait_ge(s["gm"], count("gm", i, j))
                act.activation(gb[:, 2:4, :].rearrange("p a l -> p (a l)"), m_bank["gb", j][:, SUB:],
                               ACT.Copy).then_inc(s["gbs"], 1)

            def square(i, par, q):
                act.wait_ge(s["y"], count("y", i, q))
                act.activation(t1[:], yg[:], ACT.Square, accum_out=ssq[:, q:q + 1]).then_inc(s["ssq"], 1)

            def yt_split(i, par, q):
                act.wait_ge(s["yt"], count("yt", i, q))
                act.activation(yt[:, 0, :, :].rearrange("p k t -> p (k t)"), m_bank["yt", q][:],
                               ACT.Copy).then_inc(s["yt_hi"], 1)

            def x1_split(f, par, j):
                act.wait_ge(s["x1t"], count("x1t", f, j))
                act.activation(x1t[:, 0, :, SUB * j:SUB * j + SUB],
                               f_bank["x1t", j][:].rearrange("p (k t) -> p k t", k=KD),
                               ACT.Copy).then_inc(s["x1t_hi"], 1)

            def gelu(f, par, n):
                act.wait_ge(s["gate"], count("gate", f, n))
                wait_before(act, "lo", f, n - 2)
                act.activation(hid[:, n % 2, columns(f)], f_bank["gate", n][:, columns(f)], ACT.Gelu_apprx_tanh).then_inc(s["gelu"], 1)

            def split(f, par, n):
                act.wait_ge(s["inter"], count("inter", f, n))
                wait_before(act, "down", f, n - 2)
                act.activation(hl[:, n % 2, 0, columns(f)], hid[:, n % 2, columns(f)], ACT.Copy).then_inc(s["hi"], 1)

            def dq(i, par, q):
                r = q % 2
                act.wait_ge(piece_loaded[r], 32 * (q // 2 + 1))
                act.activation(scl[:, r, :], scl[:, r, :], ACT.Copy, scale=2.0 ** 14).then_inc(scale_ready, 1)

            def dl(i, par, q):
                mat, c0, r = q // PIECES, q % PIECES * PIECE, q % 2
                act.wait_ge(piece_f32, q + 1)
                act.activation(weight_piece(mat, 0, c0), wf_piece(r), ACT.Copy).then_inc(piece_hi, 1)

            drive(act, "act", dict(xn_split=xn_split, dt_copy=dt_copy, dt_bias=dt_bias, exps=exps, decay_matrix=decay_matrix, taps=taps,
                            silu=silu, gate=gate, gb_copy=gb_copy, square=square, yt_split=yt_split,
                            x1_split=x1_split, gelu=gelu, split=split, dq=dq, dl=dl, wi_split=wi_split,
                            wo_split=wo_split, rates=rates), lambda: None)

        @block.vector
        def _(dve):
            def link(name, i, k, ins):
                ins.then_inc(s[name], 1)
                dve.wait_ge(s[name], count(name, i, k))

            def before_aggr(name, i, k, ins):
                link(name, i, k, ins)
                dve.memset(pause[:], 0.0)

            def wi_split(i, par, _):
                dve.wait_ge(wi_hi, 1)
                dve.tensor_tensor(wi[:, 1, 0, :], wi_raw[:, 0, :], wi[:, 0, 0, :].bitcast(F32),
                                  ALU.subtract).then_inc(wi_ready, 1)
                dve.wait_ge(wi_hi, 3)
                dve.tensor_tensor(wdt[:, :, HEADS:], wi_raw[:, :, ZX - HEADS:], wdt[:, :, 0:HEADS].bitcast(F32),
                                  ALU.subtract).then_inc(wi_ready, 1)

            def rates(i, par, _):
                dve.wait_ge(a_exp, 1)
                dve.tensor_scalar(a_neg[:], a_neg[:], -1.0, None, ALU.mult).then_inc(a_ready, 1)
                dve.wait_ge(a_ready, 1)
                dve.wait_ge(consts_ready, 1)

            def wo_split(i, par, _):
                dve.wait_ge(wo_loaded, 16)
                for k in range(KI):
                    last = dve.tensor_scalar(wo_raw[:, k, :], wo_raw[:, k, :], nw[:, k:k + 1], None, ALU.mult)
                last.then_inc(wo_scaled, 1)

            def wo_lo(i, par, _):
                dve.wait_ge(wo_hi, 1)
                dve.tensor_tensor(wo[:, 1, :, :], wo_raw[:], wo[:, 0, :, :].bitcast(F32),
                                  ALU.subtract).then_inc(wo_ready, 1)

            def stats1(i, par, j):
                dve.wait_ge(x_loaded[j], i * 16 + 16 * j)
                x = xin[:, j, :, :]
                for c in range(2):
                    last = dve.bn_stats(st1[:, c, :], x[:, c, :])
                before_aggr("ln1_link", i, 2 * j, last)
                for c in range(2):
                    last = dve.bn_aggr(mv1[:, c, :], st1[:, c, :])
                link("ln1_link", i, 2 * j + 1, last)
                dve.tensor_scalar(ve1[:], mv1[:, :, 1], EPS, None, ALU.add).then_inc(s["var1"], 1)

            def xn_(i, par, j):
                x = xin[:, j, :, :]
                dve.wait_ge(s["rstd1"], count("rstd1", i, j))
                wait_before(dve, "xt", i, j - 1)
                for c in range(2):
                    last = dve.tensor_scalar(xn[:, c, :], x[:, c, :], mv1[:, c, 0:1], rs1[:, c:c + 1],
                                             ALU.subtract, ALU.mult)
                last.then_inc(s["xn"], 1)

            def xn_split(i, par, j):
                dve.wait_ge(s["xnt_hi"], count("xnt_hi", i, j))
                dve.tensor_tensor(xnt[:, 1, :, :], m_bank["xt", j][:].rearrange("p (k t) -> p k t", k=KD),
                                  xnt[:, 0, :, :].bitcast(F32), ALU.subtract).then_inc(s["xnt"], 1)

            def dt_bias(i, par, j):
                dve.wait_ge(s["dt_t"], count("dt_t", i, j))
                dve.tensor_tensor(spa[:].rearrange("p (c h) -> p c h", c=2),
                                  m_bank["dt_t", j][:, 0:16].rearrange("p (c h) -> p c h", c=2),
                                  dtb[:].unsqueeze(1).broadcast_to([P, 2, HEADS]), ALU.add).then_inc(s["dt_read"], 1)
                dve.wait_ge(s["dt_read"], count("dt_read", i, j))
                dve.scalar_tensor_tensor(out=spn[:], in0=spa[:], scalar=-1.0, in1=spa[:], op0=ALU.mult,
                                         op1=ALU.min).then_inc(s["spn"], 1)

            def softplus(i, par, j):
                dve.wait_ge(s["softln"], count("softln", i, j))
                link("dt_link", i, 6 * j + 0, dve.tensor_scalar(spw[:], spe[:], 1.0, 1.0, ALU.add, ALU.subtract))
                link("dt_link", i, 6 * j + 1, dve.tensor_scalar(spw[:], spw[:], TINY, None, ALU.max))
                link("dt_link", i, 6 * j + 2, dve.reciprocal(spr[:], spw[:]))
                link("dt_link", i, 6 * j + 3, dve.scalar_tensor_tensor(out=spw[:], in0=spl[:], scalar=TINY, in1=spr[:],
                                                              op0=ALU.max, op1=ALU.mult))
                link("dt_link", i, 6 * j + 4, dve.scalar_tensor_tensor(out=spr[:], in0=spw[:], scalar=1.0, in1=spe[:],
                                                              op0=ALU.min, op1=ALU.mult))
                link("dt_link", i, 6 * j + 5, dve.scalar_tensor_tensor(out=dt_[:, j, :], in0=spa[:], scalar=0.0, in1=spr[:],
                                                              op0=ALU.max, op1=ALU.add))
                shape = [P, 3, 2, HEADS]
                dve.tensor_tensor(da[:, :, 0:16].rearrange("p r (c h) -> p r c h", c=2),
                                  dt_[:, j, :].rearrange("p (c h) -> p c h", c=2).unsqueeze(1).broadcast_to(shape),
                                  a_neg[:].unsqueeze(1).unsqueeze(1).broadcast_to(shape), ALU.mult).then_inc(s["da"], 1)

            def decays(i, par, j):
                ps = m_bank["cs", j][0:96, 0:CH]
                dve.wait_ge(s["cs"], count("cs", i, j))
                link("cs_link", i, 3 * j, dve.tensor_copy(t3[:], ps))
                dve.tensor_tensor(rest3[0:64, :], ps[0:64, :], t3[0:64, :], ALU.subtract).then_inc(s["cs_read"], 1)
                dve.wait_ge(s["cs_read"], count("cs_read", i, j))
                link("cs_link", i, 3 * j + 1, dve.tensor_copy(t3[0:64, :], rest3[0:64, :]))
                link("cs_link", i, 3 * j + 2, dve.tensor_tensor(rest3[0:32, :], rest3[0:32, :], t3[0:32, :], ALU.subtract))
                dve.tensor_copy(t3[0:32, :], rest3[0:32, :]).then_inc(s["t3"], 1)

            def sums(i, par, j):
                wait_before(dve, "ex", i, j - 1)
                dve.wait_ge(s["ct"], count("ct", i, j))
                dve.tensor_copy(ct_[:, 0:3:2, :], m_bank["ct", j][:, 0:32].rearrange("p (a n) -> p a n", a=2)).then_inc(
                    s["ct_read"], 1)
                dve.wait_ge(s["ct_read"], count("ct_read", i, j))
                dve.tensor_tensor(ct_[:, 1, :], ct_[:, 2, :], ct_[:, 0, :], ALU.subtract).then_inc(s["sums"], 1)

            def decay_sums(i, par, k):
                c, h0 = k // 2 % 2, 4 * (k % 2)
                dve.wait_ge(s["ct_read"], count("ct_read", i, k // 4))
                dve.wait_ge(s["seg"], count("seg", i, k))
                for h in range(4):
                    r = HEADS * c + h0 + h
                    last = dve.tensor_scalar(lmat[:, c, h0 + h, :], m_bank["seg", k][:, CH * h:CH * h + CH],
                                             ct_[:, 0, r:r + 1], 0.0, ALU.subtract, ALU.min)
                last.then_inc(s["upto_s"], 1)

            def gb_copy(i, par, j):
                dve.wait_ge(s["gb"], count("gb", i, j))
                dve.tensor_tensor(gb[:, 0:2, :], m_bank["gb", j][:, 0:SUB].rearrange("p (c l) -> p c l", c=2),
                                  upto[:].unsqueeze(1).broadcast_to([P, 2, CH]), ALU.mult).then_inc(s["gm"], 1)

            def conv(i, par, k):
                pr, slot = k % 3, k % 2
                pair = slice(2 * pr, 2 * pr + 2)
                wait_before(dve, "hist", i, k - 2)
                dve.tensor_copy(raw[:, slot, :, 0:TAPS - 1], hist[:, pair, :]).then_inc(s["hin"], 1)
                dve.wait_ge(s["hin"], count("hin", i, k))
                dve.wait_ge(s["tap"], count("tap", i, k))
                at = {}
                for r, tap in enumerate((2, 1, 0)):
                    for e in range(2):
                        ct = 2 * pr + e
                        if e in at:
                            dve.wait_ge(s["conv_link"], count("conv_link", i, at[e]))
                        ins = dve.scalar_tensor_tensor(out=xc[:, ct, :], in0=raw[:, slot, e, tap:tap + SUB],
                                                       scalar=cw[:, ct, tap:tap + 1], in1=xc[:, ct, :],
                                                       op0=ALU.mult, op1=ALU.add)
                        at[e] = 5 * k + 2 * r + e
                        ins.then_inc(s["conv_link"] if 2 * r + e < 5 else s["conv"], 1)
                dve.wait_ge(s["conv"], count("conv", i, k))
                if par == 0 and k < 3:
                    last = dve.memset(hist[:, pair, :], 0.0)
                else:
                    last = dve.tensor_copy(hist[:, pair, :], raw[:, slot, :, SUB:SUB + TAPS - 1])
                last.then_inc(s["hist"], 1)

            def decayed_products(i, par, q):
                c = q % 2
                dve.wait_ge(s["lmat"], count("lmat", i, 2 * q + 1))
                dve.wait_ge(s["gm"], count("gm", i, q // 2))
                dve.tensor_tensor(lmat[:, c, :, :], lmat[:, c, :, :],
                                  gb[:, c, :].unsqueeze(1).broadcast_to([P, HEADS, CH]), ALU.mult).then_inc(s["m"], 1)

            def xdt_(i, par, q):
                c = q % 2
                ps = per_head(m_bank["xtr", q][:])
                wait_before(dve, "ssq", i, q - 1)
                dve.wait_ge(s["xtr"], count("xtr", i, q))
                dve.tensor_tensor(per_head(xdt[:]), ps, spread_heads(dt_[:, q // 2, 8 * c:8 * c + 8]), ALU.mult).then_inc(s["xdt"], 1)
                dve.tensor_tensor(per_head(yg[:]), ps, spread_heads(dsk[:]), ALU.mult).then_inc(s["skip"], 1)

            def yoff(i, par, q):
                c = q % 2
                dve.wait_ge(s["ex"], count("ex", i, q // 2))
                dve.wait_ge(s["yo"], count("yo", i, q))
                dve.tensor_tensor(per_head(t1[:]), per_head(m_bank["yo", q][:]), spread_heads(ex[:, q // 2, 0, c, :]),
                                  ALU.mult).then_inc(s["t1"], 1)

            def state_(i, par, q):
                dve.wait_ge(s["decayed"], count("decayed", i, q))
                dve.wait_ge(s["st"], count("st", i, q))
                if par == 0 and q == 1:
                    dve.memset(state[:], 0.0).then_inc(s["state"], 1)
                else:
                    dve.tensor_tensor(state[:], m_bank["st", q][:], state[:], ALU.add).then_inc(s["state"], 1)

            def ydiag(i, par, q):
                dve.wait_ge(s["yskip"], count("yskip", i, q))
                dve.wait_ge(s["yd"], count("yd", i, q))
                dve.tensor_tensor(yg[:], m_bank["yd", q][:], yg[:], ALU.add).then_inc(s["ydiag"], 1)
                dve.wait_ge(s["ydiag"], count("ydiag", i, q))
                dve.wait_ge(s["sz"], count("sz", i, q))
                dve.tensor_tensor(yg[:], yg[:], sz[:, q % 2, :], ALU.mult).then_inc(s["y"], 1)

            def yt_split(i, par, q):
                dve.wait_ge(s["yt_hi"], count("yt_hi", i, q))
                dve.tensor_tensor(yt[:, 1, :, :].rearrange("p k t -> p (k t)"), m_bank["yt", q][:],
                                  yt[:, 0, :, :].rearrange("p k t -> p (k t)").bitcast(F32),
                                  ALU.subtract).then_inc(s["yts"], 1)

            def stats2(i, par, q):
                ps = m_bank["out", q][:, 0:DM]
                dve.wait_ge(s["out"], count("out", i, q))
                before_aggr("out_link", i, 6 * q, dve.bn_stats(st2[:], ps))
                link("out_link", i, 6 * q + 1, dve.bn_aggr(mv2[:], st2[:]))
                dve.wait_ge(s["ssq"], count("ssq", i, q))
                link("out_link", i, 6 * q + 2, dve.tensor_scalar(e2[:], ssq[:, q:q + 1], EPS / DI, EPS * EPS,
                                                                 ALU.mult, ALU.add))
                dve.tensor_tensor(ve2[:], mv2[:, 1:2], e2[:], ALU.add).then_inc(s["var2"], 1)

            def ln2(i, par, q):
                ps = m_bank["out", q][:, 0:DM]
                x = xb[:, par, q, :]
                dve.wait_ge(s["rstd2"], count("rstd2", i, q))
                link("out_link", i, 6 * q + 3, dve.tensor_tensor(mr2[:], mv2[:, 0:1], rs2[:], ALU.mult))
                if q == 0 and not (isinstance(i, int) and i < 2):
                    dve.wait_ge(out_stored, i * 32 - 48)
                dve.scalar_tensor_tensor(out=x, in0=ps, scalar=rs2[:], in1=xin[:, q // 2, q % 2, :], op0=ALU.mult,
                                         op1=ALU.add).then_inc(s["attn"], 1)
                dve.wait_ge(s["attn"], count("attn", i, q))
                dve.tensor_scalar(x, x, mr2[:], None, ALU.subtract).then_inc(s["x1"], 1)
                dve.wait_ge(s["x1"], count("x1", i, q))
                before_aggr("out_link", i, 6 * q + 4, dve.bn_stats(st3[:], x))
                link("out_link", i, 6 * q + 5, dve.bn_aggr(mv3[:, q, :], st3[:]))
                dve.tensor_scalar(ve3[:], mv3[:, q, 1:2], EPS, None, ALU.add).then_inc(s["var3"], 1)

            def x1n_(f, par, t):
                if t == 2 and isinstance(f, int) and f == 0:
                    for r in range(2):
                        dve.wait_ge(piece_lo[r], MATS * PIECES // 2)
                dve.wait_ge(s["rstd3"], count("rstd3", f, t))
                dve.wait_ge(s["x1"], count("x1", f, t))
                wait_before(dve, "x1t", f, t // 2 - 1)
                dve.tensor_scalar(x1n[:, t % 2, :, :], xb[:, par, t, :].rearrange("p (n two) -> p two n", two=2),
                                  mv3[:, t, 0:1], rs3[:, t:t + 1], ALU.subtract, ALU.mult).then_inc(s["x1n"], 1)

            def x1_split(f, par, j):
                dve.wait_ge(s["x1t_hi"], count("x1t_hi", f, j))
                dve.tensor_tensor(x1t[:, 1, :, SUB * j:SUB * j + SUB],
                                  f_bank["x1t", j][:].rearrange("p (k t) -> p k t", k=KD),
                                  x1t[:, 0, :, SUB * j:SUB * j + SUB].bitcast(F32), ALU.subtract).then_inc(s["x1ts"], 1)

            def inter(f, par, n):
                dve.wait_ge(s["gelu"], count("gelu", f, n))
                dve.wait_ge(s["up"], count("up", f, n))
                at = columns(f)
                dve.tensor_tensor(hid[:, n % 2, at], f_bank["up", n][:, at], hid[:, n % 2, at],
                                  ALU.mult).then_inc(s["inter"], 1)

            def fin(f, par, _):
                at = slice(tiles(f)[0], tiles(f)[-1] + 1)
                dve.wait_ge(s["down"], count("down", f, NT - 1))
                for t in tiles(f):
                    last = dve.bn_stats(st4[:, t, :], db[t // 2][:, t % 2 * DM:t % 2 * DM + DM])
                before_aggr("fin_link", f, 0, last)
                for t in tiles(f):
                    last = dve.bn_aggr(mv4[:, t, :], st4[:, t, :])
                link("fin_link", f, 1, last)
                dve.tensor_scalar(ve4[:, at], mv4[:, at, 1], EPS, None, ALU.add).then_inc(s["var4"], 1)

            def ln4(f, par, _):
                at = slice(tiles(f)[0], tiles(f)[-1] + 1)
                dve.wait_ge(s["rstd4"], count("rstd4", f, 0))
                link("fin_link", f, 2, dve.tensor_tensor(mr4[:, at], mv4[:, at, 0], rs4[:, at], ALU.mult))
                for t in tiles(f):
                    x = xb[:, par, t, :]
                    last = dve.scalar_tensor_tensor(out=x, in0=db[t // 2][:, t % 2 * DM:t % 2 * DM + DM],
                                                    scalar=rs4[:, t:t + 1], in1=x, op0=ALU.mult, op1=ALU.add)
                last.then_inc(s["d_read"], 1)
                dve.wait_ge(s["d_read"], count("d_read", f, 0))
                for t in tiles(f):
                    x = xb[:, par, t, :]
                    last = dve.tensor_scalar(x, x, mr4[:, t:t + 1], None, ALU.subtract)
                    if t % 2:
                        last.then_inc(s["outs"], 1)

            dq_links = [0]

            def dq(i, par, q):
                r = q % 2

                def step(ins):
                    dq_links[0] += 1
                    ins.then_inc(dve_dq, 1)
                    dve.wait_ge(dve_dq, dq_links[0])

                w = words[:, r, :]
                if q:
                    dve.wait_ge(codes_ready, q)
                dve.wait_ge(piece_loaded[r], 32 * (q // 2 + 1))
                dve.tensor_scalar(low[:], w, 28, 19, ALU.logical_shift_left, ALU.arith_shift_right)
                step(dve.tensor_scalar(high[:], w, 24, 3, ALU.logical_shift_left, ALU.arith_shift_right))
                step(dve.tensor_scalar(low[:], low[:], CODE_BITS, None, ALU.bitwise_and))
                dve.scalar_tensor_tensor(out=w, in0=high[:], scalar=(CODE_BITS << 16) - (1 << 32), in1=low[:],
                                         op0=ALU.bitwise_and, op1=ALU.bitwise_or).then_inc(codes_ready, 1)

            def scale(i, par, q):
                r = q % 2
                dve.wait_ge(codes_ready, q + 1)
                dve.wait_ge(scale_ready, q + 1)
                if q:
                    dve.wait_ge(piece_f32, q)
                if q >= 2:
                    dve.wait_ge(piece_lo[r], q // 2)
                codes = words[:, r, :].bitcast(F16).rearrange("p (n two) -> p two n", two=2)
                for e in range(2):
                    last = dve.tensor_tensor(wf[:, r, e, :], codes[:, e, :], scl[:, r, :], ALU.mult)
                last.then_inc(piece_f32, 1)

            def dl(i, par, q):
                mat, c0, r = q // PIECES, q % PIECES * PIECE, q % 2
                dve.wait_ge(piece_hi, q + 1)
                dve.tensor_tensor(weight_piece(mat, 1, c0), wf_piece(r), weight_piece(mat, 0, c0).bitcast(F32),
                                  ALU.subtract).then_inc(piece_lo[q % 2], 1)

            drive(dve, "dve", dict(stats1=stats1, xn=xn_, xn_split=xn_split, dt_bias=dt_bias, softplus=softplus, decays=decays, sums=sums, decay_sums=decay_sums,
                            conv=conv, gb_copy=gb_copy,
                            decayed_products=decayed_products, xdt=xdt_, yoff=yoff, state=state_, ydiag=ydiag,
                            yt_split=yt_split, stats2=stats2, ln2=ln2, x1n=x1n_, x1_split=x1_split, inter=inter, fin=fin, ln4=ln4, dq=dq, scale=scale,
                            dl=dl, wi_split=wi_split, rates=rates, wo_split=wo_split, wo_lo=wo_lo), lambda: None)

        @block.tensor
        def _(pe):
            def bank_read(uses, use, i):
                u = [v[:2] for v in uses].index(use)
                it = i - AWAY[uses[u][2]]
                v, back = u, 0
                while not isinstance(it, int) or it - back >= -1:
                    v -= 3
                    if v < 0:
                        v, back = max(w for w in range(len(uses)) if w % 3 == u % 3), back + 1
                    name, k, whose, step = uses[v]
                    if there(step, k, it - back + AWAY[whose]):
                        pe.wait_ge(s[read_by[name]], count(read_by[name], it - back + AWAY[whose], k))
                        return

            def split_matmul(ps, lhs, rhs, nk, start=True, stop=True, check=False):
                todo = [(a, b, k) for k in range(nk) for a, b in PASSES]
                for n, (a, b, k) in enumerate(todo):
                    last = pe.matmul(ps, lhs(a, k), rhs(b, k), start=start and n == 0,
                                     stop=stop and n == len(todo) - 1, skip_group_check=check)
                return last

            def identity():
                pe.wait_ge(ident_ready, 1)

            def xt(i, par, j):
                ps = m_bank["xt", j]
                pe.wait_ge(s["xn"], count("xn", i, j))
                bank_read(m_uses, ("xt", j), i)
                for c in range(2):
                    for k in range(KD):
                        last = pe.transpose(ps[:, SUB * k + CH * c:SUB * k + CH * c + CH], xn[:, c, P * k:P * k + P],
                                            ident[:])
                last.then_inc(s["xt"], 1)

            def dt(i, par, j):
                ps = m_bank["dt", j]
                if isinstance(i, int) and i == 0:
                    pe.wait_ge(wi_ready, 3)
                pe.wait_ge(s["xnt"], count("xnt", i, j))
                bank_read(m_uses, ("dt", j), i)
                for k in range(KD):
                    pe.matmul(ps[0:2 * HEADS, 0:SUB], wdt[:, k, :], xnt[:, 0, k, :], start=k == 0,
                              stop=False, skip_group_check=True)
                for k in range(KD):
                    last = pe.matmul(ps[0:HEADS, 0:SUB], wdt[:, k, 0:HEADS], xnt[:, 1, k, :], start=False,
                                     stop=k == KD - 1, skip_group_check=True)
                last.then_inc(s["dt"], 1)

            def dt_t(i, par, j):
                pe.wait_ge(s["dt_rows"], count("dt_rows", i, j))
                bank_read(m_uses, ("dt_t", j), i)
                for c in range(2):
                    last = pe.matmul(m_bank["dt_t", j][:, HEADS * c:HEADS * c + HEADS], dt_rows[:, CH * c:CH * c + CH],
                                     both[:], start=True, stop=True)
                last.then_inc(s["dt_t"], 1)

            def ip(i, par, q):
                ps = m_bank["ip", q]
                if isinstance(i, int) and i == 0 and q == 3:
                    pe.wait_ge(wi_ready, 3)
                pe.wait_ge(s["xnt"], count("xnt", i, q // 3))
                bank_read(m_uses, ("ip", q), i)
                for e in range(2):
                    c0 = DI + P * (2 * (q % 3) + e)
                    last = split_matmul(ps[:, SUB * e:SUB * e + SUB], lambda a, k: wi[:, a, k, c0:c0 + P],
                                        lambda b, k: xnt[:, b, k, :], KD)
                last.then_inc(s["ip"], 1)

            def cs(i, par, j):
                ps = m_bank["cs", j]
                if isinstance(i, int) and i == 0:
                    pe.wait_ge(consts_ready, 1)
                pe.wait_ge(s["da"], count("da", i, j))
                bank_read(m_uses, ("cs", j), i)
                pe.matmul(ps[0:96, 0:CH], da[:].rearrange("p r n -> p (r n)"), upto[:], start=True,
                          stop=True).then_inc(s["cs"], 1)

            def ct(i, par, j):
                pe.wait_ge(s["t3"], count("t3", i, j))
                bank_read(m_uses, ("ct", j), i)
                pe.matmul(m_bank["ct", j][:, 0:16], t3[:], pick[:], start=True, stop=True)
                pe.matmul(m_bank["ct", j][:, 16:32], t3[:, CH - 1:CH].broadcast_to([96, CH]), pick[:], start=True,
                          stop=True).then_inc(s["ct"], 1)

            def seg(i, par, k):
                c, h0 = k // 2 % 2, 4 * (k % 2)
                bank_read(m_uses, ("seg", k), i)
                for h in range(4):
                    r = HEADS * c + h0 + h
                    last = pe.matmul(m_bank["seg", k][:, CH * h:CH * h + CH],
                                     pick[:, r:r + 1].broadcast_to([96, CH]), t3[:], start=True, stop=True)
                last.then_inc(s["seg"], 1)

            def z(i, par, q):
                bank_read(m_uses, ("z", q), i)
                c = q % 2
                split_matmul(m_bank["z", q][:], lambda a, k: xnt[:, a, k, CH * c:CH * c + CH],
                             lambda b, k: wi[:, b, k, 0:DI], KD).then_inc(s["z"], 1)

            def gb_(i, par, j):
                ps = m_bank["gb", j]
                pe.wait_ge(s["xc"], count("xc", i, 3 * j + 2))
                bank_read(m_uses, ("gb", j), i)
                for c in range(2):
                    pe.matmul(ps[:, CH * c:CH * c + CH], xc[:, 4, CH * c:CH * c + CH], xc[:, 5, CH * c:CH * c + CH],
                              start=True, stop=True)
                for c in range(2):
                    last = pe.transpose(ps[:, SUB + CH * c:SUB + CH * c + CH], xc[:, 4, CH * c:CH * c + CH], ident[:])
                last.then_inc(s["gb"], 1)

            def xtr(i, par, q):
                c = q % 2
                bank_read(m_uses, ("xtr", q), i)
                for k in range(KI):
                    last = pe.transpose(m_bank["xtr", q][:, P * k:P * k + P], xc[:, k, CH * c:CH * c + CH], ident[:])
                last.then_inc(s["xtr"], 1)

            def yo(i, par, q):
                c = q % 2
                wait_before(pe, "state", i, q - 1)
                bank_read(m_uses, ("yo", q), i)
                pe.matmul(m_bank["yo", q][:], xc[:, 5, CH * c:CH * c + CH], state[:], start=True,
                          stop=True).then_inc(s["yo"], 1)

            def yd(i, par, q):
                c = q % 2
                pe.wait_ge(s["xdt"], count("xdt", i, q))
                pe.wait_ge(s["m"], count("m", i, q))
                bank_read(m_uses, ("yd", q), i)
                for h in range(HEADS):
                    last = pe.matmul(m_bank["yd", q][:, HD * h:HD * h + HD], lmat[:, c, h, :], xdt[:, HD * h:HD * h + HD],
                                     start=True, stop=True)
                last.then_inc(s["yd"], 1)

            def st(i, par, q):
                c = q % 2
                pe.wait_ge(s["xdd"], count("xdd", i, q))
                pe.wait_ge(s["gbs"], count("gbs", i, q // 2))
                bank_read(m_uses, ("st", q), i)
                pe.matmul(m_bank["st", q][:], gb[:, 2 + c, :], xdd[:], start=True, stop=True).then_inc(s["st"], 1)

            def yt_(i, par, q):
                pe.wait_ge(s["y"], count("y", i, q))
                bank_read(m_uses, ("yt", q), i)
                for k in range(KI):
                    last = pe.transpose(m_bank["yt", q][:, CH * k:CH * k + CH], yg[:, P * k:P * k + P], ident[:])
                last.then_inc(s["yt"], 1)

            def out_(i, par, q):
                if isinstance(i, int) and i == 0 and q == 2:
                    pe.wait_ge(wo_ready, 1)
                pe.wait_ge(s["yts"], count("yts", i, q))
                bank_read(m_uses, ("out", q), i)
                split_matmul(m_bank["out", q][:, 0:DM], lambda a, k: yt[:, a, k, :], lambda b, k: wo[:, b, k, :],
                             KI).then_inc(s["out"], 1)

            def x1t_(f, par, j):
                ps = f_bank["x1t", j]
                pe.wait_ge(s["x1n"], count("x1n", f, 2 * j + 1))
                bank_read(f_uses, ("x1t", j), f)
                for c in range(2):
                    for k in range(KD):
                        last = pe.transpose(ps[:, SUB * k + CH * c:SUB * k + CH * c + CH], x1n[:, c, k, :], ident[:])
                last.then_inc(s["x1t"], 1)

            def gu(f, par, n):
                at = columns(f)
                if n == 0:
                    pe.wait_ge(s["x1ts"], count("x1ts", f, tiles(f)[-1] // 2))
                for name, w in (("gate", wg), ("up", wu)):
                    bank_read(f_uses, (name, n), f)
                    split_matmul(f_bank[name, n][:, at], lambda a, k: w[:, a, k, P * n:P * n + P],
                                 lambda b, k: x1t[:, b, k, at], KD).then_inc(s[name], 1)

            def dn(f, par, n):
                pe.wait_ge(s["lo"], count("lo", f, n))
                if n == 0:
                    wait_before(pe, "d_read", f - 1, 0)
                for t in tiles(f):
                    last = split_matmul(db[t // 2][:, t % 2 * DM:t % 2 * DM + DM],
                                        lambda a, k: hl[:, n % 2, a, CH * t:CH * t + CH],
                                        lambda b, k: wd[:, b, n, :], 1, start=(n == 0 and t % 2 == 0),
                                        stop=(n == NT - 1), check=True)
                last.then_inc(s["down"], 1)

            def dl(i, par, _):
                for r in range(2):
                    pe.wait_ge(piece_lo[r], MATS * PIECES // 2)

            drive(pe, "pe", dict(xt=xt, dt=dt, dt_t=dt_t, ip=ip, cs=cs, ct=ct, seg=seg, z=z, gb=gb_, xtr=xtr, yo=yo, yd=yd, st=st, yt=yt_, out=out_,
                           x1t=x1t_, gu=gu, dn=dn, dl=dl), identity)


def kernel(**inputs):
    import numpy as _np
    import concourse.bacc as _bacc
    from concourse import mybir as _mybir
    from concourse.bass_utils import run_bass_kernel_spmd as _run

    x = {k.replace("L0_attn_", "").replace("L0_ffn_", ""): _np.asarray(v) for k, v in inputs.items()}

    def columns(a):
        return a.reshape(8, 128, 2, -1).transpose(3, 0, 2, 1).reshape(a.shape[1], -1)

    def down_words(a):
        return a.T.reshape(8, 128, 256).transpose(1, 0, 2).reshape(128, -1)

    def down_scales(a):
        return a.T.reshape(8, 8, 256).transpose(1, 0, 2).reshape(8, -1)

    arrays = {
        "u": x["u"],
        "in_proj": x["in_proj_kernel"],
        "conv_w": x["conv1d_weight"].reshape(6, 128, 4).transpose(1, 0, 2),
        "conv_b": x["conv1d_bias"].reshape(6, 128).T,
        "dt_bias": x["dt_bias"],
        "a_log": x["A_log"],
        "d_skip": x["D"],
        "norm_w": x["norm_weight"].reshape(4, 128).T,
        "out_proj": x["out_proj_kernel"],
        "packed": _np.stack([columns(x["gate_W_packed"]), columns(x["up_W_packed"]), down_words(x["down_W_packed"])]),
        "scales": _np.stack([columns(x["gate_scales"]), columns(x["up_scales"]), down_scales(x["down_scales"])]),
    }
    arrays = {f"in_{k}": _np.ascontiguousarray(v) for k, v in arrays.items()}
    nc = _bacc.Bacc("TRN2", target_bir_lowering=False, num_devices=1)
    args = [nc.dram_tensor(k, v.shape, _mybir.dt.from_np(v.dtype), kind="ExternalInput").ap() for k, v in arrays.items()]
    args.append(nc.dram_tensor("out_0", (BATCH, SEQ, DM), F32, kind="ExternalOutput").ap())
    build(nc, *args)
    r = _run(nc, [arrays], core_ids=[0])
    return r.results[0]["out_0"]
```
